# Optimizing a Trainium2 kernel written in Bass

```python
import numpy as np
import jax
import jax.numpy as jnp

def _softmax(x, axis=-1):
    return jax.nn.softmax(x, axis=axis)

def _gelu(x):
    return jax.nn.gelu(x, approximate=True)

def _silu(x):
    return jax.nn.silu(x)

def _sigmoid(x):
    return jax.nn.sigmoid(x)

def _layernorm(x, axis=-1, eps=1e-05):
    m = jnp.mean(x, axis=axis, keepdims=True)
    v = jnp.var(x, axis=axis, keepdims=True)
    return (x - m) / jnp.sqrt(v + eps)

def _scatter_add(tgt, idx, src, axis=0):
    return tgt.at[idx].add(src)

def _segment_sum(src, seg, n):
    return jax.ops.segment_sum(src, seg, n)
kernel_name = 'mk_vit_tower_d2_tok_img512_r4_66d335'

def setup_inputs(seed: int=0):
    np.random.seed(seed)
    _w = jnp.asarray

    def _rec_inputs():
        import jax
        import jax.numpy as jnp
        _rk = jax.random.key(seed)
        x = -0.000477451 + 1.00034 * jax.random.normal(jax.random.fold_in(_rk, 1), (8, 32, 32, 29), jnp.float32)
        return x
    x = _rec_inputs()

    def _L0_tok_setup():
        import jax, jax.numpy as jnp
        import numpy as np
        import math
        H, W_DIM, D_MODEL, B = (32, 32, 128, 128)
        F_TOTAL = 29
        SEQ_LEN = H * W_DIM

        def make_pe(seq_len: int, d_model: int) -> jnp.ndarray:
            position = np.arange(seq_len, dtype=np.float32)[:, None]
            div_term = np.exp(np.arange(0, d_model, 2, dtype=np.float32) * (-math.log(10000.0) / d_model))
            pe = np.zeros((seq_len, d_model), dtype=np.float32)
            pe[:, 0::2] = np.sin(position * div_term)
            pe[:, 1::2] = np.cos(position * div_term)
            return jnp.asarray(pe)
        key = jax.random.key(seed)
        k1, k2 = jax.random.split(key)
        state_tensor = jax.random.normal(k1, (B, H, W_DIM, F_TOTAL), dtype=jnp.float32)
        W = jax.random.normal(k2, (F_TOTAL, D_MODEL), dtype=jnp.float32) * 0.05
        return {'state_tensor': state_tensor, 'W': W}
    _L0_tok_all = _L0_tok_setup()
    _L0_tok_in = {k: v for k, v in _L0_tok_all.items() if k in ('W',)}
    del _L0_tok_all

    def _L0_attn_setup():
        import jax, jax.numpy as jnp
        import numpy as np
        NUM_HEAD = 8
        DIM_MODEL = 128
        DIM_HEAD = DIM_MODEL // NUM_HEAD
        LN_EPS = 1e-05
        key = jax.random.key(seed)
        ks = jax.random.split(key, 12)
        B, L, D = (4, 512, DIM_MODEL)
        s = 0.02
        return {'x': jax.random.normal(ks[0], (B, L, D), dtype=jnp.float32), 'Wq': jax.random.normal(ks[1], (D, D), dtype=jnp.float32) * s, 'bq': jnp.zeros((D,), dtype=jnp.float32), 'Wk': jax.random.normal(ks[2], (D, D), dtype=jnp.float32) * s, 'bk': jnp.zeros((D,), dtype=jnp.float32), 'Wv': jax.random.normal(ks[3], (D, D), dtype=jnp.float32) * s, 'bv': jnp.zeros((D,), dtype=jnp.float32), 'Wo': jax.random.normal(ks[4], (D, D), dtype=jnp.float32) * s, 'bo': jnp.zeros((D,), dtype=jnp.float32), 'gamma': jnp.ones((D,), dtype=jnp.float32), 'beta': jnp.zeros((D,), dtype=jnp.float32)}
    _L0_attn_all = _L0_attn_setup()
    _L0_attn_in = {k: v for k, v in _L0_attn_all.items() if k in ('Wq', 'bq', 'Wk', 'bk', 'Wv', 'bv', 'Wo', 'bo', 'gamma', 'beta')}
    del _L0_attn_all

    def _L0_ffn_setup():
        import jax, jax.numpy as jnp
        import numpy as np
        B, S, D = (32, 128, 128)
        E, H, O, K = (8, 512, 128, 2)
        key = jax.random.key(seed)
        ks = jax.random.split(key, 5)
        sc = lambda k, shape, scale: jax.random.normal(k, shape, jnp.float32) * scale
        return {'x': sc(ks[0], (B, S, D), 1.0), 'attn_w': sc(ks[1], (D, 1), 0.05), 'attn_b': jnp.zeros((1,), jnp.float32), 'gate_w': sc(ks[2], (D, E), 0.05), 'gate_b': jnp.zeros((E,), jnp.float32), 'w1': sc(ks[3], (E, D, H), 0.02), 'b1': jnp.zeros((E, H), jnp.float32), 'w2': sc(ks[4], (E, H, O), 0.02), 'b2': jnp.zeros((E, O), jnp.float32)}
    _L0_ffn_all = _L0_ffn_setup()
    _L0_ffn_in = {k: v for k, v in _L0_ffn_all.items() if k in ('attn_w', 'attn_b', 'gate_w', 'gate_b', 'w1', 'b1', 'w2', 'b2')}
    del _L0_ffn_all

    def _L1_attn_setup():
        import jax, jax.numpy as jnp
        import numpy as np
        NUM_HEADS = 8
        BLOCK_SIZE = 32
        WINDOW = 64
        key = jax.random.key(seed)
        ks = jax.random.split(key, 5)
        B, N, C = (8, 2048, 128)
        s = 0.02
        return {'x': jax.random.normal(ks[0], (B, N, C), dtype=jnp.float32), 'W_qkv': jax.random.normal(ks[1], (C, 3 * C), dtype=jnp.float32) * s, 'b_qkv': jax.random.normal(ks[2], (3 * C,), dtype=jnp.float32) * s, 'W_proj': jax.random.normal(ks[3], (C, C), dtype=jnp.float32) * s, 'b_proj': jax.random.normal(ks[4], (C,), dtype=jnp.float32) * s}
    _L1_attn_all = _L1_attn_setup()
    _L1_attn_in = {k: v for k, v in _L1_attn_all.items() if k in ('W_qkv', 'b_qkv', 'W_proj', 'b_proj')}
    del _L1_attn_all

    def _L1_ffn_setup():
        import jax, jax.numpy as jnp
        import numpy as np
        NUM_EXPERTS = 8
        TOP_K = 2
        key = jax.random.key(seed)
        ks = jax.random.split(key, 6)
        d, h, E = (128, 512, NUM_EXPERTS)
        s = 0.02
        return {'x': jax.random.normal(ks[0], (4, 1024, d), dtype=jnp.float32), 'Wr': jax.random.normal(ks[1], (d, E), dtype=jnp.float32) * s, 'W1': jax.random.normal(ks[2], (E, d, h), dtype=jnp.float32) * s, 'b1': jax.random.normal(ks[3], (E, h), dtype=jnp.float32) * s, 'W2': jax.random.normal(ks[4], (E, h, d), dtype=jnp.float32) * s, 'b2': jax.random.normal(ks[5], (E, d), dtype=jnp.float32) * s}
    _L1_ffn_all = _L1_ffn_setup()
    _L1_ffn_in = {k: v for k, v in _L1_ffn_all.items() if k in ('Wr', 'W1', 'b1', 'W2', 'b2')}
    del _L1_ffn_all
    return {'x': x, 'L0_tok_W': _L0_tok_in['W'], 'L0_attn_Wq': _L0_attn_in['Wq'], 'L0_attn_bq': _L0_attn_in['bq'], 'L0_attn_Wk': _L0_attn_in['Wk'], 'L0_attn_bk': _L0_attn_in['bk'], 'L0_attn_Wv': _L0_attn_in['Wv'], 'L0_attn_bv': _L0_attn_in['bv'], 'L0_attn_Wo': _L0_attn_in['Wo'], 'L0_attn_bo': _L0_attn_in['bo'], 'L0_attn_gamma': _L0_attn_in['gamma'], 'L0_attn_beta': _L0_attn_in['beta'], 'L0_ffn_attn_w': _L0_ffn_in['attn_w'], 'L0_ffn_attn_b': _L0_ffn_in['attn_b'], 'L0_ffn_gate_w': _L0_ffn_in['gate_w'], 'L0_ffn_gate_b': _L0_ffn_in['gate_b'], 'L0_ffn_w1': _L0_ffn_in['w1'], 'L0_ffn_b1': _L0_ffn_in['b1'], 'L0_ffn_w2': _L0_ffn_in['w2'], 'L0_ffn_b2': _L0_ffn_in['b2'], 'L1_attn_W_qkv': _L1_attn_in['W_qkv'], 'L1_attn_b_qkv': _L1_attn_in['b_qkv'], 'L1_attn_W_proj': _L1_attn_in['W_proj'], 'L1_attn_b_proj': _L1_attn_in['b_proj'], 'L1_ffn_Wr': _L1_ffn_in['Wr'], 'L1_ffn_W1': _L1_ffn_in['W1'], 'L1_ffn_b1': _L1_ffn_in['b1'], 'L1_ffn_W2': _L1_ffn_in['W2'], 'L1_ffn_b2': _L1_ffn_in['b2']}

def reference(x, L0_tok_W, L0_attn_Wq, L0_attn_bq, L0_attn_Wk, L0_attn_bk, L0_attn_Wv, L0_attn_bv, L0_attn_Wo, L0_attn_bo, L0_attn_gamma, L0_attn_beta, L0_ffn_attn_w, L0_ffn_attn_b, L0_ffn_gate_w, L0_ffn_gate_b, L0_ffn_w1, L0_ffn_b1, L0_ffn_w2, L0_ffn_b2, L1_attn_W_qkv, L1_attn_b_qkv, L1_attn_W_proj, L1_attn_b_proj, L1_ffn_Wr, L1_ffn_W1, L1_ffn_b1, L1_ffn_W2, L1_ffn_b2):
    import jax
    import jax.numpy as jnp

    def _L0_tok_ref(state_tensor, W):
        import jax, jax.numpy as jnp
        import numpy as np
        import math
        H, W_DIM, D_MODEL, B = (32, 32, 128, 128)
        F_TOTAL = 29
        SEQ_LEN = H * W_DIM

        def make_pe(seq_len: int, d_model: int) -> jnp.ndarray:
            position = np.arange(seq_len, dtype=np.float32)[:, None]
            div_term = np.exp(np.arange(0, d_model, 2, dtype=np.float32) * (-math.log(10000.0) / d_model))
            pe = np.zeros((seq_len, d_model), dtype=np.float32)
            pe[:, 0::2] = np.sin(position * div_term)
            pe[:, 1::2] = np.cos(position * div_term)
            return jnp.asarray(pe)
        b, h, w, f = state_tensor.shape
        s = h * w
        x = state_tensor.reshape(b, s, f)
        emb = jnp.einsum('bsf,fd->bsd', x, W)
        pe = make_pe(s * 2, W.shape[1])[:s]
        return emb + pe[None, :, :]

    def _L0_attn_ref(x, Wq, bq, Wk, bk, Wv, bv, Wo, bo, gamma, beta):
        import jax, jax.numpy as jnp
        import numpy as np
        NUM_HEAD = 8
        DIM_MODEL = 128
        DIM_HEAD = DIM_MODEL // NUM_HEAD
        LN_EPS = 1e-05
        B, L, D = x.shape
        H, dh = (NUM_HEAD, D // NUM_HEAD)
        Q = x @ Wq.T + bq
        K = x @ Wk.T + bk
        V = x @ Wv.T + bv
        Q = Q.reshape(B * H, L, dh)
        K = K.reshape(B * H, L, dh)
        V = V.reshape(B * H, L, dh)
        scale = dh ** (-0.5)
        attn = jax.nn.softmax(jnp.einsum('bqd,bkd->bqk', Q, K) * scale, axis=-1)
        context = jnp.einsum('bqk,bkd->bqd', attn, V)
        context = context.reshape(B, L, D)
        out = context @ Wo.T + bo
        out = out + x
        mu = jnp.mean(out, axis=-1, keepdims=True)
        var = jnp.mean(jnp.square(out - mu), axis=-1, keepdims=True)
        out = (out - mu) / jnp.sqrt(var + LN_EPS) * gamma + beta
        return out

    def _L0_ffn_ref(x, attn_w, attn_b, gate_w, gate_b, w1, b1, w2, b2):
        import jax, jax.numpy as jnp
        import numpy as np
        B, S, D = (32, 128, 128)
        E, H, O, K = (8, 512, 128, 2)
        scores = x @ attn_w + attn_b
        aw = jax.nn.softmax(scores, axis=1)
        pooled = jnp.sum(x * aw, axis=1)
        gates = jax.nn.softmax(pooled @ gate_w + gate_b, axis=-1)
        _, idx = jax.lax.top_k(gates, K)
        mask = jnp.sum(jax.nn.one_hot(idx, E, dtype=gates.dtype), axis=-2)
        g = gates * mask
        g = g / (jnp.sum(g, axis=-1, keepdims=True) + 1e-09)
        h = jax.nn.gelu(jnp.einsum('bsd,edh->ebsh', x, w1) + b1[:, None, None, :], approximate=False)
        eo = jax.nn.gelu(jnp.einsum('ebsh,eho->ebso', h, w2) + b2[:, None, None, :], approximate=False)
        return jnp.einsum('ebso,be->bso', eo, g)

    def _L1_attn_ref(x, W_qkv, b_qkv, W_proj, b_proj):
        import jax, jax.numpy as jnp
        import numpy as np
        NUM_HEADS = 8
        BLOCK_SIZE = 32
        WINDOW = 64
        B, N, C = x.shape
        h = NUM_HEADS
        dh = C // h
        scale = jnp.asarray(dh, x.dtype) ** (-0.5)
        qkv = (x @ W_qkv + b_qkv).reshape(B, N, h, 3 * dh)
        q = qkv[..., :dh].reshape(B, N, C)
        k = qkv[..., dh:2 * dh].reshape(B, N, C)
        v = qkv[..., 2 * dh:].reshape(B, N, C)
        nb = N // BLOCK_SIZE
        qb = q.reshape(B, nb, BLOCK_SIZE, C)
        kb = k.reshape(B, nb, BLOCK_SIZE, C)
        vb = v.reshape(B, nb, BLOCK_SIZE, C)
        attn = jnp.einsum('bisc,bjsc->bisj', qb, kb) * scale
        i_idx = jnp.arange(nb)[:, None]
        j_idx = jnp.arange(nb)[None, :]
        band = (j_idx >= i_idx - WINDOW) & (j_idx <= i_idx + WINDOW)
        neg = jnp.finfo(attn.dtype).min
        attn = jnp.where(band[None, :, None, :], attn, neg)
        attn = jax.nn.softmax(attn, axis=-1)
        out = jnp.einsum('bisj,bjsc->bisc', attn, vb)
        out = out.reshape(B, N, C)
        return out @ W_proj + b_proj

    def _L1_ffn_ref(x, Wr, W1, b1, W2, b2):
        import jax, jax.numpy as jnp
        import numpy as np
        NUM_EXPERTS = 8
        TOP_K = 2
        B, S, D = x.shape
        E = Wr.shape[1]
        flat = x.reshape(B * S, D)
        logits = flat @ Wr
        top_vals, top_idx = jax.lax.top_k(logits, TOP_K)
        top_w = jax.nn.softmax(top_vals, axis=-1)
        N = flat.shape[0]
        gates = jnp.zeros((N, E), dtype=flat.dtype).at[jnp.arange(N)[:, None], top_idx].add(top_w)
        out = jnp.zeros_like(flat)
        for e in range(E):
            hdn = jax.nn.gelu(flat @ W1[e] + b1[e], approximate=False)
            y = hdn @ W2[e] + b2[e]
            out = out + gates[:, e:e + 1] * y
        return out.reshape(B, S, D)
    h = _L0_tok_ref(x, L0_tok_W)
    h = h + _L0_attn_ref(_layernorm(h, axis=-1), L0_attn_Wq, L0_attn_bq, L0_attn_Wk, L0_attn_bk, L0_attn_Wv, L0_attn_bv, L0_attn_Wo, L0_attn_bo, L0_attn_gamma, L0_attn_beta)
    h = h + _L0_ffn_ref(_layernorm(h, axis=-1), L0_ffn_attn_w, L0_ffn_attn_b, L0_ffn_gate_w, L0_ffn_gate_b, L0_ffn_w1, L0_ffn_b1, L0_ffn_w2, L0_ffn_b2)
    h = h + _L1_attn_ref(_layernorm(h, axis=-1), L1_attn_W_qkv, L1_attn_b_qkv, L1_attn_W_proj, L1_attn_b_proj)
    h = h + _L1_ffn_ref(_layernorm(h, axis=-1), L1_ffn_Wr, L1_ffn_W1, L1_ffn_b1, L1_ffn_W2, L1_ffn_b2)
    return h

_drawn_inputs = setup_inputs


def setup_inputs(seed=0):
    import zlib

    import numpy as np

    out = dict(_drawn_inputs(seed))
    spreads = {'L0_attn_bq': (0.0, 0.8),
     'L0_attn_bk': (0.0, 0.8),
     'L0_attn_bv': (0.0, 0.8),
     'L0_attn_bo': (0.0, 0.1),
     'L0_attn_gamma': (1.0, 0.2),
     'L0_attn_beta': (0.0, 0.1),
     'L0_ffn_gate_b': (0.0, 0.8),
     'L0_ffn_b1': (0.0, 0.8),
     'L0_ffn_b2': (0.0, 0.457)}
    factors = {'L0_attn_Wq': 8.0,
     'L0_attn_Wk': 8.0,
     'L0_attn_Wv': 7.03,
     'L0_attn_Wo': 6.631,
     'L0_ffn_attn_w': 3.547,
     'L0_ffn_w1': 5.399,
     'L0_ffn_w2': 4.916,
     'L1_attn_W_qkv': 3.886,
     'L1_attn_b_qkv': 8.0,
     'L1_attn_W_proj': 4.024,
     'L1_attn_b_proj': 4.877,
     'L1_ffn_Wr': 2.854,
     'L1_ffn_b1': 33.644,
     'L1_ffn_b2': 7.05,
     'L1_ffn_W1': 3.13}
    for name, (base, spread) in spreads.items():
        noise = np.random.default_rng([zlib.crc32(name.encode()), seed]).standard_normal(out[name].shape)
        drawn = base * np.exp(spread * noise) if base else spread * noise
        out[name] = jnp.asarray(drawn.astype(out[name].dtype))
    for name, factor in factors.items():
        out[name] = (out[name] * factor).astype(out[name].dtype)
    return out
```

```python
from contextlib import ExitStack

import concourse.bass as bass
from concourse import mybir

F32 = mybir.dt.float32
F32R = mybir.dt.float32r
BF16 = mybir.dt.bfloat16
I32 = mybir.dt.int32
ALU = mybir.AluOpType
ACT = mybir.ActivationFunctionType
AX = mybir.AxisListType.X

P = 128
EPS = 1e-5
CH = 512
TPC = CH // P
LIMIT = 60.0


class Tally:

    def __init__(self, start):
        self.start, self.count = start, 0

    def next(self):
        self.count += 1
        return self.start + self.count

    def ends(self, count):
        assert self.count == count, (self.count, count)


class Core:

    def __init__(self, nc, ctx, tag):
        self.nc, self.ctx, self.tag = nc, ctx, tag

    def sb(self, name, shape, dt=F32):
        return self.ctx.enter_context(self.nc.sbuf_tensor(f"{self.tag}_{name}", shape, dt))

    def ps(self, name, shape):
        return self.ctx.enter_context(self.nc.psum_tensor(f"{self.tag}_{name}", shape, F32))

    def sem(self, name):
        return self.ctx.enter_context(self.nc.semaphore(f"{self.tag}_{name}"))


def split_f32r(nc, eng, hi, lo, src):
    nc.vector.tensor_copy(hi, src)
    eng.drain()
    return nc.vector.tensor_tensor(lo, src, hi.bitcast(F32), ALU.subtract)


def product(nc, out, w_hi, w_lo, x_hi, x_lo, first=True, last=True):
    nc.tensor.matmul(out, w_lo, x_hi, start=first, stop=False)
    nc.tensor.matmul(out, w_hi, x_lo, start=False, stop=False)
    return nc.tensor.matmul(out, w_hi, x_hi, start=False, stop=last)


def normalise(nc, dve, src, dst, stat, mv, veps, rs, var_done, rs_done, n):
    for i in range(TPC):
        nc.vector.bn_stats(stat[:, i, :], src(i))
    dve.drain()
    for i in range(TPC):
        nc.vector.bn_aggr(mv[:, i, :], stat[:, i, :])
    dve.drain()
    nc.vector.tensor_scalar(veps[:, :], mv[:, :, 1], EPS, None, ALU.add).then_inc(var_done, 1)
    dve.wait_ge(rs_done, n)
    for i in range(TPC):
        last = nc.vector.tensor_scalar(dst(i), src(i), mv[:, i, 0:1], rs[:, i:i + 1], ALU.subtract, ALU.mult)
    return last


def embed_and_attend(nc, H, ident, half, mean1, rstd1, score1, ins, B, S, D, NH):
    DH = D // NH
    T = S // P
    KT = NH
    F = ins["xT"].shape[0]
    CPB = S // CH
    SCALE = float(DH) ** -0.5
    NPR = 4
    NSC = 3
    PAIRS = [(0, 0), (0, 1), (1, 0), (1, 1), (0, 2), (2, 0)]
    KQ = DH * len(PAIRS)
    KG = KQ + 3
    assert T == NH == 8 and DH == 16 and CPB == 2 and KG <= P

    with ExitStack() as ctx:
        c = Core(nc, ctx, "a0")
        qs = [c.sb(f"qs{p}", [P, KT, S], BF16) for p in range(2)]
        ks = [c.sb(f"ks{p}", [P, KT, S], BF16) for p in range(2)]
        v = [c.sb(f"v{p}", [P, T, KT, 32]) for p in range(2)]
        n0 = [c.sb(f"n0{p}", [P, T, D]) for p in range(2)]
        xt = [c.sb(f"xt{p}", [F, S]) for p in range(2)]
        probs = [c.sb(f"probs{p}", [P, KT * P]) for p in range(NPR)]
        pe_tab = c.sb("pe_tab", [P, T, D])
        w_tok = c.sb("w_tok", [F, D])
        w_raw = c.sb("w_raw", [D, 4, D])
        wq_hi, wq_lo, wk_hi, wk_lo = (c.sb(n, [D, D], F32R) for n in ("wq_hi", "wq_lo", "wk_hi", "wk_lo"))
        bcol = c.sb("bcol", [D, 2])
        brow = c.sb("brow", [P, 5, D])
        nT = c.sb("nT", [D, CH])
        nT_hi, nT_lo = c.sb("nT_hi", [D, CH], F32R), c.sb("nT_lo", [D, CH], F32R)
        qf = [c.sb(f"qf{p}", [D, CH]) for p in range(2)]
        rem = c.sb("rem", [D, CH])
        sq = [c.sb(f"sq{p}", [D, CH], BF16) for p in range(2)]
        pieces_f = c.sb("pieces_f", [D, 32])
        pieces = c.sb("pieces", [D, 32], BF16)
        norms2 = c.sb("norms2", [64, CPB])
        worst, pair2, most2 = c.sb("worst", [64, 1]), c.sb("pair2", [32, 2]), c.sb("most2", [32, 2])
        bound2, unsafe = c.sb("bound2", [1, 1]), c.sb("unsafe", [1, 1], I32)
        parts = [c.sb(f"parts{p}", [D, 3, CH], BF16) for p in range(2)]
        stat, mv = c.sb("stat", [P, TPC, 6]), c.sb("mv", [P, TPC, 2])
        veps, rs = c.sb("veps", [P, TPC]), c.sb("rs", [P, TPC])
        negmax = c.sb("negmax", [P, 2 * KT, T])
        gf, gr = c.sb("gf", [KT * T, P]), c.sb("gr", [KT * T, P])
        gparts = c.sb("gparts", [KT * T, 3, P], BF16)
        o_sb = c.sb("o_sb", [P, 2 * P])
        rden = c.sb("rden", [P, KT])
        ctx_tm, ctxT = c.sb("ctx_tm", [P, KT, DH]), c.sb("ctxT", [D, P])
        res = c.sb("res", [P, TPC, D])
        dq = [nc.dram_tensor(f"qparts{p}", [D, 3, CH], BF16).ap() for p in range(2)]
        dk = [nc.dram_tensor(f"kparts{p}", [D, 3, CH], BF16).ap() for p in range(2)]

        psS = [c.ps(f"psS{p}", [P, 2, CH]) for p in range(NSC)]
        psO = c.ps("psO", [P, CH])
        psA = c.ps("psA", [P, CH])

        (w_in, wsplit, x_in0, x_in1, emb_ps, var_done, rs_done, n0_done, nt_ps,  q_ps, k_ps, v_ps,
         psA_free, qparts_done, kparts_done, qparts_out, kparts_out, stack_in, pre_qk, pre_max, gt_ps,
         gparts_done, guard_in, qk_done, exp_done, pv_done, o_evac, ht_ps,  ct_ps,
         op_done, sq_done, n_ps, norms_done, waited, qf_done, kf_done, unsafe_done) = (c.sem(n) for n in (
            "w_in wsplit x_in0 x_in1 emb_ps var_done rs_done n0_done nt_ps q_ps k_ps v_ps "
            "psA_free qparts_done kparts_done qparts_out kparts_out stack_in pre_qk pre_max gt_ps "
            "gparts_done guard_in qk_done exp_done pv_done o_evac ht_ps ct_ps "
            "op_done sq_done n_ps norms_done waited qf_done kf_done unsafe_done").split())

        x_in = (x_in0, x_in1)
        N_W = 14
        STACK = 16 * 2 * len(PAIRS) * CPB
        GUARD = 16 * 3
        PSA_EMBED = 6 * CPB
        PSA_BATCH = 1 + 3 * T + PSA_EMBED
        RS_EMBED, RS_BATCH = CPB, 3 * CPB

        STEPS = {(0, 2): ("E", 0), (0, 5): ("E", 1), (1, 2): ("T", 0), (1, 5): ("q", 0), (2, 2): ("k", 0),
                 (2, 5): ("v", 0), (3, 2): ("T", 1), (3, 5): ("N", 0), (4, 2): ("q", 1), (4, 5): ("k", 1),
                 (5, 2): ("v", 1), (5, 5): ("N", 1)}

        def rounds(eng, batch):
            with eng.Fori(0, B // 2 - 1) as it:
                for par in range(2):
                    batch(it * 2 + par, par, True)
            for par in range(2):
                batch(B - 2 + par, par, par == 0)

        block = ctx.enter_context(nc.Block())

        @block.sync
        def _(sp):
            for i, n in enumerate(("Wq", "Wk", "Wv", "Wo")):
                sp.dma_start(w_raw[:, i, :], ins[n]).then_inc(w_in, 16)
            sp.dma_start(w_tok[:, :], ins["Wtok"]).then_inc(w_in, 16)
            sp.dma_start(pe_tab[:, :, :], ins["pe"].rearrange("(t p) d -> p t d", p=P)).then_inc(w_in, 16)
            for i, n in enumerate(("bq", "bk")):
                sp.dma_start(bcol[:, i:i + 1], ins[n].rearrange("(d o) -> d o", o=1)).then_inc(w_in, 16)
            sp.dma_start(pieces_f[:, :], ins["pieces"]).then_inc(w_in, 16)
            for i, n in enumerate(("bv", "bo", "gamma", "beta", "attn_w")):
                sp.dma_start(brow[:, i, :], ins[n].rearrange("(o d) -> o d", o=1).broadcast_to([P, D])).then_inc(w_in, 16)
            sp.sem_inc(qparts_out, 16)
            sp.sem_inc(kparts_out, 16)

            def has_x(b):
                return not isinstance(b, int)

            def load_x(b, par):
                sp.dma_start(xt[par][:, :], ins["xT"][:, bass.ds(b * S, S)]).then_inc(x_in[par], 16)

            def redistribute(b, par):
                for ch in range(CPB):
                    for kind, done, out, dram in ((0, qparts_done, qparts_out, dq), (1, kparts_done, kparts_out, dk)):
                        sp.wait_ge(done, b * CPB + ch + 1)
                        sp.dma_start(dram[ch], parts[kind][:, :, :]).then_inc(out, 16)
                        sp.wait_ge(out, (b * CPB + ch) * 16 + 32)
                        src = dram[ch].rearrange("(j d) a t -> d j a t", d=DH)
                        for g, pair in enumerate(PAIRS):
                            sp.dma_start((qs, ks)[kind][par][g * DH:(g + 1) * DH, :, ch * CH:(ch + 1) * CH],
                                         src[:, :, pair[kind], :]).then_inc(stack_in, 16)

            def batch(b, par, more):
                sp.wait_ge(gparts_done, b + 1)
                for i in range(3):
                    sp.dma_start(qs[par][KQ + i:KQ + i + 1, :, :].rearrange("o j (h t) -> o (j h) t", t=P),
                                 gparts[:, i, :]).then_inc(guard_in, 16)
                if more:
                    if has_x(b):
                        sp.wait_ge(emb_ps, (b + 1) * CPB)
                        load_x(b + 2, par)
                    redistribute(b + 1, 1 - par)

            load_x(0, 0)
            load_x(1, 1)
            redistribute(0, 0)
            rounds(sp, batch)

        @block.gpsimd
        def _(pool):
            def root(turns):
                pool.wait_ge(var_done, turns.next())
                nc.gpsimd.tensor_tensor(rs[:, :], veps[:, :], half[:, 0:TPC], ALU.pow).then_inc(rs_done, 1)

            def embed_step(kind, ch, b, turns):
                if kind == "E":
                    root(turns)
                elif kind in ("q", "k"):
                    i = "qk".index(kind)
                    pool.wait_ge((qf_done, kf_done)[i], b * CPB + (ch + 1))
                    nc.gpsimd.tensor_tensor(sq[i][:, :], qf[i][:, :], qf[i][:, :], ALU.mult).then_inc(sq_done, 1)
                elif kind == "N" and ch == CPB - 1:
                    pool.wait_ge(norms_done, b + 1)
                    pool.sem_inc(waited, 1)
                    nc.gpsimd.partition_all_reduce(most2[:, :], pair2[:, :], 32, bass.bass_isa.ReduceOp.max)
                    pool.drain()
                    nc.gpsimd.tensor_tensor(bound2[:, :], most2[0:1, 0:1], most2[0:1, 1:2], ALU.mult)
                    pool.drain()
                    nc.gpsimd.tensor_scalar(unsafe[:, :], bound2[:, :], LIMIT * LIMIT, None, ALU.is_gt).then_inc(unsafe_done, 1)

            def batch(b, par, more):
                turns = Tally(RS_EMBED + b * RS_BATCH)
                for h in range(T):
                    for kt in range(KT):
                        if more and (h, kt) in STEPS:
                            embed_step(*STEPS[h, kt], b + 1, turns)
                    if h == TPC:
                        root(turns)
                        root(turns)
                root(turns)
                root(turns)
                turns.ends(RS_BATCH if more else RS_BATCH - RS_EMBED)

            turns = Tally(0)
            for kind, ch in STEPS.values():
                embed_step(kind, ch, 0, turns)
            rounds(pool, batch)

        @block.scalar
        def _(act):
            def batch(b, par, more):
                for h in range(T):
                    for kt in range(KT):
                        u = b * (T * KT) + (h * KT + kt)
                        act.wait_ge(qk_done, u + 1)
                        act.wait_ge(pv_done, u + 1)
                        nc.scalar.activation(probs[kt % NPR][:, :], psS[(h * KT + kt) % NSC][:, :, :].rearrange("p a n -> p (a n)"),
                                             ACT.Exp).then_inc(exp_done, 1)
            rounds(act, batch)

        @block.tensor
        def _(pe):
            def take(uses):
                pe.wait_ge(psA_free, uses.next())

            def embed_step(kind, ch, b, par, uses):
                n = b * CPB + (ch + 1)
                if kind == "E":
                    pe.wait_ge(x_in[par], (b + (2 - par)) * 8)
                    take(uses)
                    for i in range(TPC):
                        last = nc.tensor.matmul(psA[:, i * P:(i + 1) * P], xt[par][:, ch * CH + i * P:ch * CH + (i + 1) * P],
                                                w_tok[:, :], start=True, stop=True)
                    last.then_inc(emb_ps, 1)
                elif kind == "T":
                    pe.wait_ge(n0_done, n)
                    take(uses)
                    for i in range(TPC):
                        last = nc.tensor.transpose(psA[:, i * P:(i + 1) * P], n0[par][:, ch * TPC + i, :], ident[:, :])
                    last.then_inc(nt_ps, 1)
                elif kind in ("q", "k"):
                    take(uses)
                    hi, lo, done = (wq_hi, wq_lo, q_ps) if kind == "q" else (wk_hi, wk_lo, k_ps)
                    product(nc, psA[:, :], hi[:, :], lo[:, :], nT_hi[:, :], nT_lo[:, :]).then_inc(done, 1)
                elif kind == "N":
                    pe.wait_ge(sq_done, 2 * n)
                    take(uses)
                    for i in range(2):
                        last = nc.tensor.matmul(psA[32 * i:32 * i + 32, :], pieces[:, :], sq[i][:, :], start=True, stop=True)
                    last.then_inc(n_ps, 1)
                else:
                    take(uses)
                    for i in range(TPC):
                        last = nc.tensor.matmul(psA[:, i * P:(i + 1) * P], nT[:, i * P:(i + 1) * P], w_raw[:, 2, :],
                                                start=True, stop=True)
                    last.then_inc(v_ps, 1)

            def maximum(b, par, psA_free, uses):
                for j in range(KT):
                    for h in range(T):
                        u = j * T + h
                        if u >= 2:
                            pe.wait_ge(pre_max, b * (T * KT) + (u - 1))
                        for a in range(2):
                            last = nc.tensor.matmul(psS[u % 2][:, a, :], qs[par][0:KQ, j, h * P:(h + 1) * P],
                                                    ks[par][0:KQ, 4 * a:4 * a + 4, h * P:(h + 1) * P], start=True, stop=True)
                        last.then_inc(pre_qk, 1)
                pe.wait_ge(pre_max, (b + 1) * (T * KT))
                pe.wait_ge(psA_free, uses.start + 1)
                nc.tensor.transpose(psA[:, 0:P], negmax[:, :, :].rearrange("p j h -> p (j h)"), ident[:, :]).then_inc(gt_ps, 1)

            def batch(b, par, more):
                uses = Tally(PSA_EMBED + b * PSA_BATCH)
                pe.wait_ge(stack_in, (b + 1) * STACK)
                pe.wait_ge(unsafe_done, b + 1)
                pe.sem_inc(waited, 1)
                with pe.If(pe.value_load(unsafe[0:1, 0:1], min_val=0, max_val=1)):
                    maximum(b, par, psA_free, uses)
                uses.next()
                pe.wait_ge(guard_in, (b + 1) * GUARD)

                def scores(u):
                    h, kt = divmod(u, KT)
                    for a in range(2):
                        last = nc.tensor.matmul(psS[u % NSC][:, a, :], ks[par][0:KG, kt, h * P:(h + 1) * P],
                                                qs[par][0:KG, 4 * a:4 * a + 4, h * P:(h + 1) * P], start=True, stop=True)
                    last.then_inc(qk_done, 1)

                def weigh(h, kt):
                    if kt == 0:
                        pe.wait_ge(o_evac, b * T + (h + 1))
                    pe.wait_ge(exp_done, b * (T * KT) + (h * KT + kt + 1))
                    for g in range(4):
                        last = nc.tensor.matmul(psO[32 * g:32 * g + 32, 0:2 * P], v[par][:, h, kt, :],
                                                probs[kt % NPR][:, g * 2 * P:(g + 1) * 2 * P], start=(kt == 0), stop=(kt == KT - 1))
                    last.then_inc(pv_done, 1)

                def turn(h):
                    pe.wait_ge(o_evac, b * T + (h + 2))
                    take(uses)
                    for a in range(2):
                        last = nc.tensor.transpose(psA[:, a * P:(a + 1) * P], o_sb[:, a * P:(a + 1) * P], ident[:, :])
                    last.then_inc(ht_ps, 1)

                def turn_back(h):
                    take(uses)
                    nc.tensor.transpose(psA[:, 0:P], ctx_tm[:, :, :].rearrange("p j d -> p (j d)"), ident[:, :]).then_inc(ct_ps, 1)

                def project(h):
                    take(uses)
                    nc.tensor.matmul(psA[:, 0:P], ctxT[:, :], w_raw[:, 3, :], start=True, stop=True).then_inc(op_done, 1)

                for u in range(NSC - 1):
                    scores(u)
                for h in range(T):
                    for kt in range(KT):
                        if h * KT + kt + NSC - 1 < T * KT:
                            scores(h * KT + kt + NSC - 1)
                        weigh(h, kt)
                        if h and kt == 1:
                            turn(h - 1)
                        if h and kt == 4:
                            turn_back(h - 1)
                        if h and kt == 6:
                            project(h - 1)
                        if more and (h, kt) in STEPS:
                            embed_step(*STEPS[h, kt], b + 1, 1 - par, uses)
                turn(T - 1)
                turn_back(T - 1)
                project(T - 1)
                uses.ends(PSA_BATCH if more else PSA_BATCH - PSA_EMBED)

            pe.sem_inc(pv_done, NPR)
            pe.wait_ge(wsplit, 1)
            uses = Tally(0)
            for kind, ch in STEPS.values():
                embed_step(kind, ch, 0, 0, uses)
            uses.ends(PSA_EMBED)
            rounds(pe, batch)

        @block.vector
        def _(dve):
            dve.sem_inc(psA_free, 1)
            dve.sem_inc(o_evac, 1)
            for p in range(2):
                nc.vector.memset(v[p][:, :, :, :], 0.0)
                nc.vector.memset(ks[p][KQ:KG, :, :], 1.0)
            nc.vector.memset(negmax[:, :, :], 0.0)
            dve.drain()
            for p in range(2):
                nc.vector.memset(v[p][:, :, :, DH:DH + 1], 1.0)
            dve.wait_ge(w_in, N_W * 16)
            nc.vector.tensor_copy(pieces[:, :], pieces_f[:, :])
            split_f32r(nc, dve, wq_hi[:, :], wq_lo[:, :], w_raw[:, 0, :])
            split_f32r(nc, dve, wk_hi[:, :], wk_lo[:, :], w_raw[:, 1, :]).then_inc(wsplit, 1)

            def thirds(dst, src, scratch, begun=None):
                first = nc.vector.tensor_copy(dst[0], src)
                if begun is not None:
                    first.then_inc(begun, 1)
                dve.drain()
                nc.vector.tensor_tensor(scratch, src, dst[0], ALU.subtract)
                dve.drain()
                nc.vector.tensor_copy(dst[1], scratch)
                dve.drain()
                return nc.vector.tensor_tensor(dst[2], scratch, dst[1], ALU.subtract)

            def embed_read(kind, ch, b, par):
                n = b * CPB + (ch + 1)
                if kind == "E":
                    dve.wait_ge(emb_ps, n)
                    nc.vector.tensor_tensor(H[:, bass.ds(b * T + ch * TPC, TPC), :], psA[:, :].rearrange("p (i d) -> p i d", d=D),
                                            pe_tab[:, ch * TPC:(ch + 1) * TPC, :], ALU.add).then_inc(psA_free, 1)
                elif kind == "T":
                    dve.wait_ge(nt_ps, n)
                    nc.vector.tensor_copy(nT_hi[:, :], psA[:, :])
                    nc.vector.tensor_copy(nT[:, :], psA[:, :])
                    dve.drain()
                    nc.vector.tensor_tensor(nT_lo[:, :], psA[:, :], nT_hi[:, :].bitcast(F32), ALU.subtract).then_inc(psA_free, 1)
                elif kind in ("q", "k"):
                    i = "qk".index(kind)
                    dve.wait_ge((q_ps, k_ps)[i], n)
                    nc.vector.tensor_scalar(qf[i][:, :], psA[:, :], bcol[:, i:i + 1], (SCALE, 1.0)[i], ALU.add, ALU.mult).then_inc(psA_free, 1)
                elif kind == "N":
                    dve.wait_ge(n_ps, n)
                    nc.vector.tensor_reduce(norms2[:, ch:ch + 1], psA[0:64, :], AX, ALU.max).then_inc(psA_free, 1)
                else:
                    dve.wait_ge(v_ps, n)
                    nc.vector.tensor_tensor(v[par][:, ch * TPC:(ch + 1) * TPC, :, 0:DH], psA[:, :].rearrange("p (i j d) -> p i j d", j=KT, d=DH),
                                            brow[:, 0:1, :].rearrange("p o (j d) -> p o j d", d=DH).broadcast_to([P, TPC, KT, DH]),
                                            ALU.add).then_inc(psA_free, 1)

            def embed_rest(kind, ch, b, par, norms):
                n = b * CPB + (ch + 1)
                if kind == "E":
                    dve.drain()
                    normalise(nc, dve, lambda i: H[:, bass.ds(b * T + (ch * TPC + i), 1), :], lambda i: n0[par][:, ch * TPC + i:ch * TPC + i + 1, :],
                              stat, mv, veps, rs, var_done, rs_done, norms.next()).then_inc(n0_done, 1)
                elif kind in ("q", "k"):
                    i = "qk".index(kind)
                    dve.drain()
                    dve.wait_ge((qparts_out, kparts_out)[i], n * 16)
                    thirds([parts[i][:, a, :] for a in range(3)], qf[i][:, :], rem[:, :], (qf_done, kf_done)[i]).then_inc((qparts_done, kparts_done)[i], 1)
                elif kind == "N" and ch == CPB - 1:
                    dve.drain()
                    nc.vector.tensor_reduce(worst[:, :], norms2[:, :], AX, ALU.max)
                    dve.drain()
                    nc.vector.tensor_copy(pair2[:, 0:1], worst[0:32, :])
                    nc.vector.tensor_copy(pair2[:, 1:2], worst[32:64, :]).then_inc(norms_done, 1)

            def embed_step(kind, ch, b, par, norms):
                embed_read(kind, ch, b, par)
                embed_rest(kind, ch, b, par, norms)

            def finish(b, half_, norms):
                rows = [brow[:, i:i + 1, :].broadcast_to([P, TPC, D]) for i in range(5)]
                nc.vector.tensor_tensor(res[:, :, :], res[:, :, :], rows[1], ALU.add)
                dve.drain()
                normalise(nc, dve, lambda i: res[:, i, :], lambda i: res[:, i, :], stat, mv, veps, rs, var_done, rs_done, norms.next())
                dve.drain()
                nc.vector.tensor_tensor(res[:, :, :], res[:, :, :], rows[2], ALU.mult)
                dve.drain()
                nc.vector.tensor_tensor(res[:, :, :], res[:, :, :], rows[3], ALU.add)
                dve.drain()
                out = H[:, bass.ds(b * T + half_ * TPC, TPC), :]
                nc.vector.tensor_tensor(out, out, res[:, :, :], ALU.add)
                dve.drain()
                tiles = bass.ds(b * T + half_ * TPC, TPC)
                normalise(nc, dve, lambda i: H[:, bass.ds(b * T + (half_ * TPC + i), 1), :], lambda i: res[:, i:i + 1, :],
                          stat, mv, veps, rs, var_done, rs_done, norms.next())
                nc.vector.tensor_copy(mean1[:, tiles], mv[:, :, 0])
                nc.vector.tensor_copy(rstd1[:, tiles], rs[:, :])
                dve.drain()
                nc.vector.tensor_tensor(res[:, :, :], res[:, :, :], rows[4], ALU.mult)
                dve.drain()
                nc.vector.tensor_reduce(score1[:, tiles], res[:, :, :], AX, ALU.add)
                dve.drain()

            def maximum(b):
                for j in range(KT):
                    for h in range(T):
                        u = j * T + h
                        dve.wait_ge(pre_qk, b * (T * KT) + (u + 1))
                        nc.vector.tensor_reduce(negmax[:, j, h:h + 1], psS[u % 2][:, :, :].rearrange("p a n -> p (a n)"), AX, ALU.max,
                                                negate=True).then_inc(pre_max, 1)
                dve.wait_ge(gt_ps, b + 1)
                nc.vector.tensor_copy(gf[:, :], psA[0:T * KT, 0:P]).then_inc(psA_free, 1)
                dve.drain()
                thirds([gparts[:, a, :] for a in range(3)], gf[:, :], gr[:, :])

            def no_maximum():
                dve.sem_inc(pre_max, T * KT)
                dve.sem_inc(gt_ps, 1)
                dve.sem_inc(pre_qk, T * KT)
                nc.vector.memset(gparts[:, :, :], 0.0)
                dve.drain()
                dve.sem_inc(psA_free, 1)

            def batch(b, par, more):
                norms = Tally(RS_EMBED + b * RS_BATCH)
                dve.wait_ge(unsafe_done, b + 1)
                dve.sem_inc(waited, 1)
                with dve.If(dve.value_load(unsafe[0:1, 0:1], min_val=0, max_val=1)):
                    maximum(b)
                with dve.Else():
                    no_maximum()
                dve.drain()
                dve.sem_inc(gparts_done, 1)

                def out_of_psum(h):
                    dve.wait_ge(pv_done, b * (T * KT) + ((h + 1) * KT + NPR))
                    nc.vector.tensor_copy(o_sb[:, :], psO[:, 0:2 * P]).then_inc(o_evac, 1)

                def divide(h):
                    dve.wait_ge(ht_ps, b * T + (h + 1))
                    o = psA[:, 0:2 * P].rearrange("p (a g e) -> p a g e", a=2, e=32)
                    r = rden[:, :].rearrange("p (a g o) -> p a g o", a=2, o=1)
                    nc.vector.reciprocal(r, o[:, :, :, DH:DH + 1])
                    dve.drain()
                    nc.vector.tensor_tensor(ctx_tm[:, :, :].rearrange("p (g a) d -> p a g d", a=2), o[:, :, :, 0:DH],
                                            r.broadcast_to([P, 2, 4, DH]), ALU.mult).then_inc(psA_free, 1)

                def evacuate(h):
                    dve.wait_ge(ct_ps, b * T + (h + 1))
                    nc.vector.tensor_copy(ctxT[:, :], psA[:, 0:P]).then_inc(psA_free, 1)

                def add_input(h):
                    dve.wait_ge(op_done, b * T + (h + 1))
                    nc.vector.tensor_tensor(res[:, h % TPC, :], psA[:, 0:P], n0[par][:, h, :], ALU.add).then_inc(psA_free, 1)

                for h in range(T):
                    steps = [STEPS.get((h, kt)) if more else None for kt in (2, 5)]
                    if h:
                        out_of_psum(h - 1)
                        divide(h - 1)
                    for i, step in enumerate(steps):
                        if step:
                            embed_read(*step, b + 1, 1 - par)
                        if h:
                            (evacuate, add_input)[i](h - 1)
                        if step:
                            embed_rest(*step, b + 1, 1 - par, norms)
                    if h == TPC:
                        dve.drain()
                        finish(b, 0, norms)
                out_of_psum(T - 1)
                divide(T - 1)
                evacuate(T - 1)
                add_input(T - 1)
                dve.drain()
                finish(b, 1, norms)
                norms.ends(RS_BATCH if more else RS_BATCH - RS_EMBED)

            norms = Tally(0)
            for kind, ch in STEPS.values():
                embed_step(kind, ch, 0, 0, norms)
            norms.ends(RS_EMBED)
            rounds(dve, batch)


def rank(nc, dve, out, more, same, p, lower):
    shape = list(more.shape)
    mine, theirs = p.unsqueeze(3).broadcast_to(shape), p.unsqueeze(2).broadcast_to(shape)
    nc.vector.tensor_tensor(more, theirs, mine, ALU.is_gt)
    nc.vector.tensor_tensor(same, theirs, mine, ALU.is_equal)
    dve.drain()
    nc.vector.tensor_tensor(same, same, lower.unsqueeze(1).broadcast_to(shape), ALU.mult)
    dve.drain()
    nc.vector.tensor_tensor(more, more, same, ALU.add)
    dve.drain()
    return nc.vector.tensor_reduce(out, more, AX, ALU.add)


def sequence_experts(nc, H, ident, mean1, rstd1, score1, ins, B, S, D):
    E, _, HID = ins["w1"].shape
    NB = HID // P
    T = S // P
    NT = B * T
    CPB = S // CH
    K = 2
    IT = K * CPB
    assert NB == 4 and CPB == 2 and E == B == 8

    with ExitStack() as ctx:
        c = Core(nc, ctx, "f0")
        x_hi = [c.sb(f"x_hi{i}", [D, CH], F32R) for i in range(CPB)]
        x_lo = [c.sb(f"x_lo{i}", [D, CH], F32R) for i in range(CPB)]
        f = c.sb("f", [P, TPC, D])
        raw1 = [c.sb(f"raw1{r}", [D, HID]) for r in range(K)]
        raw2 = [c.sb(f"raw2{r}", [P, NB, D]) for r in range(K)]
        rawb = [c.sb(f"rawb{r}", [P, NB + 1]) for r in range(K)]
        bias = [c.sb(f"bias{r}", [P, NB + 1]) for r in range(K)]
        w1_hi = [c.sb(f"w1_hi{r}", [D, HID], F32R) for r in range(K)]
        w1_lo = [c.sb(f"w1_lo{r}", [D, HID], F32R) for r in range(K)]
        w2_hi = [c.sb(f"w2_hi{r}", [P, NB, D], F32R) for r in range(K)]
        w2_lo = [c.sb(f"w2_lo{r}", [P, NB, D], F32R) for r in range(K)]
        g = c.sb("g", [P, NB, CH])
        g_hi = [c.sb(f"g_hi{i}", [P, NB, CH], F32R) for i in range(2)]
        g_lo = [c.sb(f"g_lo{i}", [P, NB, CH], F32R) for i in range(2)]
        y = [c.sb(f"y{i}", [D, CH]) for i in range(2)]
        acc = [c.sb(f"acc{i}", [D, CH]) for i in range(CPB)]
        gate = c.sb("gate", [P, B, K])
        chosen = c.sb("chosen", [1, B * K], I32)
        attn_b, ones = c.sb("attn_b", [P, 1]), c.sb("ones", [P, P])
        sc, e_sc = c.sb("sc", [P, B, T]), c.sb("e_sc", [P, B, T])
        mx, mx_all, zs, rz, corr = (c.sb(n, [P, B]) for n in ("mx", "mx_all", "zs", "rz", "corr"))
        spread = c.sb("spread", [P, NT, B])
        own = c.sb("own", [P, NT, B])
        pooled, pooledT = c.sb("pooled", [B, D]), c.sb("pooledT", [D, B])
        gate_w, gate_b = c.sb("gate_w", [D, E]), c.sb("gate_b", [B, E])
        lg, pr = c.sb("lg", [B, E]), c.sb("pr", [B, 1, E])
        nmx, sm, rsm = c.sb("nmx", [B, 1]), c.sb("sm", [B, 1]), c.sb("rsm", [B, 1])
        beats, ties, rk = c.sb("beats", [B, 1, E, E]), c.sb("ties", [B, 1, E, E]), c.sb("rk", [B, 1, E])
        lower = c.sb("lower", [P, E, E])
        places = c.sb("places", [P, 2, K, E])
        sel, val = c.sb("sel", [B, K, E]), c.sb("val", [B, K, E])
        g2, i2, i2i = c.sb("g2", [B, K]), c.sb("i2", [B, K]), c.sb("i2i", [B, K], I32)
        d_gate = nc.dram_tensor("d_gate", [B, K], F32).ap()
        d_chosen = nc.dram_tensor("d_chosen", [B, K], I32).ap()

        psH = [c.ps(f"psH{i}", [P, CH]) for i in range(NB)]
        psY = [c.ps(f"psY{i}", [P, CH]) for i in range(2)]
        psX, psT = c.ps("psX", [P, CH]), c.ps("psT", [P, CH])

        (tab_in, step, mx_done, pool_done, exp_done, gate_out, gate_in, f_done, f_ps, x_done, h_ps, g_done, lo_done,
         y_ps, y_done, acc_done, t_ps, t_read) = (c.sem(n) for n in (
            "tab_in step mx_done pool_done exp_done gate_out gate_in f_done f_ps x_done h_ps g_done lo_done "
            "y_ps y_done acc_done t_ps t_read").split())
        raw1_in, raw2_in, w1_done, w2_done = ([c.sem(f"{n}{r}") for r in range(K)] for n in ("raw1_in", "raw2_in", "w1_done", "w2_done"))
        pe_gate, dve_gate = c.sem("pe_gate"), c.sem("dve_gate")
        ITEMS = [(r, ch) for r in range(K) for ch in range(CPB)]

        block = ctx.enter_context(nc.Block())

        def rounds(eng, batch):
            with eng.Fori(0, B - 1) as b:
                batch(b, True)
            batch(B - 1, False)

        @block.sync
        def _(sp):
            for dst, n in ((own[:, :, :], "own"), (lower[:, :, :], "lower"), (places[:, :, :, :], "places")):
                sp.dma_start(dst, ins[n]).then_inc(tab_in, 16)
            sp.dma_start(attn_b[:, :], ins["attn_b"].rearrange("(o d) -> o d", o=1).broadcast_to([P, 1])).then_inc(tab_in, 16)
            sp.dma_start(gate_w[:, :], ins["gate_w"]).then_inc(tab_in, 16)
            sp.dma_start(gate_b[:, :], ins["gate_b"].rearrange("(o d) -> o d", o=1).broadcast_to([B, E])).then_inc(tab_in, 16)
            sp.wait_ge(dve_gate, 6)
            sp.dma_start(d_gate, g2[:, :]).then_inc(gate_out, 16)
            sp.dma_start(d_chosen, i2i[:, :]).then_inc(gate_out, 16)
            sp.wait_ge(gate_out, 32)
            sp.dma_start(gate[:, :, :], d_gate.rearrange("(o b) k -> o b k", o=1).broadcast_to([P, B, K])).then_inc(gate_in, 16)
            sp.dma_start(chosen[:, :], d_chosen.rearrange("(o b) k -> o (b k)", o=1)).then_inc(gate_in, 16)
            sp.wait_ge(gate_in, 32)

            def load(b, r, which):
                e = sp.value_load(chosen[0:1, bass.ds(b * K + r, 1)], min_val=0, max_val=E - 1)
                if which == 1:
                    sp.dma_start(raw1[r][:, :], ins["w1"][bass.ds(e, 1), :, :].rearrange("o d h -> d (o h)")).then_inc(raw1_in[r], 16)
                else:
                    sp.dma_start(raw2[r][:, :, :], ins["w2"][bass.ds(e, 1), :, :].rearrange("o (n p) d -> p (o n) d", p=P)).then_inc(raw2_in[r], 16)
                    sp.dma_start(rawb[r][:, :], ins["b12"][bass.ds(e, 1), :, :].rearrange("o p n -> p (o n)")).then_inc(raw2_in[r], 16)

            def batch(b, more):
                if more:
                    for r in range(K):
                        sp.wait_ge(w1_done[r], b + 1)
                        sp.sem_inc(step, 1)
                        load(b + 1, r, 1)
                        sp.wait_ge(w2_done[r], b + 1)
                        sp.sem_inc(step, 1)
                        load(b + 1, r, 2)

            for r in range(K):
                load(0, r, 1)
                load(0, r, 2)
            rounds(sp, batch)

        @block.gpsimd
        def _(pool):
            pool.wait_ge(mx_done, 1)
            nc.gpsimd.partition_all_reduce(mx_all[:, :], mx[:, :], P, bass.bass_isa.ReduceOp.max).then_inc(pool_done, 1)

        @block.scalar
        def _(act):
            act.wait_ge(dve_gate, 1)
            nc.scalar.activation(e_sc[:, :, :], sc[:, :, :], ACT.Exp).then_inc(exp_done, 1)
            act.wait_ge(dve_gate, 5)
            nc.scalar.activation(pr[:, 0, :], lg[:, :], ACT.Exp, bias=nmx[:, :]).then_inc(exp_done, 1)

            def hidden(b, k):
                r, ch = ITEMS[k]
                act.wait_ge(w2_done[r], b + 1)
                for n in range(NB):
                    m = (b * IT + k) * NB + n
                    act.wait_ge(h_ps, m + 1)
                    act.wait_ge(y_ps, b * IT + (k + 1))
                    nc.scalar.activation(g_hi[k % 2][:, n, :], psH[n][:, :], ACT.Gelu, bias=bias[r][:, n:n + 1])
                    act.wait_ge(lo_done, m + 1)
                    nc.scalar.activation(g[:, n, :], psH[n][:, :], ACT.Gelu, bias=bias[r][:, n:n + 1]).then_inc(g_done, 1)

            def output(b, k):
                r, ch = ITEMS[k]
                act.wait_ge(y_ps, b * IT + (k + 3))
                act.wait_ge(acc_done, b * IT + (k + 1))
                nc.scalar.activation(y[k % 2][:, :], psY[k % 2][:, :], ACT.Gelu, bias=bias[r][:, NB:NB + 1]).then_inc(y_done, 1)

            def batch(b, more):
                for k in range(IT):
                    if k + 1 < IT:
                        hidden(b, k + 1)
                    elif more:
                        hidden(b + 1, 0)
                    output(b, k)

            hidden(0, 0)
            rounds(act, batch)

        @block.tensor
        def _(pe):
            pe.wait_ge(dve_gate, 2)
            nc.tensor.matmul(psT[:, 0:B], ones[:, :], zs[:, :], start=True, stop=True).then_inc(pe_gate, 1)
            pe.wait_ge(dve_gate, 3)
            for n in range(NT):
                nc.tensor.matmul(psT[0:B, 0:D], spread[:, n, :], H[:, n, :], start=(n == 0), stop=False)
            nc.tensor.matmul(psT[0:B, 0:D], corr[:, :], ones[:, :], start=False, stop=True).then_inc(pe_gate, 1)
            pe.wait_ge(dve_gate, 4)
            nc.tensor.transpose(psX[:, 0:B], pooled[:, :], ident[0:B, 0:B]).then_inc(pe_gate, 1)
            pe.wait_ge(x_done, 1)
            nc.tensor.matmul(psT[0:B, 0:E], pooledT[:, :], gate_w[:, :], start=True, stop=True).then_inc(pe_gate, 1)

            def first(b, k, n):
                r, ch = ITEMS[k]
                if n == 0:
                    pe.wait_ge(w1_done[r], b + 1)
                    pe.wait_ge(x_done, b * CPB + (ch + 2))
                pe.wait_ge(g_done, (b * IT + k) * NB + (n + 1))
                product(nc, psH[n][:, :], w1_hi[r][:, n * P:(n + 1) * P], w1_lo[r][:, n * P:(n + 1) * P],
                        x_hi[ch][:, :], x_lo[ch][:, :]).then_inc(h_ps, 1)

            def second(b, k, n):
                r, ch = ITEMS[k]
                if n == 0:
                    pe.wait_ge(w2_done[r], b + 1)
                    pe.wait_ge(y_done, b * IT + (k + 1))
                pe.wait_ge(lo_done, (b * IT + k) * NB + (n + 1 + NB))
                last = product(nc, psY[k % 2][:, :], w2_hi[r][:, n, :], w2_lo[r][:, n, :], g_hi[k % 2][:, n, :],
                               g_lo[k % 2][:, n, :], first=(n == 0), last=(n == NB - 1))
                if n == NB - 1:
                    last.then_inc(y_ps, 1)

            def turn_x(b, ch):
                pe.wait_ge(f_done, b * CPB + (ch + 1))
                pe.wait_ge(x_done, b * CPB + (ch + 1))
                for i in range(TPC):
                    last = nc.tensor.transpose(psX[:, i * P:(i + 1) * P], f[:, i, :], ident[:, :])
                last.then_inc(f_ps, 1)

            def turn_y(b, ch):
                pe.wait_ge(acc_done, b * IT + (CPB + ch + 3))
                pe.wait_ge(t_read, b * CPB + (ch + 1))
                for i in range(TPC):
                    last = nc.tensor.transpose(psT[:, i * P:(i + 1) * P], acc[ch][:, i * P:(i + 1) * P], ident[:, :])
                last.then_inc(t_ps, 1)

            def batch(b, more):
                for k in range(IT):
                    for n in range(NB):
                        if k + 1 < IT:
                            first(b, k + 1, n)
                        elif more:
                            first(b + 1, 0, n)
                        second(b, k, n)
                    if more and k >= CPB:
                        turn_x(b + 1, k - CPB)
                    if k == IT - 1:
                        turn_y(b, 0)
                turn_y(b, 1)

            pe.sem_inc(y_ps, 2)
            pe.wait_ge(pe_gate, 4)
            for ch in range(CPB):
                turn_x(0, ch)
            for n in range(NB):
                first(0, 0, n)
            rounds(pe, batch)

        @block.vector
        def _(dve):
            nc.vector.memset(ones[:, :], 1.0)
            dve.sem_inc(lo_done, NB)
            dve.sem_inc(acc_done, 2)
            dve.sem_inc(t_read, 1)
            dve.sem_inc(g_done, NB)
            dve.sem_inc(y_done, 2)
            dve.wait_ge(tab_in, 16 * 6)
            nc.vector.tensor_scalar(sc[:, :, :], score1[:, :].rearrange("p (b t) -> p b t", b=B), attn_b[:, :], None, ALU.add)
            dve.drain()
            nc.vector.tensor_reduce(mx[:, :], sc[:, :, :], AX, ALU.max).then_inc(mx_done, 1)
            dve.wait_ge(pool_done, 1)
            nc.vector.tensor_tensor(sc[:, :, :], sc[:, :, :], mx_all[:, :].unsqueeze(2).broadcast_to([P, B, T]), ALU.subtract).then_inc(dve_gate, 1)
            dve.wait_ge(exp_done, 1)
            nc.vector.tensor_reduce(zs[:, :], e_sc[:, :, :], AX, ALU.add).then_inc(dve_gate, 1)
            dve.wait_ge(pe_gate, 1)
            nc.vector.reciprocal(rz[:, :], psT[:, 0:B])
            dve.drain()
            nc.vector.tensor_tensor(e_sc[:, :, :], e_sc[:, :, :], rz[:, :].unsqueeze(2).broadcast_to([P, B, T]), ALU.mult)
            dve.drain()
            nc.vector.tensor_tensor(e_sc[:, :, :], e_sc[:, :, :], rstd1[:, :].rearrange("p (b t) -> p b t", b=B), ALU.mult)
            dve.drain()
            nc.vector.tensor_tensor(sc[:, :, :], e_sc[:, :, :], mean1[:, :].rearrange("p (b t) -> p b t", b=B), ALU.mult)
            dve.drain()
            nc.vector.tensor_reduce(corr[:, :], sc[:, :, :], AX, ALU.add, negate=True)
            nc.vector.tensor_tensor(spread[:, :, :], own[:, :, :], e_sc[:, :, :].rearrange("p b t -> p (b t)").unsqueeze(2).broadcast_to([P, NT, B]),
                                    ALU.mult).then_inc(dve_gate, 1)
            dve.wait_ge(pe_gate, 2)
            nc.vector.tensor_copy(pooled[:, :], psT[0:B, 0:D]).then_inc(dve_gate, 1)
            dve.wait_ge(pe_gate, 3)
            nc.vector.tensor_copy(pooledT[:, :], psX[:, 0:B]).then_inc(x_done, 1)
            dve.wait_ge(pe_gate, 4)
            nc.vector.tensor_tensor(lg[:, :], psT[0:B, 0:E], gate_b[:, :], ALU.add)
            dve.drain()
            nc.vector.tensor_reduce(nmx[:, :], lg[:, :], AX, ALU.max, negate=True).then_inc(dve_gate, 1)
            dve.wait_ge(exp_done, 2)
            nc.vector.tensor_reduce(sm[:, :], pr[:, 0, :], AX, ALU.add)
            dve.drain()
            nc.vector.reciprocal(rsm[:, :], sm[:, :])
            dve.drain()
            nc.vector.tensor_scalar(pr[:, 0, :], pr[:, 0, :], rsm[:, :], None, ALU.mult)
            dve.drain()
            rank(nc, dve, rk[:, :, :], beats[:, :, :, :], ties[:, :, :, :], pr[:, :, :], lower[0:B, :, :])
            dve.drain()
            nc.vector.tensor_tensor(sel[:, :, :], rk[:, :, :].broadcast_to([B, K, E]), places[0:B, 0, :, :], ALU.is_equal)
            dve.drain()
            nc.vector.tensor_tensor(val[:, :, :], sel[:, :, :], pr[:, :, :].broadcast_to([B, K, E]), ALU.mult)
            dve.drain()
            nc.vector.tensor_reduce(g2[:, :], val[:, :, :], AX, ALU.add)
            dve.drain()
            nc.vector.tensor_tensor(val[:, :, :], sel[:, :, :], places[0:B, 1, :, :], ALU.mult)
            dve.drain()
            nc.vector.tensor_reduce(i2[:, :], val[:, :, :], AX, ALU.add)
            nc.vector.tensor_reduce(sm[:, :], g2[:, :], AX, ALU.add)
            dve.drain()
            nc.vector.tensor_copy(i2i[:, :], i2[:, :])
            nc.vector.tensor_scalar(sm[:, :], sm[:, :], 1e-9, None, ALU.add)
            dve.drain()
            nc.vector.reciprocal(rsm[:, :], sm[:, :])
            dve.drain()
            nc.vector.tensor_scalar(g2[:, :], g2[:, :], rsm[:, :], None, ALU.mult).then_inc(dve_gate, 1)

            def split_w1(b, r):
                dve.wait_ge(raw1_in[r], (b + 1) * 16)
                split_f32r(nc, dve, w1_hi[r][:, :], w1_lo[r][:, :], raw1[r][:, :]).then_inc(w1_done[r], 1)

            def split_w2(b, r):
                dve.wait_ge(raw2_in[r], (b + 1) * 32)
                nc.vector.tensor_copy(bias[r][:, :], rawb[r][:, :])
                split_f32r(nc, dve, w2_hi[r][:, :, :], w2_lo[r][:, :, :], raw2[r][:, :, :]).then_inc(w2_done[r], 1)

            def normal_x(b, ch):
                for i in range(TPC):
                    n = b * T + (ch * TPC + i)
                    last = nc.vector.tensor_scalar(f[:, i:i + 1, :], H[:, bass.ds(n, 1), :], mean1[:, bass.ds(n, 1)], rstd1[:, bass.ds(n, 1)],
                                                   ALU.subtract, ALU.mult)
                last.then_inc(f_done, 1)

            def split_x(b, ch):
                dve.wait_ge(f_ps, b * CPB + (ch + 1))
                split_f32r(nc, dve, x_hi[ch][:, :], x_lo[ch][:, :], psX[:, :]).then_inc(x_done, 1)

            def lows(b, k):
                for n in range(NB):
                    dve.wait_ge(g_done, (b * IT + k) * NB + (n + 1 + NB))
                    nc.vector.tensor_tensor(g_lo[k % 2][:, n, :], g[:, n, :], g_hi[k % 2][:, n, :].bitcast(F32), ALU.subtract).then_inc(lo_done, 1)

            def weigh(b, k):
                r, ch = ITEMS[k]
                dve.wait_ge(y_done, b * IT + (k + 3))
                gr = gate[:, bass.ds(b, 1), r]
                if r == 0:
                    nc.vector.tensor_scalar(acc[ch][:, :], y[k % 2][:, :], gr, None, ALU.mult).then_inc(acc_done, 1)
                else:
                    nc.vector.scalar_tensor_tensor(acc[ch][:, :], y[k % 2][:, :], gr, acc[ch][:, :], ALU.mult, ALU.add).then_inc(acc_done, 1)

            def add(b, ch):
                dve.wait_ge(t_ps, b * CPB + (ch + 1))
                out = H[:, bass.ds(b * T + ch * TPC, TPC), :]
                nc.vector.tensor_tensor(out, out, psT[:, :].rearrange("p (i d) -> p i d", d=D), ALU.add).then_inc(t_read, 1)

            def batch(b, more):
                for k in range(IT):
                    if k == 0:
                        split_w1(b, 1)
                    if k + 1 < IT:
                        lows(b, k + 1)
                    elif more:
                        lows(b + 1, 0)
                    if k == 1 and more:
                        dve.wait_ge(h_ps, (b * IT + 2) * NB)
                        split_w1(b + 1, 0)
                    if k == 0:
                        dve.wait_ge(y_ps, b * IT + 2)
                        split_w2(b, 1)
                    if k == 2 and more:
                        dve.wait_ge(y_done, b * IT + 4)
                        split_w2(b + 1, 0)
                    if more and k >= CPB:
                        normal_x(b + 1, k - CPB)
                    weigh(b, k)
                    if more and k >= CPB:
                        split_x(b + 1, k - CPB)
                for ch in range(CPB):
                    add(b, ch)

            dve.wait_ge(gate_in, 32)
            for ch in range(CPB):
                normal_x(0, ch)
                split_x(0, ch)
            split_w1(0, 0)
            split_w2(0, 0)
            lows(0, 0)
            rounds(dve, batch)


def block_attention(nc, H, zd, gates, ident, half, ins, B, S, D):
    SB = 32
    SG = P // SB
    T = S // P
    G = SB // SG
    E = ins["Wr"].shape[1]
    CPB = S // CH
    SCALE = float(D // 8) ** -0.5
    assert S == SB * SB and G == T and CPB == 2

    with ExitStack() as ctx:
        c = Core(nc, ctx, "a1")
        f, xT = c.sb("f", [P, T, D]), c.sb("xT", [D, S])
        x_hi, x_lo = c.sb("x_hi", [D, S], F32R), c.sb("x_lo", [D, S], F32R)
        w_qk, w_v, w_proj, w_r = c.sb("w_qk", [D, 2, D]), c.sb("w_v", [D, D]), c.sb("w_proj", [D, D]), c.sb("w_r", [D, E])
        w_hi, w_lo = c.sb("w_hi", [D, 2, D], F32R), c.sb("w_lo", [D, 2, D], F32R)
        bcol = c.sb("bcol", [D, 3])
        brow, ones = c.sb("brow", [1, CH]), c.sb("ones", [1, P])
        lower = c.sb("lower", [P, E, E])
        qk = [c.sb(n, [D, S]) for n in ("q", "k")]
        v = c.sb("v", [P, G, D])
        mx, sm = c.sb("mx", [P, G]), c.sb("sm", [P, G])
        sc, pr = c.sb("sc", [P, G, SB]), c.sb("pr", [P, G, SB])
        diag = c.sb("diag", [P, G, P])
        oT, zT = c.sb("oT", [D, S]), c.sb("zT", [D, S])
        zrow = c.sb("zrow", [P, T, D])
        stat, mv = c.sb("stat", [P, TPC, 6]), c.sb("mv", [P, TPC, 2])
        veps, rs = c.sb("veps", [P, TPC]), c.sb("rs", [P, TPC])
        lg, el = c.sb("lg", [P, T, E]), c.sb("el", [P, T, E])
        beats, ties = c.sb("beats", [P, T, E, E]), c.sb("ties", [P, T, E, E])
        rk, gm, gs = c.sb("rk", [P, T, E]), c.sb("gm", [P, T]), c.sb("gs", [P, T])

        psX = [c.ps(f"psX{i}", [P, CH]) for i in range(2)]
        psQ = [c.ps(f"psQ{i}", [P, CH]) for i in range(2)]
        psO = [c.ps(f"psO{i}", [P, CH]) for i in range(2)]
        psS, psP = c.ps("psS", [P, CH]), c.ps("psP", [P, CH])
        SC = G * SB

        (w_in, ready, var_done, rs_done, f_done, x_ps, x_done, qk_ps, qk_done, v_ps, v_done, s_ps, sub_done, exp_done,
         diag_done, o_ps, o_done, p_ps, h_done, zn_done, z_ps, z_done, l_ps, lsub_done, lexp_done, z_out, sent) = (c.sem(n) for n in (
            "w_in ready var_done rs_done f_done x_ps x_done qk_ps qk_done v_ps v_done s_ps sub_done exp_done "
            "diag_done o_ps o_done p_ps h_done zn_done z_ps z_done l_ps lsub_done lexp_done z_out sent").split())

        def rounds(eng, iteration):
            iteration(0, False, True, True)
            with eng.Fori(1, B - 2) as b:
                iteration(b, True, True, True)
            iteration(B - 2, True, True, False)
            iteration(B - 1, True, False, False)

        def roots_before(b):
            return 2 * CPB + b * 2 * CPB if not isinstance(b, int) or b < B - 1 else 2 * CPB + (B - 2) * 2 * CPB + CPB

        block = ctx.enter_context(nc.Block())

        @block.sync
        def _(sp):
            for dst, n in ((w_qk[:, :, :], "Wqk"), (w_v[:, :], "Wv1"), (w_proj[:, :], "Wproj"), (w_r[:, :], "Wr"),
                           (bcol[:, :], "b_qkv"), (lower[:, :, :], "lower")):
                sp.dma_start(dst, ins[n]).then_inc(w_in, 16)
            sp.dma_start(brow[:, :].rearrange("o (i d) -> o i d", d=D),
                         ins["b_proj"].rearrange("(o i d) -> o i d", o=1, i=1).broadcast_to([1, TPC, D])).then_inc(w_in, 16)

            def iteration(b, z, one, two):
                sp.wait_ge(zn_done, (b + 1) * CPB)
                sp.dma_start(zd[bass.ds(b * T, T), :, :].rearrange("t p d -> p t d"), zrow[:, :, :]).then_inc(z_out, 16)
                sp.wait_ge(z_out, b * 16 + 16)
                sp.sem_inc(sent, 1)

            rounds(sp, iteration)

        @block.gpsimd
        def _(pool):
            def root(n):
                pool.wait_ge(var_done, n)
                nc.gpsimd.tensor_tensor(rs[:, :], veps[:, :], half[:, 0:TPC], ALU.pow).then_inc(rs_done, 1)

            def iteration(b, z, one, two):
                for i in range(2 * CPB if two else CPB):
                    root(roots_before(b) + (i + 1))

            for i in range(2 * CPB):
                root(i + 1)
            rounds(pool, iteration)

        @block.scalar
        def _(act):
            def project_read(n):
                if not (isinstance(n, int) and n == 0):
                    act.wait_ge(s_ps, n)
                for m in range(4):
                    act.wait_ge(qk_ps, n * 4 + (m + 1))
                    ch, i = divmod(m, 2)
                    nc.scalar.activation(qk[i][:, ch * CH:(ch + 1) * CH], psQ[m % 2][:, :], ACT.Identity, bias=bcol[:, i:i + 1]).then_inc(qk_done, 1)
                act.wait_ge(o_ps, n * 2 + 1)
                for h in range(2):
                    act.wait_ge(v_ps, n * 2 + (h + 1))
                    nc.scalar.activation(v[:, h * TPC:(h + 1) * TPC, :], psX[h][:, :].rearrange("p (i d) -> p i d", d=D), ACT.Copy).then_inc(v_done, 1)

            def route_exp(n):
                act.wait_ge(lsub_done, n + 1)
                nc.scalar.activation(el[:, :, :], lg[:, :, :], ACT.Exp).then_inc(lexp_done, 1)

            def iteration(b, z, one, two):
                act.wait_ge(sub_done, b + 1)
                nc.scalar.activation(pr[:, :, :], sc[:, :, :], ACT.Exp, scale=SCALE).then_inc(exp_done, 1)
                tokens = oT[:, :].rearrange("d (i s) -> d s i", s=SB)
                act.wait_ge(p_ps, b * 2 + 1)
                for h in range(2):
                    act.wait_ge(o_ps, b * 2 + (h + 2))
                    nc.scalar.activation(tokens[:, h * SB // 2:(h + 1) * SB // 2, :], psO[h][:, :].rearrange("d (s i) -> d s i", i=SB), ACT.Identity, bias=bcol[:, 2:3]).then_inc(o_done, 1)
                if one:
                    project_read(b + 1)
                if z:
                    route_exp(b - 1)

            act.sem_inc(o_done, 2)
            act.wait_ge(w_in, 16 * 7)
            project_read(0)
            rounds(act, iteration)
            route_exp(B - 1)

        @block.tensor
        def _(pe):
            def turn(n, free):
                for ch in range(CPB):
                    pe.wait_ge(f_done, n * CPB + (ch + 1))
                    if free is not None:
                        pe.wait_ge(free[0], free[1] + ch)
                    for i in range(TPC):
                        last = nc.tensor.transpose(psX[ch][:, i * P:(i + 1) * P], f[:, ch * TPC + i, :], ident[:, :])
                    last.then_inc(x_ps, 1)

            def turn_z(n):
                for ch in range(CPB):
                    pe.wait_ge(zn_done, n * CPB + (ch + 1))
                    for i in range(TPC):
                        last = nc.tensor.transpose(psX[ch][:, i * P:(i + 1) * P], zrow[:, ch * TPC + i, :], ident[:, :])
                    last.then_inc(z_ps, 1)

            def project(n):
                first = isinstance(n, int) and n == 0
                for m in range(4):
                    ch, i = divmod(m, 2)
                    pe.wait_ge(x_done, n * CPB + (ch + 1))
                    if not first or m >= 2:
                        pe.wait_ge(qk_done, n * 4 + (m - 1))
                    cols = slice(ch * CH, (ch + 1) * CH)
                    product(nc, psQ[m % 2][:, :], w_hi[:, i, :], w_lo[:, i, :], x_hi[:, cols], x_lo[:, cols]).then_inc(qk_ps, 1)

            def place(src, s):
                return src[:, :].rearrange("d (i s) -> d s i", s=SB)[:, s, :]

            def values(n):
                for g in range(G):
                    last = nc.tensor.matmul(psX[g // TPC][:, g % TPC * D:(g % TPC + 1) * D], xT[:, g * P:(g + 1) * P], w_v[:, :], start=True, stop=True)
                    if g % TPC == TPC - 1:
                        last.then_inc(v_ps, 1)

            def scores(n):
                pe.wait_ge(qk_done, n * 4 + 4)
                if not (isinstance(n, int) and n == 0):
                    pe.wait_ge(sub_done, n)
                for g in range(G):
                    for a in range(SG):
                        last = nc.tensor.matmul(psS[a * SB:(a + 1) * SB, g * SB:(g + 1) * SB], place(qk[0], g * SG + a), place(qk[1], g * SG + a),
                                                start=True, stop=True)
                last.then_inc(s_ps, 1)

            def attend(b):
                pe.wait_ge(diag_done, b + 1)
                pe.wait_ge(v_done, b * 2 + 2)
                for h in range(2):
                    pe.wait_ge(o_done, b * 2 + (h + 1))
                    for i in range(TPC):
                        g = h * TPC + i
                        last = nc.tensor.matmul(psO[h][:, i * P:(i + 1) * P], v[:, g, :], diag[:, g, :], start=True, stop=True)
                    last.then_inc(o_ps, 1)

            def output(b):
                pe.wait_ge(o_done, b * 2 + 4)
                for h in range(2):
                    pe.wait_ge(h_done, b * 2 + (h + 1))
                    nc.tensor.matmul(psP[:, :], ones[:, :], brow[:, :], start=True, stop=False)
                    for i in range(TPC):
                        t = h * TPC + i
                        last = nc.tensor.matmul(psP[:, i * P:(i + 1) * P], oT[:, t * P:(t + 1) * P], w_proj[:, :], start=False, stop=(i == TPC - 1))
                    last.then_inc(p_ps, 1)

            def logits(n):
                pe.wait_ge(z_done, (n + 1) * CPB)
                for t in range(T):
                    last = nc.tensor.matmul(psS[:, SC + t * E:SC + (t + 1) * E], zT[:, t * P:(t + 1) * P], w_r[:, :], start=True, stop=True)
                last.then_inc(l_ps, 1)

            def iteration(b, z, one, two):
                if z:
                    pe.wait_ge(v_done, b * 2 + 2)
                    turn_z(b - 1)
                attend(b)
                if one:
                    turn(b + 1, (z_done, b * CPB - (CPB - 1)) if z else (v_done, 1))
                    project(b + 1)
                output(b)
                if one:
                    values(b + 1)
                if z:
                    logits(b - 1)
                if one:
                    scores(b + 1)

            pe.sem_inc(o_ps, 1)
            pe.sem_inc(p_ps, 1)
            pe.wait_ge(ready, 1)
            turn(0, None)
            project(0)
            values(0)
            scores(0)
            rounds(pe, iteration)
            pe.wait_ge(z_done, (B - 1) * CPB)
            turn_z(B - 1)
            logits(B - 1)

        @block.vector
        def _(dve):
            norms = Tally(0)

            def normal(n, dst, done, turns):
                for ch in range(CPB):
                    normalise(nc, dve, lambda i: H[:, bass.ds(n * T + (ch * TPC + i), 1), :], dst(ch),
                              stat, mv, veps, rs, var_done, rs_done, turns.next()).then_inc(done, 1)

            def normal_x(n, turns):
                normal(n, lambda ch: lambda i: f[:, ch * TPC + i:ch * TPC + i + 1, :], f_done, turns)

            def normal_z(n, turns):
                if not (isinstance(n, int) and n == 0):
                    dve.wait_ge(z_ps, n * CPB)
                    dve.wait_ge(z_out, n * 16)
                normal(n, lambda ch: lambda i: zrow[:, ch * TPC + i:ch * TPC + i + 1, :], zn_done, turns)

            def split_x(n):
                if not (isinstance(n, int) and n == 0):
                    dve.wait_ge(v_ps, n * 2)
                for ch in range(CPB):
                    cols = slice(ch * CH, (ch + 1) * CH)
                    dve.wait_ge(x_ps, n * CPB + (ch + 1))
                    nc.vector.tensor_copy(x_hi[:, cols], psX[ch][:, :])
                    nc.vector.tensor_copy(xT[:, :].rearrange("d (s i) -> d i s", i=SB)[:, ch * SB // 2:(ch + 1) * SB // 2, :],
                                          psX[ch][:, :].rearrange("d (i s) -> d i s", s=SB))
                    dve.drain()
                    nc.vector.tensor_tensor(x_lo[:, cols], psX[ch][:, :], x_hi[:, cols].bitcast(F32), ALU.subtract).then_inc(x_done, 1)

            def copy_z(n):
                for ch in range(CPB):
                    dve.wait_ge(z_ps, n * CPB + (ch + 1))
                    nc.vector.tensor_copy(zT[:, ch * CH:(ch + 1) * CH], psX[ch][:, :]).then_inc(z_done, 1)

            def attention(b):
                s = psS[:, 0:SC].rearrange("p (g j) -> p g j", j=SB)
                dve.wait_ge(s_ps, b + 1)
                nc.vector.tensor_reduce(mx[:, :], s, AX, ALU.max)
                dve.drain()
                nc.vector.tensor_tensor(sc[:, :, :], s, mx[:, :].unsqueeze(2).broadcast_to([P, G, SB]), ALU.subtract).then_inc(sub_done, 1)
                dve.wait_ge(exp_done, b + 1)
                nc.vector.tensor_reduce(sm[:, :], pr[:, :, :], AX, ALU.add)
                dve.drain()
                nc.vector.reciprocal(sm[:, :], sm[:, :])
                dve.drain()
                nc.vector.tensor_tensor(pr[:, :, :], pr[:, :, :], sm[:, :].unsqueeze(2).broadcast_to([P, G, SB]), ALU.mult)
                dve.drain()
                dve.wait_ge(o_ps, b * 2 + 1)
                for a in range(SG):
                    rows = slice(a * SB, (a + 1) * SB)
                    last = nc.vector.transpose(diag[rows, :, rows], pr[rows, :, :])
                last.then_inc(diag_done, 1)

            def add(b):
                for h in range(2):
                    dve.wait_ge(p_ps, b * 2 + (h + 2))
                    out = H[:, bass.ds(b * T + h * TPC, TPC), :]
                    nc.vector.tensor_tensor(out, out, psP[:, :].rearrange("p (i d) -> p i d", d=D), ALU.add).then_inc(h_done, 1)

            def route(n, one):
                dve.wait_ge(l_ps, n + 1)
                if one:
                    dve.wait_ge(s_ps, n + 3)
                whole = [P, T, E]
                nc.vector.tensor_copy(lg[:, :, :], psS[:, SC:SC + T * E].rearrange("p (t e) -> p t e", e=E))
                dve.drain()
                rank(nc, dve, rk[:, :, :], beats[:, :, :, :], ties[:, :, :, :], lg[:, :, :], lower[:, :, :])
                nc.vector.tensor_reduce(gm[:, :], lg[:, :, :], AX, ALU.max)
                dve.drain()
                nc.vector.tensor_tensor(lg[:, :, :], lg[:, :, :], gm[:, :].unsqueeze(2).broadcast_to(whole), ALU.subtract).then_inc(lsub_done, 1)
                nc.vector.tensor_scalar(rk[:, :, :], rk[:, :, :], 2.0, None, ALU.is_lt)
                dve.drain()
                dve.wait_ge(lexp_done, n + 1)
                nc.vector.tensor_tensor(el[:, :, :], el[:, :, :], rk[:, :, :], ALU.mult)
                dve.drain()
                nc.vector.tensor_reduce(gs[:, :], el[:, :, :], AX, ALU.add)
                dve.drain()
                nc.vector.reciprocal(gs[:, :], gs[:, :])
                dve.drain()
                nc.vector.tensor_tensor(gates[:, bass.ds(n * T, T), :], el[:, :, :], gs[:, :].unsqueeze(2).broadcast_to(whole), ALU.mult)
                dve.drain()

            def iteration(b, z, one, two):
                turns = Tally(roots_before(b))
                attention(b)
                if z:
                    copy_z(b - 1)
                if one:
                    split_x(b + 1)
                if two:
                    normal_x(b + 2, turns)
                add(b)
                if z:
                    route(b - 1, one)
                dve.drain()
                normal_z(b, turns)
                turns.ends(2 * CPB if two else CPB)

            dve.sem_inc(h_done, 1)
            nc.vector.memset(diag[:, :, :], 0.0)
            nc.vector.memset(ones[:, :], 1.0)
            dve.wait_ge(w_in, 16 * 7)
            split_f32r(nc, dve, w_hi[:, :, :], w_lo[:, :, :], w_qk[:, :, :]).then_inc(ready, 1)
            turns = Tally(0)
            normal_x(0, turns)
            split_x(0)
            normal_x(1, turns)
            rounds(dve, iteration)
            copy_z(B - 1)
            route(B - 1, False)


def token_experts(nc, H, zd, gates, ident, ins, B, S, D):
    E, _, HID = ins["W1"].shape
    NB = HID // P
    C = B * S // CH
    TURN = 4
    assert NB == 4 and C % 2 == 0

    with ExitStack() as ctx:
        c = Core(nc, ctx, "f1")
        raw1, raw2 = c.sb("raw1", [D, HID]), c.sb("raw2", [P, NB, D])
        w1_hi, w1_lo = ([c.sb(f"{n}{e}", [D, HID], F32R) for e in range(E)] for n in ("w1_hi", "w1_lo"))
        w2_hi, w2_lo = ([c.sb(f"{n}{e}", [P, NB, D], F32R) for e in range(E)] for n in ("w2_hi", "w2_lo"))
        bias = c.sb("bias", [P, E, NB + 1])
        x_hi, x_lo = ([c.sb(f"{n}{i}", [D, CH], F32R) for i in range(2)] for n in ("x_hi", "x_lo"))
        g = c.sb("g", [P, NB, CH])
        g_hi, g_lo = ([c.sb(f"{n}{i}", [P, NB, CH], F32R) for i in range(2)] for n in ("g_hi", "g_lo"))
        y = [c.sb(f"y{i}", [D, CH]) for i in range(2)]
        zc = [c.sb(f"zc{i}", [P, TPC, D]) for i in range(2)]

        psH = [c.ps(f"psH{i}", [P, CH]) for i in range(NB)]
        psY = [c.ps(f"psY{i}", [P, CH]) for i in range(2)]
        psX, psT = c.ps("psX", [P, CH]), c.ps("psT", [P, CH])
        b_in, w1_in, w2_in, w_done, x_ps, x_done, h_ps, g_done, lo_done, y_ps, y_done, t_ps, t_read = (c.sem(n) for n in (
            "b_in w1_in w2_in w_done x_ps x_done h_ps g_done lo_done y_ps y_done t_ps t_read").split())
        z_in = [c.sem(f"z_in{i}") for i in range(2)]

        block = ctx.enter_context(nc.Block())

        def rounds(eng, chunk):
            with eng.Fori(0, C // 2 - 1) as it:
                for par in range(2):
                    chunk(it * 2 + par, par, True)
            for par in range(2):
                chunk(C - 2 + par, par, par == 0)

        @block.sync
        def _(sp):
            def load(q, par):
                sp.dma_start(zc[par][:, :, :], zd[bass.ds(q * TPC, TPC), :, :].rearrange("t p d -> p t d")).then_inc(z_in[par], 16)

            def chunk(q, par, more):
                if not isinstance(q, int):
                    sp.wait_ge(x_ps, q + 1)
                    load(q + 2, par)

            for q in range(2):
                load(q, q)
            sp.dma_start(bias[:, :, :], ins["B12"].rearrange("e p n -> p e n")).then_inc(b_in, 16)
            for e in range(E):
                if e:
                    sp.wait_ge(w_done, e)
                sp.dma_start(raw1[:, :], ins["W1"][e]).then_inc(w1_in, 16)
                sp.dma_start(raw2[:, :, :], ins["W2"][e].rearrange("(n p) d -> p n d", p=P)).then_inc(w2_in, 16)
            rounds(sp, chunk)

        @block.scalar
        def _(act):
            def hidden(m, e):
                act.wait_ge(y_ps, m + 1)
                for n in range(NB):
                    act.wait_ge(h_ps, m * NB + (n + 1))
                    nc.scalar.activation(g_hi[e % 2][:, n, :], psH[n][:, :], ACT.Gelu, bias=bias[:, e, n:n + 1])
                    act.wait_ge(lo_done, m * NB + (n + 1))
                    nc.scalar.activation(g[:, n, :], psH[n][:, :], ACT.Gelu, bias=bias[:, e, n:n + 1]).then_inc(g_done, 1)

            def output(m, e):
                act.wait_ge(y_ps, m + 3)
                act.wait_ge(t_ps, m + 1)
                nc.scalar.activation(y[e % 2][:, :], psY[e % 2][:, :], ACT.Identity, bias=bias[:, e, NB:NB + 1]).then_inc(y_done, 1)

            def chunk(q, par, more):
                for e in range(E):
                    if e + 1 < E or more:
                        hidden(q * E + (e + 1), (e + 1) % E)
                    output(q * E + e, e)

            act.wait_ge(b_in, 16)
            hidden(0, 0)
            rounds(act, chunk)

        @block.tensor
        def _(pe):
            def first(m, e, par, n):
                pe.wait_ge(g_done, m * NB + (n + 1))
                product(nc, psH[n][:, :], w1_hi[e][:, n * P:(n + 1) * P], w1_lo[e][:, n * P:(n + 1) * P],
                        x_hi[par][:, :], x_lo[par][:, :]).then_inc(h_ps, 1)

            def second(m, e, n):
                if n == 0:
                    pe.wait_ge(y_done, m + 1)
                pe.wait_ge(lo_done, m * NB + (n + 1 + NB))
                last = product(nc, psY[e % 2][:, :], w2_hi[e][:, n, :], w2_lo[e][:, n, :], g_hi[e % 2][:, n, :],
                               g_lo[e % 2][:, n, :], first=(n == 0), last=(n == NB - 1))
                if n == NB - 1:
                    last.then_inc(y_ps, 1)

            def turn_x(q, par):
                pe.wait_ge(z_in[par], (q - par) * 8 + 16)
                if not (isinstance(q, int) and q == 0):
                    pe.wait_ge(x_done, q)
                for i in range(TPC):
                    last = nc.tensor.transpose(psX[:, i * P:(i + 1) * P], zc[par][:, i, :], ident[:, :])
                last.then_inc(x_ps, 1)

            def turn_y(m, e):
                pe.wait_ge(y_done, m + 3)
                pe.wait_ge(t_read, m + 1)
                for i in range(TPC):
                    last = nc.tensor.transpose(psT[:, i * P:(i + 1) * P], y[e % 2][:, i * P:(i + 1) * P], ident[:, :])
                last.then_inc(t_ps, 1)

            def chunk(q, par, more, start=False):
                for e in range(E):
                    m = q * E + e
                    for n in range(NB):
                        if e + 1 < E:
                            first(m + 1, e + 1, par, n)
                        elif more:
                            if n == 0:
                                pe.wait_ge(x_done, q + 2)
                            first(m + 1, 0, 1 - par, n)
                        second(m, e, n)
                    if e or not start:
                        turn_y(m - 1, (e - 1) % E)
                    if more and e == TURN:
                        turn_x(q + 1, 1 - par)
                if not more:
                    turn_y(q * E + (E - 1), E - 1)

            pe.sem_inc(y_ps, 2)
            pe.sem_inc(t_ps, 2)
            turn_x(0, 0)
            pe.wait_ge(w_done, E)
            pe.wait_ge(x_done, 1)
            for n in range(NB):
                first(0, 0, 0, n)
            chunk(0, 0, True, start=True)
            chunk(1, 1, True)
            with pe.Fori(1, C // 2 - 1) as it:
                for par in range(2):
                    chunk(it * 2 + par, par, True)
            for par in range(2):
                chunk(C - 2 + par, par, par == 0)

        @block.vector
        def _(dve):
            def split_x(q, par):
                dve.wait_ge(x_ps, q + 1)
                split_f32r(nc, dve, x_hi[par][:, :], x_lo[par][:, :], psX[:, :]).then_inc(x_done, 1)

            def lows(m, e):
                for n in range(NB):
                    dve.wait_ge(g_done, m * NB + (n + 1 + NB))
                    if n == 0:
                        dve.wait_ge(y_ps, m + 1)
                    nc.vector.tensor_tensor(g_lo[e % 2][:, n, :], g[:, n, :], g_hi[e % 2][:, n, :].bitcast(F32), ALU.subtract).then_inc(lo_done, 1)

            def weigh(m, q, e):
                dve.wait_ge(t_ps, m + 3)
                for i in range(TPC):
                    tile = bass.ds(q * TPC + i, 1)
                    out = H[:, tile, :]
                    last = nc.vector.scalar_tensor_tensor(out, psT[:, i * P:(i + 1) * P].unsqueeze(1), gates[:, tile, e], out, ALU.mult, ALU.add)
                last.then_inc(t_read, 1)

            def chunk(q, par, more, start=False):
                for e in range(E):
                    m = q * E + e
                    if e + 1 < E or more:
                        lows(m + 1, (e + 1) % E)
                    if e:
                        weigh(m - 1, q, e - 1)
                    elif not start:
                        weigh(m - 1, q - 1, E - 1)
                    if more and e == TURN:
                        split_x(q + 1, 1 - par)
                if not more:
                    weigh(q * E + (E - 1), q, E - 1)

            dve.sem_inc(g_done, NB)
            dve.sem_inc(lo_done, NB)
            dve.sem_inc(y_done, 2)
            dve.sem_inc(t_read, 1)
            split_x(0, 0)
            for e in range(E):
                dve.wait_ge(w1_in, 16 * (e + 1))
                split_f32r(nc, dve, w1_hi[e][:, :], w1_lo[e][:, :], raw1[:, :])
                dve.wait_ge(w2_in, 16 * (e + 1))
                split_f32r(nc, dve, w2_hi[e][:, :, :], w2_lo[e][:, :, :], raw2[:, :, :]).then_inc(w_done, 1)
            lows(0, 0)
            chunk(0, 0, True, start=True)
            chunk(1, 1, True)
            with dve.Fori(1, C // 2 - 1) as it:
                for par in range(2):
                    chunk(it * 2 + par, par, True)
            for par in range(2):
                chunk(C - 2 + par, par, par == 0)


def tower(nc, ins, out):
    B, S, D, NH = 8, 1024, 128, 8
    nc.disable_value_cache = True
    with ExitStack() as ctx:
        c = Core(nc, ctx, "all")
        H = c.sb("H", [P, B * S // P, D])
        ident = c.sb("ident", [P, P])
        half = c.sb("half", [P, 8])
        mean1, rstd1, score1 = (c.sb(n, [P, B * S // P]) for n in ("mean1", "rstd1", "score1"))
        ld = c.sem("ld")
        with nc.Block() as block:
            @block.sync
            def _(sp):
                sp.dma_start(ident[:, :], ins["ident"]).then_inc(ld, 16)
                sp.wait_ge(ld, 16)

            @block.vector
            def _(dve):
                nc.vector.memset(half[:, :], -0.5)
        embed_and_attend(nc, H, ident, half, mean1, rstd1, score1, ins, B, S, D, NH)
        sequence_experts(nc, H, ident, mean1, rstd1, score1, ins, B, S, D)
        gates = c.sb("gates", [P, B * S // P, ins["Wr"].shape[1]])
        zd = nc.dram_tensor("zd", [B * S // P, P, D], F32).ap()
        block_attention(nc, H, zd, gates, ident, half, ins, B, S, D)
        token_experts(nc, H, zd, gates, ident, ins, B, S, D)
        done = c.sem("done")
        with nc.Block() as block:
            @block.sync
            def _(sp):
                sp.dma_start(out.rearrange("(t p) d -> p t d", p=P), H[:, :, :]).then_inc(done, 16)
                sp.wait_ge(done, 16)


def host(inputs):
    import math
    import numpy as np
    g = {k: np.asarray(v) for k, v in inputs.items()}
    b, h, w, f = g["x"].shape
    S, D = h * w, g["L0_tok_W"].shape[1]
    pos = np.arange(2 * S, dtype=np.float32)[:, None]
    div = np.exp(np.arange(0, D, 2, dtype=np.float32) * (-math.log(10000.0) / D))
    pe = np.zeros((2 * S, D), np.float32)
    pe[:, 0::2], pe[:, 1::2] = np.sin(pos * div), np.cos(pos * div)
    a = {"xT": g["x"].reshape(b * S, f).T, "Wtok": g["L0_tok_W"], "pe": pe[:S], "ident": np.eye(128, dtype=np.float32),
         "pieces": (np.arange(D)[:, None] // 16 == np.arange(32)).astype(np.float32)}
    for n in ("Wq", "Wk", "Wv", "Wo"):
        a[n] = g["L0_attn_" + n].T
    for n in ("bq", "bk", "bv", "bo", "gamma", "beta"):
        a[n] = g["L0_attn_" + n]
    E, B = 8, b
    a["attn_w"] = g["L0_ffn_attn_w"].reshape(D)
    a["attn_b"] = g["L0_ffn_attn_b"]
    a["gate_w"], a["gate_b"] = g["L0_ffn_gate_w"], g["L0_ffn_gate_b"]
    a["w1"], a["w2"] = g["L0_ffn_w1"], g["L0_ffn_w2"]

    def biases(b1, b2):
        return np.concatenate([b1.reshape(E, 4, 128).transpose(0, 2, 1), b2[:, :, None]], axis=2)
    a["b12"] = biases(g["L0_ffn_b1"], g["L0_ffn_b2"])
    w, b3 = g["L1_attn_W_qkv"].reshape(D, 8, 3, 16), g["L1_attn_b_qkv"].reshape(8, 3, 16)
    a["Wqk"] = w[:, :, 0:2].transpose(0, 2, 1, 3).reshape(D, 2, D)
    a["Wv1"] = w[:, :, 2].reshape(D, D)
    a["b_qkv"] = b3.transpose(0, 2, 1).reshape(D, 3)
    a["Wproj"], a["b_proj"] = g["L1_attn_W_proj"], g["L1_attn_b_proj"]
    a["Wr"], a["W1"], a["W2"] = g["L1_ffn_Wr"], g["L1_ffn_W1"], g["L1_ffn_W2"]
    a["B12"] = biases(g["L1_ffn_b1"], g["L1_ffn_b2"])
    T = S // 128
    a["own"] = np.tile((np.arange(B * T)[:, None] // T == np.arange(B)).astype(np.float32), (128, 1, 1))
    a["lower"] = np.tile(np.tril(np.ones((E, E), np.float32), -1), (128, 1, 1))
    r, e = np.meshgrid(np.arange(2), np.arange(E), indexing="ij")
    a["places"] = np.tile(np.stack([r, e]).astype(np.float32), (128, 1, 1, 1))
    return {k: np.ascontiguousarray(v) for k, v in a.items()}


def kernel(**inputs):
    import numpy as np
    import concourse.bacc as bacc
    from concourse.bass_utils import run_bass_kernel_spmd

    arrays = host(inputs)
    shape = inputs["x"].shape
    S, D = shape[1] * shape[2], inputs["L0_tok_W"].shape[1]
    nc = bacc.Bacc("TRN2", target_bir_lowering=False, num_devices=1)
    ins = {n: nc.dram_tensor(n, a.shape, mybir.dt.from_np(a.dtype), kind="ExternalInput").ap() for n, a in arrays.items()}
    out = nc.dram_tensor("out", [shape[0] * S, D], F32, kind="ExternalOutput").ap()
    tower(nc, ins, out)
    r = run_bass_kernel_spmd(nc, [arrays], core_ids=[0])
    return r.results[0]["out"].reshape(shape[0], S, D)
```

```python
from contextlib import ExitStack

import concourse.bass as bass
from concourse import mybir

F32 = mybir.dt.float32
F32R = mybir.dt.float32r
BF16 = mybir.dt.bfloat16
I32 = mybir.dt.int32
U32 = mybir.dt.uint32
ALU = mybir.AluOpType
ACT = mybir.ActivationFunctionType
AX = mybir.AxisListType.X

P = 128
EPS = 1e-5
CH = 512
TPC = CH // P
ROW = P + 2
LIMIT = 60.0


class Tally:

    def __init__(self, start):
        self.start, self.count = start, 0

    def next(self):
        self.count += 1
        return self.start + self.count

    def ends(self, count):
        assert self.count == count, (self.count, count)


class Core:

    def __init__(self, nc, ctx, tag):
        self.nc, self.ctx, self.tag = nc, ctx, tag

    def sb(self, name, shape, dt=F32):
        return self.ctx.enter_context(self.nc.sbuf_tensor(f"{self.tag}_{name}", shape, dt))

    def ps(self, name, shape):
        return self.ctx.enter_context(self.nc.psum_tensor(f"{self.tag}_{name}", shape, F32))

    def sem(self, name):
        return self.ctx.enter_context(self.nc.semaphore(f"{self.tag}_{name}"))


def split_f32r(nc, eng, hi, lo, src):
    nc.vector.tensor_copy(hi, src)
    eng.drain()
    return nc.vector.tensor_tensor(lo, src, hi.bitcast(F32), ALU.subtract)


def product(nc, out, w_hi, w_lo, x_hi, x_lo, first=True, last=True):
    nc.tensor.matmul(out, w_lo, x_hi, start=first, stop=False)
    nc.tensor.matmul(out, w_hi, x_lo, start=False, stop=False)
    return nc.tensor.matmul(out, w_hi, x_hi, start=False, stop=last)


def normalise(nc, dve, src, dst, stat, mv, veps, rs, var_done, rs_done, n):
    for i in range(TPC):
        nc.vector.bn_stats(stat[:, i, :], src(i))
    dve.drain()
    for i in range(TPC):
        nc.vector.bn_aggr(mv[:, i, :], stat[:, i, :])
    dve.drain()
    nc.vector.tensor_scalar(veps[:, :], mv[:, :, 1], EPS, None, ALU.add).then_inc(var_done, 1)
    dve.wait_ge(rs_done, n)
    for i in range(TPC):
        last = nc.vector.tensor_scalar(dst(i), src(i), mv[:, i, 0:1], rs[:, i:i + 1], ALU.subtract, ALU.mult)
    return last


def embed_and_attend(nc, H, ident, half, mean1, rstd1, score1, ins, B, S, D, NH):
    DH = D // NH
    T = S // P
    KT = NH
    F = ins["xT"].shape[0]
    CPB = S // CH
    SCALE = float(DH) ** -0.5
    NPR = 4
    NSC = 3
    PAIRS = [(0, 0), (0, 1), (1, 0), (1, 1), (0, 2), (2, 0)]
    KQ = DH * len(PAIRS)
    KG = KQ + 3
    assert T == NH == 8 and DH == 16 and CPB == 2 and KG <= P

    with ExitStack() as ctx:
        c = Core(nc, ctx, "a0")
        qs = [c.sb(f"qs{p}", [P, KT, S], BF16) for p in range(2)]
        ks = [c.sb(f"ks{p}", [P, KT, S], BF16) for p in range(2)]
        v = [c.sb(f"v{p}", [P, T, KT, 32]) for p in range(2)]
        n0 = [c.sb(f"n0{p}", [P, T, D]) for p in range(2)]
        xt = [c.sb(f"xt{p}", [F, S]) for p in range(2)]
        probs = [c.sb(f"probs{p}", [P, KT * P]) for p in range(NPR)]
        pe_tab = c.sb("pe_tab", [P, T, D])
        w_tok = c.sb("w_tok", [F, D])
        w_raw = c.sb("w_raw", [D, 4, D])
        wq_hi, wq_lo, wk_hi, wk_lo = (c.sb(n, [D, D], F32R) for n in ("wq_hi", "wq_lo", "wk_hi", "wk_lo"))
        bcol = c.sb("bcol", [D, 2])
        brow = c.sb("brow", [P, 5, D])
        nT = c.sb("nT", [D, CH])
        nT_hi, nT_lo = c.sb("nT_hi", [D, CH], F32R), c.sb("nT_lo", [D, CH], F32R)
        qf = [c.sb(f"qf{p}", [D, CH]) for p in range(2)]
        rem = c.sb("rem", [D, CH])
        sq = [c.sb(f"sq{p}", [D, CH], BF16) for p in range(2)]
        pieces_f = c.sb("pieces_f", [D, 32])
        pieces = c.sb("pieces", [D, 32], BF16)
        norms2 = c.sb("norms2", [64, CPB])
        worst, pair2, most2 = c.sb("worst", [64, 1]), c.sb("pair2", [32, 2]), c.sb("most2", [32, 2])
        bound2, unsafe = c.sb("bound2", [1, 1]), c.sb("unsafe", [1, 1], I32)
        parts = [c.sb(f"parts{p}", [D, 3, CH], BF16) for p in range(2)]
        stat, mv = c.sb("stat", [P, TPC, 6]), c.sb("mv", [P, TPC, 2])
        veps, rs = c.sb("veps", [P, TPC]), c.sb("rs", [P, TPC])
        negmax = c.sb("negmax", [P, 2 * KT, T])
        gf, gr = c.sb("gf", [KT * T, P]), c.sb("gr", [KT * T, P])
        gparts = c.sb("gparts", [KT * T, 3, P], BF16)
        o_sb = c.sb("o_sb", [P, 2 * P])
        rden = c.sb("rden", [P, KT])
        ctx_tm, ctxT = c.sb("ctx_tm", [P, KT, DH]), c.sb("ctxT", [D, P])
        res = c.sb("res", [P, TPC, D])
        dq = [nc.dram_tensor(f"qparts{p}", [D, 3, CH], BF16).ap() for p in range(2)]
        dk = [nc.dram_tensor(f"kparts{p}", [D, 3, CH], BF16).ap() for p in range(2)]

        psS = [c.ps(f"psS{p}", [P, 2, CH]) for p in range(NSC)]
        psO = c.ps("psO", [P, CH])
        psA = c.ps("psA", [P, CH])

        (w_in, wsplit, x_in0, x_in1, emb_ps, var_done, rs_done, n0_done, nt_ps,  q_ps, k_ps, v_ps,
         psA_free, qparts_done, kparts_done, qparts_out, kparts_out, stack_in, pre_qk, pre_max, gt_ps,
         gparts_done, guard_in, qk_done, exp_done, pv_done, o_evac, ht_ps,  ct_ps,
         op_done, sq_done, n_ps, norms_done, waited, qf_done, kf_done, unsafe_done) = (c.sem(n) for n in (
            "w_in wsplit x_in0 x_in1 emb_ps var_done rs_done n0_done nt_ps q_ps k_ps v_ps "
            "psA_free qparts_done kparts_done qparts_out kparts_out stack_in pre_qk pre_max gt_ps "
            "gparts_done guard_in qk_done exp_done pv_done o_evac ht_ps ct_ps "
            "op_done sq_done n_ps norms_done waited qf_done kf_done unsafe_done").split())

        x_in = (x_in0, x_in1)
        N_W = 14
        STACK = 16 * 2 * len(PAIRS) * CPB
        GUARD = 16 * 3
        PSA_EMBED = 6 * CPB
        PSA_BATCH = 1 + 3 * T + PSA_EMBED
        RS_EMBED, RS_BATCH = CPB, 3 * CPB

        STEPS = {(0, 2): ("E", 0), (0, 5): ("E", 1), (1, 2): ("T", 0), (1, 5): ("q", 0), (2, 2): ("k", 0),
                 (2, 5): ("v", 0), (3, 2): ("T", 1), (3, 5): ("N", 0), (4, 2): ("q", 1), (4, 5): ("k", 1),
                 (5, 2): ("v", 1), (5, 5): ("N", 1)}

        def rounds(eng, batch):
            with eng.Fori(0, B // 2 - 1) as it:
                for par in range(2):
                    batch(it * 2 + par, par, True)
            for par in range(2):
                batch(B - 2 + par, par, par == 0)

        block = ctx.enter_context(nc.Block())

        @block.sync
        def _(sp):
            for i, n in enumerate(("Wq", "Wk", "Wv", "Wo")):
                sp.dma_start(w_raw[:, i, :], ins[n]).then_inc(w_in, 16)
            sp.dma_start(w_tok[:, :], ins["Wtok"]).then_inc(w_in, 16)
            sp.dma_start(pe_tab[:, :, :], ins["pe"].rearrange("(t p) d -> p t d", p=P)).then_inc(w_in, 16)
            for i, n in enumerate(("bq", "bk")):
                sp.dma_start(bcol[:, i:i + 1], ins[n].rearrange("(d o) -> d o", o=1)).then_inc(w_in, 16)
            sp.dma_start(pieces_f[:, :], ins["pieces"]).then_inc(w_in, 16)
            for i, n in enumerate(("bv", "bo", "gamma", "beta", "attn_w")):
                sp.dma_start(brow[:, i, :], ins[n].rearrange("(o d) -> o d", o=1).broadcast_to([P, D])).then_inc(w_in, 16)
            sp.sem_inc(qparts_out, 16)
            sp.sem_inc(kparts_out, 16)

            def has_x(b):
                return not isinstance(b, int)

            def load_x(b, par):
                sp.dma_start(xt[par][:, :], ins["xT"][:, bass.ds(b * S, S)]).then_inc(x_in[par], 16)

            def redistribute(b, par):
                for ch in range(CPB):
                    for kind, done, out, dram in ((0, qparts_done, qparts_out, dq), (1, kparts_done, kparts_out, dk)):
                        sp.wait_ge(done, b * CPB + ch + 1)
                        sp.dma_start(dram[ch], parts[kind][:, :, :]).then_inc(out, 16)
                        sp.wait_ge(out, (b * CPB + ch) * 16 + 32)
                        src = dram[ch].rearrange("(j d) a t -> d j a t", d=DH)
                        for g, pair in enumerate(PAIRS):
                            sp.dma_start((qs, ks)[kind][par][g * DH:(g + 1) * DH, :, ch * CH:(ch + 1) * CH],
                                         src[:, :, pair[kind], :]).then_inc(stack_in, 16)

            def batch(b, par, more):
                sp.wait_ge(gparts_done, b + 1)
                for i in range(3):
                    sp.dma_start(qs[par][KQ + i:KQ + i + 1, :, :].rearrange("o j (h t) -> o (j h) t", t=P),
                                 gparts[:, i, :]).then_inc(guard_in, 16)
                if more:
                    if has_x(b):
                        sp.wait_ge(emb_ps, (b + 1) * CPB)
                        load_x(b + 2, par)
                    redistribute(b + 1, 1 - par)

            load_x(0, 0)
            load_x(1, 1)
            redistribute(0, 0)
            rounds(sp, batch)

        @block.gpsimd
        def _(pool):
            def root(turns):
                pool.wait_ge(var_done, turns.next())
                nc.gpsimd.tensor_tensor(rs[:, :], veps[:, :], half[:, 0:TPC], ALU.pow).then_inc(rs_done, 1)

            def embed_step(kind, ch, b, turns):
                if kind == "E":
                    root(turns)
                elif kind in ("q", "k"):
                    i = "qk".index(kind)
                    pool.wait_ge((qf_done, kf_done)[i], b * CPB + (ch + 1))
                    nc.gpsimd.tensor_tensor(sq[i][:, :], qf[i][:, :], qf[i][:, :], ALU.mult).then_inc(sq_done, 1)
                elif kind == "N" and ch == CPB - 1:
                    pool.wait_ge(norms_done, b + 1)
                    pool.sem_inc(waited, 1)
                    nc.gpsimd.partition_all_reduce(most2[:, :], pair2[:, :], 32, bass.bass_isa.ReduceOp.max)
                    pool.drain()
                    nc.gpsimd.tensor_tensor(bound2[:, :], most2[0:1, 0:1], most2[0:1, 1:2], ALU.mult)
                    pool.drain()
                    nc.gpsimd.tensor_scalar(unsafe[:, :], bound2[:, :], LIMIT * LIMIT, None, ALU.is_gt).then_inc(unsafe_done, 1)

            def batch(b, par, more):
                turns = Tally(RS_EMBED + b * RS_BATCH)
                for h in range(T):
                    for kt in range(KT):
                        if more and (h, kt) in STEPS:
                            embed_step(*STEPS[h, kt], b + 1, turns)
                    if h == TPC:
                        root(turns)
                        root(turns)
                root(turns)
                root(turns)
                turns.ends(RS_BATCH if more else RS_BATCH - RS_EMBED)

            turns = Tally(0)
            for kind, ch in STEPS.values():
                embed_step(kind, ch, 0, turns)
            rounds(pool, batch)

        @block.scalar
        def _(act):
            def batch(b, par, more):
                for h in range(T):
                    for kt in range(KT):
                        u = b * (T * KT) + (h * KT + kt)
                        act.wait_ge(qk_done, u + 1)
                        act.wait_ge(pv_done, u + 1)
                        nc.scalar.activation(probs[kt % NPR][:, :], psS[(h * KT + kt) % NSC][:, :, :].rearrange("p a n -> p (a n)"),
                                             ACT.Exp).then_inc(exp_done, 1)
            rounds(act, batch)

        @block.tensor
        def _(pe):
            def take(uses):
                pe.wait_ge(psA_free, uses.next())

            def embed_step(kind, ch, b, par, uses):
                n = b * CPB + (ch + 1)
                if kind == "E":
                    pe.wait_ge(x_in[par], (b + (2 - par)) * 8)
                    take(uses)
                    for i in range(TPC):
                        last = nc.tensor.matmul(psA[:, i * P:(i + 1) * P], xt[par][:, ch * CH + i * P:ch * CH + (i + 1) * P],
                                                w_tok[:, :], start=True, stop=True)
                    last.then_inc(emb_ps, 1)
                elif kind == "T":
                    pe.wait_ge(n0_done, n)
                    take(uses)
                    for i in range(TPC):
                        last = nc.tensor.transpose(psA[:, i * P:(i + 1) * P], n0[par][:, ch * TPC + i, :], ident[:, :])
                    last.then_inc(nt_ps, 1)
                elif kind in ("q", "k"):
                    take(uses)
                    hi, lo, done = (wq_hi, wq_lo, q_ps) if kind == "q" else (wk_hi, wk_lo, k_ps)
                    product(nc, psA[:, :], hi[:, :], lo[:, :], nT_hi[:, :], nT_lo[:, :]).then_inc(done, 1)
                elif kind == "N":
                    pe.wait_ge(sq_done, 2 * n)
                    take(uses)
                    for i in range(2):
                        last = nc.tensor.matmul(psA[32 * i:32 * i + 32, :], pieces[:, :], sq[i][:, :], start=True, stop=True)
                    last.then_inc(n_ps, 1)
                else:
                    take(uses)
                    for i in range(TPC):
                        last = nc.tensor.matmul(psA[:, i * P:(i + 1) * P], nT[:, i * P:(i + 1) * P], w_raw[:, 2, :],
                                                start=True, stop=True)
                    last.then_inc(v_ps, 1)

            def maximum(b, par, psA_free, uses):
                for j in range(KT):
                    for h in range(T):
                        u = j * T + h
                        if u >= 2:
                            pe.wait_ge(pre_max, b * (T * KT) + (u - 1))
                        for a in range(2):
                            last = nc.tensor.matmul(psS[u % 2][:, a, :], qs[par][0:KQ, j, h * P:(h + 1) * P],
                                                    ks[par][0:KQ, 4 * a:4 * a + 4, h * P:(h + 1) * P], start=True, stop=True)
                        last.then_inc(pre_qk, 1)
                pe.wait_ge(pre_max, (b + 1) * (T * KT))
                pe.wait_ge(psA_free, uses.start + 1)
                nc.tensor.transpose(psA[:, 0:P], negmax[:, :, :].rearrange("p j h -> p (j h)"), ident[:, :]).then_inc(gt_ps, 1)

            def batch(b, par, more):
                uses = Tally(PSA_EMBED + b * PSA_BATCH)
                pe.wait_ge(stack_in, (b + 1) * STACK)
                pe.wait_ge(unsafe_done, b + 1)
                pe.sem_inc(waited, 1)
                with pe.If(pe.value_load(unsafe[0:1, 0:1], min_val=0, max_val=1)):
                    maximum(b, par, psA_free, uses)
                uses.next()
                pe.wait_ge(guard_in, (b + 1) * GUARD)

                def scores(u):
                    h, kt = divmod(u, KT)
                    for a in range(2):
                        last = nc.tensor.matmul(psS[u % NSC][:, a, :], ks[par][0:KG, kt, h * P:(h + 1) * P],
                                                qs[par][0:KG, 4 * a:4 * a + 4, h * P:(h + 1) * P], start=True, stop=True)
                    last.then_inc(qk_done, 1)

                def weigh(h, kt):
                    if kt == 0:
                        pe.wait_ge(o_evac, b * T + (h + 1))
                    pe.wait_ge(exp_done, b * (T * KT) + (h * KT + kt + 1))
                    for g in range(4):
                        last = nc.tensor.matmul(psO[32 * g:32 * g + 32, 0:2 * P], v[par][:, h, kt, :],
                                                probs[kt % NPR][:, g * 2 * P:(g + 1) * 2 * P], start=(kt == 0), stop=(kt == KT - 1))
                    last.then_inc(pv_done, 1)

                def turn(h):
                    pe.wait_ge(o_evac, b * T + (h + 2))
                    take(uses)
                    for a in range(2):
                        last = nc.tensor.transpose(psA[:, a * P:(a + 1) * P], o_sb[:, a * P:(a + 1) * P], ident[:, :])
                    last.then_inc(ht_ps, 1)

                def turn_back(h):
                    take(uses)
                    nc.tensor.transpose(psA[:, 0:P], ctx_tm[:, :, :].rearrange("p j d -> p (j d)"), ident[:, :]).then_inc(ct_ps, 1)

                def project(h):
                    take(uses)
                    nc.tensor.matmul(psA[:, 0:P], ctxT[:, :], w_raw[:, 3, :], start=True, stop=True).then_inc(op_done, 1)

                for u in range(NSC - 1):
                    scores(u)
                for h in range(T):
                    for kt in range(KT):
                        if h * KT + kt + NSC - 1 < T * KT:
                            scores(h * KT + kt + NSC - 1)
                        weigh(h, kt)
                        if h and kt == 1:
                            turn(h - 1)
                        if h and kt == 4:
                            turn_back(h - 1)
                        if h and kt == 6:
                            project(h - 1)
                        if more and (h, kt) in STEPS:
                            embed_step(*STEPS[h, kt], b + 1, 1 - par, uses)
                turn(T - 1)
                turn_back(T - 1)
                project(T - 1)
                uses.ends(PSA_BATCH if more else PSA_BATCH - PSA_EMBED)

            pe.sem_inc(pv_done, NPR)
            pe.wait_ge(wsplit, 1)
            uses = Tally(0)
            for kind, ch in STEPS.values():
                embed_step(kind, ch, 0, 0, uses)
            uses.ends(PSA_EMBED)
            rounds(pe, batch)

        @block.vector
        def _(dve):
            dve.sem_inc(psA_free, 1)
            dve.sem_inc(o_evac, 1)
            for p in range(2):
                nc.vector.memset(v[p][:, :, :, :], 0.0)
                nc.vector.memset(ks[p][KQ:KG, :, :], 1.0)
            nc.vector.memset(negmax[:, :, :], 0.0)
            dve.drain()
            for p in range(2):
                nc.vector.memset(v[p][:, :, :, DH:DH + 1], 1.0)
            dve.wait_ge(w_in, N_W * 16)
            nc.vector.tensor_copy(pieces[:, :], pieces_f[:, :])
            split_f32r(nc, dve, wq_hi[:, :], wq_lo[:, :], w_raw[:, 0, :])
            split_f32r(nc, dve, wk_hi[:, :], wk_lo[:, :], w_raw[:, 1, :]).then_inc(wsplit, 1)

            def thirds(dst, src, scratch, begun=None):
                first = nc.vector.tensor_copy(dst[0], src)
                if begun is not None:
                    first.then_inc(begun, 1)
                dve.drain()
                nc.vector.tensor_tensor(scratch, src, dst[0], ALU.subtract)
                dve.drain()
                nc.vector.tensor_copy(dst[1], scratch)
                dve.drain()
                return nc.vector.tensor_tensor(dst[2], scratch, dst[1], ALU.subtract)

            def embed_read(kind, ch, b, par):
                n = b * CPB + (ch + 1)
                if kind == "E":
                    dve.wait_ge(emb_ps, n)
                    nc.vector.tensor_tensor(H[:, bass.ds(b * T + ch * TPC, TPC), :], psA[:, :].rearrange("p (i d) -> p i d", d=D),
                                            pe_tab[:, ch * TPC:(ch + 1) * TPC, :], ALU.add).then_inc(psA_free, 1)
                elif kind == "T":
                    dve.wait_ge(nt_ps, n)
                    nc.vector.tensor_copy(nT_hi[:, :], psA[:, :])
                    nc.vector.tensor_copy(nT[:, :], psA[:, :])
                    dve.drain()
                    nc.vector.tensor_tensor(nT_lo[:, :], psA[:, :], nT_hi[:, :].bitcast(F32), ALU.subtract).then_inc(psA_free, 1)
                elif kind in ("q", "k"):
                    i = "qk".index(kind)
                    dve.wait_ge((q_ps, k_ps)[i], n)
                    nc.vector.tensor_scalar(qf[i][:, :], psA[:, :], bcol[:, i:i + 1], (SCALE, 1.0)[i], ALU.add, ALU.mult).then_inc(psA_free, 1)
                elif kind == "N":
                    dve.wait_ge(n_ps, n)
                    nc.vector.tensor_reduce(norms2[:, ch:ch + 1], psA[0:64, :], AX, ALU.max).then_inc(psA_free, 1)
                else:
                    dve.wait_ge(v_ps, n)
                    nc.vector.tensor_tensor(v[par][:, ch * TPC:(ch + 1) * TPC, :, 0:DH], psA[:, :].rearrange("p (i j d) -> p i j d", j=KT, d=DH),
                                            brow[:, 0:1, :].rearrange("p o (j d) -> p o j d", d=DH).broadcast_to([P, TPC, KT, DH]),
                                            ALU.add).then_inc(psA_free, 1)

            def embed_rest(kind, ch, b, par, norms):
                n = b * CPB + (ch + 1)
                if kind == "E":
                    dve.drain()
                    normalise(nc, dve, lambda i: H[:, bass.ds(b * T + (ch * TPC + i), 1), :], lambda i: n0[par][:, ch * TPC + i:ch * TPC + i + 1, :],
                              stat, mv, veps, rs, var_done, rs_done, norms.next()).then_inc(n0_done, 1)
                elif kind in ("q", "k"):
                    i = "qk".index(kind)
                    dve.drain()
                    dve.wait_ge((qparts_out, kparts_out)[i], n * 16)
                    thirds([parts[i][:, a, :] for a in range(3)], qf[i][:, :], rem[:, :], (qf_done, kf_done)[i]).then_inc((qparts_done, kparts_done)[i], 1)
                elif kind == "N" and ch == CPB - 1:
                    dve.drain()
                    nc.vector.tensor_reduce(worst[:, :], norms2[:, :], AX, ALU.max)
                    dve.drain()
                    nc.vector.tensor_copy(pair2[:, 0:1], worst[0:32, :])
                    nc.vector.tensor_copy(pair2[:, 1:2], worst[32:64, :]).then_inc(norms_done, 1)

            def embed_step(kind, ch, b, par, norms):
                embed_read(kind, ch, b, par)
                embed_rest(kind, ch, b, par, norms)

            def finish(b, half_, norms):
                rows = [brow[:, i:i + 1, :].broadcast_to([P, TPC, D]) for i in range(5)]
                nc.vector.tensor_tensor(res[:, :, :], res[:, :, :], rows[1], ALU.add)
                dve.drain()
                normalise(nc, dve, lambda i: res[:, i, :], lambda i: res[:, i, :], stat, mv, veps, rs, var_done, rs_done, norms.next())
                dve.drain()
                nc.vector.tensor_tensor(res[:, :, :], res[:, :, :], rows[2], ALU.mult)
                dve.drain()
                nc.vector.tensor_tensor(res[:, :, :], res[:, :, :], rows[3], ALU.add)
                dve.drain()
                out = H[:, bass.ds(b * T + half_ * TPC, TPC), :]
                nc.vector.tensor_tensor(out, out, res[:, :, :], ALU.add)
                dve.drain()
                tiles = bass.ds(b * T + half_ * TPC, TPC)
                normalise(nc, dve, lambda i: H[:, bass.ds(b * T + (half_ * TPC + i), 1), :], lambda i: res[:, i:i + 1, :],
                          stat, mv, veps, rs, var_done, rs_done, norms.next())
                nc.vector.tensor_copy(mean1[:, tiles], mv[:, :, 0])
                nc.vector.tensor_copy(rstd1[:, tiles], rs[:, :])
                dve.drain()
                nc.vector.tensor_tensor(res[:, :, :], res[:, :, :], rows[4], ALU.mult)
                dve.drain()
                nc.vector.tensor_reduce(score1[:, tiles], res[:, :, :], AX, ALU.add)
                dve.drain()

            def maximum(b):
                for j in range(KT):
                    for h in range(T):
                        u = j * T + h
                        dve.wait_ge(pre_qk, b * (T * KT) + (u + 1))
                        nc.vector.tensor_reduce(negmax[:, j, h:h + 1], psS[u % 2][:, :, :].rearrange("p a n -> p (a n)"), AX, ALU.max,
                                                negate=True).then_inc(pre_max, 1)
                dve.wait_ge(gt_ps, b + 1)
                nc.vector.tensor_copy(gf[:, :], psA[0:T * KT, 0:P]).then_inc(psA_free, 1)
                dve.drain()
                thirds([gparts[:, a, :] for a in range(3)], gf[:, :], gr[:, :])

            def no_maximum():
                dve.sem_inc(pre_max, T * KT)
                dve.sem_inc(gt_ps, 1)
                dve.sem_inc(pre_qk, T * KT)
                nc.vector.memset(gparts[:, :, :], 0.0)
                dve.drain()
                dve.sem_inc(psA_free, 1)

            def batch(b, par, more):
                norms = Tally(RS_EMBED + b * RS_BATCH)
                dve.wait_ge(unsafe_done, b + 1)
                dve.sem_inc(waited, 1)
                with dve.If(dve.value_load(unsafe[0:1, 0:1], min_val=0, max_val=1)):
                    maximum(b)
                with dve.Else():
                    no_maximum()
                dve.drain()
                dve.sem_inc(gparts_done, 1)

                def out_of_psum(h):
                    dve.wait_ge(pv_done, b * (T * KT) + ((h + 1) * KT + NPR))
                    nc.vector.tensor_copy(o_sb[:, :], psO[:, 0:2 * P]).then_inc(o_evac, 1)

                def divide(h):
                    dve.wait_ge(ht_ps, b * T + (h + 1))
                    o = psA[:, 0:2 * P].rearrange("p (a g e) -> p a g e", a=2, e=32)
                    r = rden[:, :].rearrange("p (a g o) -> p a g o", a=2, o=1)
                    nc.vector.reciprocal(r, o[:, :, :, DH:DH + 1])
                    dve.drain()
                    nc.vector.tensor_tensor(ctx_tm[:, :, :].rearrange("p (g a) d -> p a g d", a=2), o[:, :, :, 0:DH],
                                            r.broadcast_to([P, 2, 4, DH]), ALU.mult).then_inc(psA_free, 1)

                def evacuate(h):
                    dve.wait_ge(ct_ps, b * T + (h + 1))
                    nc.vector.tensor_copy(ctxT[:, :], psA[:, 0:P]).then_inc(psA_free, 1)

                def add_input(h):
                    dve.wait_ge(op_done, b * T + (h + 1))
                    nc.vector.tensor_tensor(res[:, h % TPC, :], psA[:, 0:P], n0[par][:, h, :], ALU.add).then_inc(psA_free, 1)

                for h in range(T):
                    steps = [STEPS.get((h, kt)) if more else None for kt in (2, 5)]
                    if h:
                        out_of_psum(h - 1)
                        divide(h - 1)
                    for i, step in enumerate(steps):
                        if step:
                            embed_read(*step, b + 1, 1 - par)
                        if h:
                            (evacuate, add_input)[i](h - 1)
                        if step:
                            embed_rest(*step, b + 1, 1 - par, norms)
                    if h == TPC:
                        dve.drain()
                        finish(b, 0, norms)
                out_of_psum(T - 1)
                divide(T - 1)
                evacuate(T - 1)
                add_input(T - 1)
                dve.drain()
                finish(b, 1, norms)
                norms.ends(RS_BATCH if more else RS_BATCH - RS_EMBED)

            norms = Tally(0)
            for kind, ch in STEPS.values():
                embed_step(kind, ch, 0, 0, norms)
            norms.ends(RS_EMBED)
            rounds(dve, batch)


def rank(nc, dve, out, more, same, p, lower):
    shape = list(more.shape)
    mine, theirs = p.unsqueeze(3).broadcast_to(shape), p.unsqueeze(2).broadcast_to(shape)
    nc.vector.tensor_tensor(more, theirs, mine, ALU.is_gt)
    nc.vector.tensor_tensor(same, theirs, mine, ALU.is_equal)
    dve.drain()
    nc.vector.tensor_tensor(same, same, lower.unsqueeze(1).broadcast_to(shape), ALU.mult)
    dve.drain()
    nc.vector.tensor_tensor(more, more, same, ALU.add)
    dve.drain()
    return nc.vector.tensor_reduce(out, more, AX, ALU.add)


class Items:

    def __init__(self, R, rounds, per_x, per_w):
        self.R, self.rounds, self.per_x, self.per_w = R, rounds, per_x, per_w

    def at(self, it, k, ahead):
        k += ahead
        return (it + k // self.R if k < 0 or k >= self.R else it), k % self.R

    def x_of(self, it, k):
        return it * (self.R // self.per_x) + k // self.per_x

    def new_x(self, k):
        return k % self.per_x == 0

    def w_of(self, it, k):
        return it * (self.R // self.per_w) + k % (self.R // self.per_w)

    def new_w(self, k):
        return k < self.R // self.per_w

    def run(self, eng, body):
        def round_(it, first, last):
            for k in range(self.R):
                body(it, k, lambda ahead: (k + ahead >= 0 or not first) and (k + ahead < self.R or not last))

        round_(0, True, False)
        with eng.Fori(1, self.rounds - 1) as it:
            round_(it, False, False)
        round_(self.rounds - 1, False, True)


def expert_items(nc, c, block, items, ident, rows, raw1, raw2, rawb1, rawb2, out_func, rows_wait, rows_next, weigh,
                 raw1_in, raw2_in, w1_done, w2_done, x_ps, t_ps, NB, D):
    HID = NB * P
    R = items.R
    x_hi, x_lo = ([c.sb(f"{n}{i}", [D, CH], F32R) for i in range(2)] for n in ("x_hi", "x_lo"))
    w1_hi, w1_lo = ([c.sb(f"{n}{i}", [D, HID], F32R) for i in range(2)] for n in ("w1_hi", "w1_lo"))
    w2_hi, w2_lo = ([c.sb(f"{n}{i}", [P, NB, D], F32R) for i in range(2)] for n in ("w2_hi", "w2_lo"))
    b_hid, b_out = [c.sb(f"b_hid{i}", [P, NB]) for i in range(2)], [c.sb(f"b_out{i}", [P, 1]) for i in range(2)]
    g = c.sb("g", [P, NB, CH])
    g_hi, g_lo = ([c.sb(f"{n}{i}", [P, NB, CH], F32R) for i in range(2)] for n in ("g_hi", "g_lo"))
    y = [c.sb(f"y{i}", [D, CH]) for i in range(2)]
    psH = [c.ps(f"psH{i}", [P, CH]) for i in range(NB)]
    psY = [c.ps(f"psY{i}", [P, CH]) for i in range(2)]
    psX = c.ps("psX", [P, CH])
    psT = c.ps("psT", [P, CH])
    x_done, h_ps, g_done, lo_done, y_ps, y_done, t_read = (c.sem(n) for n in "x_done h_ps g_done lo_done y_ps y_done t_read".split())

    def xb(it, k):
        return k // items.per_x % 2

    @block.scalar
    def _(act):
        def hidden(it, k):
            m, i = it * R + k, k % 2
            act.wait_ge(w1_done, items.w_of(it, k) + 1)
            for n in range(NB):
                act.wait_ge(h_ps, m * NB + (n + 1))
                if n == 0:
                    act.wait_ge(y_ps, m + 1)
                nc.scalar.activation(g_hi[i][:, n, :], psH[n][:, :], ACT.Gelu, bias=b_hid[i][:, n:n + 1])
                act.wait_ge(lo_done, m * NB + (n + 1))
                nc.scalar.activation(g[:, n, :], psH[n][:, :], ACT.Gelu, bias=b_hid[i][:, n:n + 1]).then_inc(g_done, 1)

        def output(it, k):
            m, i = it * R + k, k % 2
            act.wait_ge(y_ps, m + 3)
            act.wait_ge(t_ps, m + 1)
            nc.scalar.activation(y[i][:, :], psY[i][:, :], out_func, bias=b_out[i][:, :]).then_inc(y_done, 1)

        def body(it, k, does):
            if does(1):
                hidden(*items.at(it, k, 1))
            output(it, k)

        hidden(0, 0)
        items.run(act, body)

    @block.tensor
    def _(pe):
        def turn_x(it, k):
            rows_wait(pe, it, k)
            j = items.x_of(it, k)
            if not (isinstance(j, int) and j == 0):
                pe.wait_ge(x_done, j)
            for i in range(TPC):
                last = nc.tensor.transpose(psX[:, i * P:(i + 1) * P], rows(it, k)[:, i, 0:D], ident[:, :])
            last.then_inc(x_ps, 1)

        def first(it, k, n):
            i, b = k % 2, xb(it, k)
            if n == 0:
                pe.wait_ge(w1_done, items.w_of(it, k) + 1)
                pe.wait_ge(x_done, items.x_of(it, k) + 1)
            pe.wait_ge(g_done, (it * R + k) * NB + (n + 1))
            product(nc, psH[n][:, :], w1_hi[i][:, n * P:(n + 1) * P], w1_lo[i][:, n * P:(n + 1) * P],
                    x_hi[b][:, :], x_lo[b][:, :]).then_inc(h_ps, 1)

        def second(it, k, n):
            m, i = it * R + k, k % 2
            if n == 0:
                pe.wait_ge(w2_done, items.w_of(it, k) + 1)
                pe.wait_ge(y_done, m + 1)
            pe.wait_ge(lo_done, m * NB + (n + 1 + NB))
            last = product(nc, psY[i][:, :], w2_hi[i][:, n, :], w2_lo[i][:, n, :], g_hi[i][:, n, :], g_lo[i][:, n, :],
                           first=(n == 0), last=(n == NB - 1))
            if n == NB - 1:
                last.then_inc(y_ps, 1)

        def turn_y(it, k):
            m = it * R + k
            pe.wait_ge(y_done, m + 3)
            pe.wait_ge(t_read, m + 1)
            for i in range(TPC):
                last = nc.tensor.transpose(psT[:, i * P:(i + 1) * P], y[k % 2][:, i * P:(i + 1) * P], ident[:, :])
            last.then_inc(t_ps, 1)

        def body(it, k, does):
            if does(2) and items.new_x((k + 2) % R):
                turn_x(*items.at(it, k, 2))
            for n in range(NB):
                if does(1):
                    first(*items.at(it, k, 1), n)
                second(it, k, n)
                if n == 1 and does(-1):
                    turn_y(*items.at(it, k, -1))

        pe.sem_inc(y_ps, 2)
        pe.sem_inc(t_ps, 2)
        turn_x(0, 0)
        if items.new_x(1):
            turn_x(0, 1)
        for n in range(NB):
            first(0, 0, n)
        items.run(pe, body)
        turn_y(items.rounds - 1, R - 1)

    @block.vector
    def _(dve):
        def split_x(it, k):
            j, b = items.x_of(it, k), xb(it, k)
            dve.wait_ge(x_ps, j + 1)
            split_f32r(nc, dve, x_hi[b][:, :], x_lo[b][:, :], psX[:, :]).then_inc(x_done, 1)

        def split_w1(it, k):
            j = items.w_of(it, k)
            dve.wait_ge(raw1_in[k % 2], (j - k % 2) * 16 + 32)
            nc.vector.tensor_copy(b_hid[k % 2][:, :], rawb1[k % 2][:, :])
            split_f32r(nc, dve, w1_hi[k % 2][:, :], w1_lo[k % 2][:, :], raw1[k % 2][:, :]).then_inc(w1_done, 1)

        def split_w2(it, k):
            j = items.w_of(it, k)
            dve.wait_ge(raw2_in[k % 2], (j - k % 2) * 16 + 32)
            dve.wait_ge(y_done, it * R + k + 1)
            nc.vector.tensor_copy(b_out[k % 2][:, :], rawb2[k % 2][:, :])
            split_f32r(nc, dve, w2_hi[k % 2][:, :, :], w2_lo[k % 2][:, :, :], raw2[k % 2][:, :, :]).then_inc(w2_done, 1)

        def low(it, k, n):
            m, i = it * R + k, k % 2
            dve.wait_ge(g_done, m * NB + (n + 1 + NB))
            nc.vector.tensor_tensor(g_lo[i][:, n, :], g[:, n, :], g_hi[i][:, n, :].bitcast(F32), ALU.subtract).then_inc(lo_done, 1)

        def body(it, k, does):
            rows_next(dve, it, k, does)
            others = [(does(2) and items.new_x((k + 2) % R), split_x, 2), (does(1) and items.new_w((k + 1) % R), split_w2, 1),
                      (does(2) and items.new_w((k + 2) % R), split_w1, 2), (does(-1), lambda it, k: weigh(dve, psT, it, k).then_inc(t_read, 1), -1)]
            for n in range(NB):
                if does(1):
                    low(*items.at(it, k, 1), n)
                due, step, ahead = others[n]
                if due:
                    step(*items.at(it, k, ahead))

        dve.sem_inc(g_done, NB)
        dve.sem_inc(lo_done, NB)
        dve.sem_inc(y_done, 2)
        dve.sem_inc(t_read, 1)
        rows_next(dve, 0, -3, lambda ahead: True)
        rows_next(dve, 0, -2, lambda ahead: True)
        split_x(0, 0)
        split_w1(0, 0)
        rows_next(dve, 0, -1, lambda ahead: True)
        if items.new_x(1):
            split_x(0, 1)
        split_w1(0, 1)
        split_w2(0, 0)
        for n in range(NB):
            low(0, 0, n)
        items.run(dve, body)
        weigh(dve, psT, items.rounds - 1, R - 1).then_inc(t_read, 1)


def sequence_gates(nc, H, mean1, rstd1, score1, gate, chosen, ins, B, S, D):
    E = ins["w1"].shape[0]
    T = S // P
    NT = B * T
    K = 2
    assert E == B == 8

    with ExitStack() as ctx:
        c = Core(nc, ctx, "g0")
        attn_b, ones = c.sb("attn_b", [P, 1]), c.sb("ones", [P, P])
        ident_b = c.sb("ident_b", [B, B])
        sc, e_sc = c.sb("sc", [P, B, T]), c.sb("e_sc", [P, B, T])
        mx, mx_all, zs, rz, corr = (c.sb(n, [P, B]) for n in ("mx", "mx_all", "zs", "rz", "corr"))
        spread = c.sb("spread", [P, NT, B])
        own = c.sb("own", [P, NT, B])
        pooled, pooledT = c.sb("pooled", [B, D]), c.sb("pooledT", [D, B])
        gate_w, gate_b = c.sb("gate_w", [D, E]), c.sb("gate_b", [B, E])
        lg, pr = c.sb("lg", [B, E]), c.sb("pr", [B, 1, E])
        nmx, sm, rsm = c.sb("nmx", [B, 1]), c.sb("sm", [B, 1]), c.sb("rsm", [B, 1])
        beats, ties, rk = c.sb("beats", [B, 1, E, E]), c.sb("ties", [B, 1, E, E]), c.sb("rk", [B, 1, E])
        lower = c.sb("lower", [P, E, E])
        places = c.sb("places", [P, 2, K, E])
        sel, val = c.sb("sel", [B, K, E]), c.sb("val", [B, K, E])
        g2, i2, i2i = c.sb("g2", [B, K]), c.sb("i2", [B, K]), c.sb("i2i", [B, K], I32)
        d_gate = nc.dram_tensor("d_gate", [B, K], F32).ap()
        d_chosen = nc.dram_tensor("d_chosen", [B, K], I32).ap()
        psX, psT = c.ps("psX", [P, CH]), c.ps("psT", [P, CH])
        tab_in, mx_done, pool_done, exp_done, gate_out, gate_in, pe_gate, dve_gate = (c.sem(n) for n in (
            "tab_in mx_done pool_done exp_done gate_out gate_in pe_gate dve_gate").split())

        block = ctx.enter_context(nc.Block())

        @block.sync
        def _(sp):
            for dst, n in ((own[:, :, :], "own"), (lower[:, :, :], "lower"), (places[:, :, :, :], "places")):
                sp.dma_start(dst, ins[n]).then_inc(tab_in, 16)
            sp.dma_start(attn_b[:, :], ins["attn_b"].rearrange("(o d) -> o d", o=1).broadcast_to([P, 1])).then_inc(tab_in, 16)
            sp.dma_start(gate_w[:, :], ins["gate_w"]).then_inc(tab_in, 16)
            sp.dma_start(gate_b[:, :], ins["gate_b"].rearrange("(o d) -> o d", o=1).broadcast_to([B, E])).then_inc(tab_in, 16)
            sp.dma_start(ident_b[:, :], ins["ident"][0:B, 0:B]).then_inc(tab_in, 16)
            sp.wait_ge(dve_gate, 7)
            sp.dma_start(d_gate, g2[:, :]).then_inc(gate_out, 16)
            sp.dma_start(d_chosen, i2i[:, :]).then_inc(gate_out, 16)
            sp.wait_ge(gate_out, 32)
            sp.dma_start(gate[:, :, :], d_gate.rearrange("(o b) k -> o b k", o=1).broadcast_to([P, B, K])).then_inc(gate_in, 16)
            sp.dma_start(chosen[:, :], d_chosen.rearrange("(o b) k -> o (b k)", o=1)).then_inc(gate_in, 16)
            sp.wait_ge(gate_in, 32)

        @block.gpsimd
        def _(pool):
            pool.wait_ge(mx_done, 1)
            nc.gpsimd.partition_all_reduce(mx_all[:, :], mx[:, :], P, bass.bass_isa.ReduceOp.max).then_inc(pool_done, 1)

        @block.scalar
        def _(act):
            act.wait_ge(dve_gate, 1)
            nc.scalar.activation(e_sc[:, :, :], sc[:, :, :], ACT.Exp).then_inc(exp_done, 1)
            act.wait_ge(dve_gate, 6)
            nc.scalar.activation(pr[:, 0, :], lg[:, :], ACT.Exp, bias=nmx[:, :]).then_inc(exp_done, 1)

        @block.tensor
        def _(pe):
            pe.wait_ge(dve_gate, 2)
            nc.tensor.matmul(psT[:, 0:B], ones[:, :], zs[:, :], start=True, stop=True).then_inc(pe_gate, 1)
            pe.wait_ge(dve_gate, 3)
            for n in range(NT):
                nc.tensor.matmul(psT[0:B, 0:D], spread[:, n, :], H[:, n, :], start=(n == 0), stop=False)
            nc.tensor.matmul(psT[0:B, 0:D], corr[:, :], ones[:, :], start=False, stop=True).then_inc(pe_gate, 1)
            pe.wait_ge(dve_gate, 4)
            nc.tensor.transpose(psX[:, 0:B], pooled[:, :], ident_b[:, :]).then_inc(pe_gate, 1)
            pe.wait_ge(dve_gate, 5)
            nc.tensor.matmul(psT[0:B, 0:E], pooledT[:, :], gate_w[:, :], start=True, stop=True).then_inc(pe_gate, 1)

        @block.vector
        def _(dve):
            nc.vector.memset(ones[:, :], 1.0)
            dve.wait_ge(tab_in, 16 * 7)
            nc.vector.tensor_scalar(sc[:, :, :], score1[:, :].rearrange("p (b t) -> p b t", b=B), attn_b[:, :], None, ALU.add)
            dve.drain()
            nc.vector.tensor_reduce(mx[:, :], sc[:, :, :], AX, ALU.max).then_inc(mx_done, 1)
            dve.wait_ge(pool_done, 1)
            nc.vector.tensor_tensor(sc[:, :, :], sc[:, :, :], mx_all[:, :].unsqueeze(2).broadcast_to([P, B, T]), ALU.subtract).then_inc(dve_gate, 1)
            dve.wait_ge(exp_done, 1)
            nc.vector.tensor_reduce(zs[:, :], e_sc[:, :, :], AX, ALU.add).then_inc(dve_gate, 1)
            dve.wait_ge(pe_gate, 1)
            nc.vector.reciprocal(rz[:, :], psT[:, 0:B])
            dve.drain()
            nc.vector.tensor_tensor(e_sc[:, :, :], e_sc[:, :, :], rz[:, :].unsqueeze(2).broadcast_to([P, B, T]), ALU.mult)
            dve.drain()
            nc.vector.tensor_tensor(e_sc[:, :, :], e_sc[:, :, :], rstd1[:, :].rearrange("p (b t) -> p b t", b=B), ALU.mult)
            dve.drain()
            nc.vector.tensor_tensor(sc[:, :, :], e_sc[:, :, :], mean1[:, :].rearrange("p (b t) -> p b t", b=B), ALU.mult)
            dve.drain()
            nc.vector.tensor_reduce(corr[:, :], sc[:, :, :], AX, ALU.add, negate=True)
            nc.vector.tensor_tensor(spread[:, :, :], own[:, :, :], e_sc[:, :, :].rearrange("p b t -> p (b t)").unsqueeze(2).broadcast_to([P, NT, B]),
                                    ALU.mult).then_inc(dve_gate, 1)
            dve.wait_ge(pe_gate, 2)
            nc.vector.tensor_copy(pooled[:, :], psT[0:B, 0:D]).then_inc(dve_gate, 1)
            dve.wait_ge(pe_gate, 3)
            nc.vector.tensor_copy(pooledT[:, :], psX[:, 0:B]).then_inc(dve_gate, 1)
            dve.wait_ge(pe_gate, 4)
            nc.vector.tensor_tensor(lg[:, :], psT[0:B, 0:E], gate_b[:, :], ALU.add)
            dve.drain()
            nc.vector.tensor_reduce(nmx[:, :], lg[:, :], AX, ALU.max, negate=True).then_inc(dve_gate, 1)
            dve.wait_ge(exp_done, 2)
            nc.vector.tensor_reduce(sm[:, :], pr[:, 0, :], AX, ALU.add)
            dve.drain()
            nc.vector.reciprocal(rsm[:, :], sm[:, :])
            dve.drain()
            nc.vector.tensor_scalar(pr[:, 0, :], pr[:, 0, :], rsm[:, :], None, ALU.mult)
            dve.drain()
            rank(nc, dve, rk[:, :, :], beats[:, :, :, :], ties[:, :, :, :], pr[:, :, :], lower[0:B, :, :])
            dve.drain()
            nc.vector.tensor_tensor(sel[:, :, :], rk[:, :, :].broadcast_to([B, K, E]), places[0:B, 0, :, :], ALU.is_equal)
            dve.drain()
            nc.vector.tensor_tensor(val[:, :, :], sel[:, :, :], pr[:, :, :].broadcast_to([B, K, E]), ALU.mult)
            dve.drain()
            nc.vector.tensor_reduce(g2[:, :], val[:, :, :], AX, ALU.add)
            dve.drain()
            nc.vector.tensor_tensor(val[:, :, :], sel[:, :, :], places[0:B, 1, :, :], ALU.mult)
            dve.drain()
            nc.vector.tensor_reduce(i2[:, :], val[:, :, :], AX, ALU.add)
            nc.vector.tensor_reduce(sm[:, :], g2[:, :], AX, ALU.add)
            dve.drain()
            nc.vector.tensor_copy(i2i[:, :], i2[:, :])
            nc.vector.tensor_scalar(sm[:, :], sm[:, :], 1e-9, None, ALU.add)
            dve.drain()
            nc.vector.reciprocal(rsm[:, :], sm[:, :])
            dve.drain()
            nc.vector.tensor_scalar(g2[:, :], g2[:, :], rsm[:, :], None, ALU.mult).then_inc(dve_gate, 1)


def sequence_experts(nc, H, ident, mean1, rstd1, gate, chosen, ins, B, S, D):
    E, _, HID = ins["w1"].shape
    NB = HID // P
    T = S // P
    CPB = S // CH
    K = 2
    assert NB == 4 and CPB == 2

    with ExitStack() as ctx:
        c = Core(nc, ctx, "f0")
        f = c.sb("f", [P, TPC, D])
        raw1 = [c.sb(f"raw1{r}", [D, HID]) for r in range(K)]
        raw2 = [c.sb(f"raw2{r}", [P, NB, D]) for r in range(K)]
        rawb1 = [c.sb(f"rawb1{r}", [P, NB]) for r in range(K)]
        rawb2 = [c.sb(f"rawb2{r}", [P, 1]) for r in range(K)]
        step, f_done, x_ps, t_ps, w1_done, w2_done = (c.sem(n) for n in "step f_done x_ps t_ps w1_done w2_done".split())
        raw1_in, raw2_in = ([c.sem(f"{n}{r}") for r in range(K)] for n in ("raw1_in", "raw2_in"))
        items = Items(K * CPB, B, K, CPB)

        block = ctx.enter_context(nc.Block())

        @block.sync
        def _(sp):
            def load(b, r, which):
                e = sp.value_load(chosen[0:1, bass.ds(b * K + r, 1)], min_val=0, max_val=E - 1)
                if which == 1:
                    sp.dma_start(raw1[r][:, :], ins["w1"][bass.ds(e, 1), :, :].rearrange("o d h -> d (o h)")).then_inc(raw1_in[r], 16)
                    sp.dma_start(rawb1[r][:, :], ins["b1"][bass.ds(e, 1), :, :].rearrange("o p n -> p (o n)")).then_inc(raw1_in[r], 16)
                else:
                    sp.dma_start(raw2[r][:, :, :], ins["w2"][bass.ds(e, 1), :, :].rearrange("o (n p) d -> p (o n) d", p=P)).then_inc(raw2_in[r], 16)
                    sp.dma_start(rawb2[r][:, :], ins["b2"][bass.ds(e, 1), :].rearrange("o p -> p o")).then_inc(raw2_in[r], 16)

            for r in range(K):
                load(0, r, 1)
                load(0, r, 2)
            with sp.Fori(0, B - 1) as b:
                for r in range(K):
                    for which, done in ((1, w1_done), (2, w2_done)):
                        sp.wait_ge(done, b * K + (r + 1))
                        sp.sem_inc(step, 1)
                        load(b + 1, r, which)

        def rows_wait(pe, it, k):
            pe.wait_ge(f_done, items.x_of(it, k) + 1)

        def rows_next(dve, it, k, does):
            if items.new_x((k + 3) % items.R) and does(3):
                b, k = items.at(it, k, 3)
                j, ch = items.x_of(b, k), k // K
                if not (isinstance(j, int) and j == 0):
                    dve.wait_ge(x_ps, j)
                for i in range(TPC):
                    n = b * T + (ch * TPC + i)
                    last = nc.vector.tensor_scalar(f[:, i:i + 1, :], H[:, bass.ds(n, 1), :], mean1[:, bass.ds(n, 1)], rstd1[:, bass.ds(n, 1)],
                                                   ALU.subtract, ALU.mult)
                last.then_inc(f_done, 1)

        def weigh(dve, psT, b, k):
            ch, r = divmod(k, K)
            dve.wait_ge(t_ps, b * items.R + (k + 3))
            out = H[:, bass.ds(b * T + ch * TPC, TPC), :]
            return nc.vector.scalar_tensor_tensor(out, psT[:, :].rearrange("p (i d) -> p i d", d=D), gate[:, bass.ds(b, 1), r], out,
                                                  ALU.mult, ALU.add)

        expert_items(nc, c, block, items, ident, lambda it, k: f, raw1, raw2, rawb1, rawb2, ACT.Gelu, rows_wait, rows_next, weigh,
                     raw1_in, raw2_in, w1_done, w2_done, x_ps, t_ps, NB, D)


def block_attention(nc, H, queue, counts, ident, half, ins, B, S, D):
    SB = 32
    SG = P // SB
    T = S // P
    G = SB // SG
    E = ins["Wr"].shape[1]
    CPB = S // CH
    K = 2
    SCALE = float(D // 8) ** -0.5
    assert S == SB * SB and G == T and CPB == 2

    with ExitStack() as ctx:
        c = Core(nc, ctx, "a1")
        f, xT = c.sb("f", [P, T, D]), c.sb("xT", [D, S])
        x_hi, x_lo = c.sb("x_hi", [D, S], F32R), c.sb("x_lo", [D, S], F32R)
        w_qk, w_v, w_proj, w_r = c.sb("w_qk", [D, 2, D]), c.sb("w_v", [D, D]), c.sb("w_proj", [D, D]), c.sb("w_r", [D, E])
        w_hi, w_lo = c.sb("w_hi", [D, 2, D], F32R), c.sb("w_lo", [D, 2, D], F32R)
        bcol = c.sb("bcol", [D, 3])
        brow, ones = c.sb("brow", [1, CH]), c.sb("ones", [1, P])
        lower = c.sb("lower", [P, E, E])
        before, all_ones = c.sb("before", [P, P]), c.sb("all_ones", [P, P])
        base = c.sb("base", [P, 1, E])
        place_of = c.sb("place_of", [P, K, B * T], I32)
        qk = [c.sb(n, [D, S]) for n in ("q", "k")]
        v = c.sb("v", [P, G, D])
        mx, sm = c.sb("mx", [P, G]), c.sb("sm", [P, G])
        sc, pr = c.sb("sc", [P, G, SB]), c.sb("pr", [P, G, SB])
        diag = c.sb("diag", [P, G, P])
        oT, zT = c.sb("oT", [D, S]), c.sb("zT", [D, S])
        row = [[c.sb(f"row{p}{k}", [P, T, ROW]) for k in range(K)] for p in range(2)]
        both, sel, pos, vals = (c.sb(n, [P, T, E]) for n in ("both", "sel", "pos", "vals"))
        slot, newc = c.sb("slot", [P, T]), c.sb("newc", [P, E])
        idx = [c.sb(f"idx{p}", [P, K, T], U32) for p in range(2)]
        stat, mv = c.sb("stat", [P, TPC, 6]), c.sb("mv", [P, TPC, 2])
        veps, rs = c.sb("veps", [P, TPC]), c.sb("rs", [P, TPC])
        lg, el = c.sb("lg", [P, T, E]), c.sb("el", [P, T, E])
        beats, ties = c.sb("beats", [P, T, E, E]), c.sb("ties", [P, T, E, E])
        rk, gm, gs = c.sb("rk", [P, T, E]), c.sb("gm", [P, T]), c.sb("gs", [P, T])

        psX = [c.ps(f"psX{i}", [P, CH]) for i in range(2)]
        psQ = [c.ps(f"psQ{i}", [P, CH]) for i in range(2)]
        psO = [c.ps(f"psO{i}", [P, CH]) for i in range(2)]
        psS, psP = c.ps("psS", [P, CH]), c.ps("psP", [P, CH])
        SC = G * SB

        (w_in, ready, var_done, rs_done, f_done, x_ps, x_done, qk_ps, qk_done, v_ps, v_done, s_ps, sub_done, exp_done,
         diag_done, o_ps, o_done, p_ps, h_done, zn_done, z_ps, z_done, l_ps, lsub_done, lexp_done, row_done, sel_done, pos_ps, slot_done, waited, sent) = (c.sem(n) for n in (
            "w_in ready var_done rs_done f_done x_ps x_done qk_ps qk_done v_ps v_done s_ps sub_done exp_done "
            "diag_done o_ps o_done p_ps h_done zn_done z_ps z_done l_ps lsub_done lexp_done row_done sel_done pos_ps slot_done waited sent").split())

        def rounds(eng, iteration):
            iteration(0, 0, False, True, True)
            iteration(1, 1, True, True, True)
            with eng.Fori(1, B // 2 - 1) as it:
                for i in range(2):
                    iteration(it * 2 + i, i, True, True, True)
            iteration(B - 2, 0, True, True, False)
            iteration(B - 1, 1, True, False, False)

        def roots_before(b):
            return 2 * CPB + b * 2 * CPB if not isinstance(b, int) or b < B - 1 else 2 * CPB + (B - 2) * 2 * CPB + CPB

        block = ctx.enter_context(nc.Block())

        @block.sync
        def _(sp):
            for dst, n in ((w_qk[:, :, :], "Wqk"), (w_v[:, :], "Wv1"), (w_proj[:, :], "Wproj"), (w_r[:, :], "Wr"),
                           (bcol[:, :], "b_qkv"), (lower[:, :, :], "lower"), (before[:, :], "before"), (base[:, :, :], "base"),
                           (place_of[:, :, :], "place_of")):
                sp.dma_start(dst, ins[n]).then_inc(w_in, 16)
            sp.dma_start(brow[:, :].rearrange("o (i d) -> o i d", d=D),
                         ins["b_proj"].rearrange("(o i d) -> o i d", o=1, i=1).broadcast_to([1, TPC, D])).then_inc(w_in, 16)

        @block.gpsimd
        def _(pool):
            def root(n):
                pool.wait_ge(var_done, n)
                nc.gpsimd.tensor_tensor(rs[:, :], veps[:, :], half[:, 0:TPC], ALU.pow).then_inc(rs_done, 1)

            def send(n, par, k):
                pool.wait_ge(slot_done, n + 1)
                pool.wait_ge(row_done, n + 1)
                pool.sem_inc(waited, 1)
                for t in range(T):
                    pool.indirect_dma_start(queue, bass.IndirectOffsetOnAxis(ap=idx[par][:, k, t:t + 1], axis=0),
                                            row[par][k][:, t, :], None).then_inc(sent, 16)

            def iteration(b, par, z, one, two):
                sends = not isinstance(b, int) or b >= 2
                n = roots_before(b)
                for i in range(2 * CPB if two else CPB):
                    if sends and two and i in (1, CPB):
                        send(b - 2, par, i // CPB)
                    elif sends and not two and i == 0:
                        send(b - 2, par, 0)
                        send(b - 2, par, 1)
                    root(n + (i + 1))

            for i in range(2 * CPB):
                root(i + 1)
            rounds(pool, iteration)
            for n in (B - 2, B - 1):
                for k in range(K):
                    send(n, n % 2, k)
            pool.wait_ge(sent, B * 16 * K * T)

        @block.scalar
        def _(act):
            def project_read(n):
                if not (isinstance(n, int) and n == 0):
                    act.wait_ge(s_ps, n)
                for m in range(4):
                    act.wait_ge(qk_ps, n * 4 + (m + 1))
                    ch, i = divmod(m, 2)
                    nc.scalar.activation(qk[i][:, ch * CH:(ch + 1) * CH], psQ[m % 2][:, :], ACT.Identity, bias=bcol[:, i:i + 1]).then_inc(qk_done, 1)
                act.wait_ge(o_ps, n * 2 + 1)
                for h in range(2):
                    act.wait_ge(v_ps, n * 2 + (h + 1))
                    nc.scalar.activation(v[:, h * TPC:(h + 1) * TPC, :], psX[h][:, :].rearrange("p (i d) -> p i d", d=D), ACT.Copy).then_inc(v_done, 1)

            def route_exp(n):
                act.wait_ge(lsub_done, n + 1)
                nc.scalar.activation(el[:, :, :], lg[:, :, :], ACT.Exp).then_inc(lexp_done, 1)

            def iteration(b, par, z, one, two):
                act.wait_ge(sub_done, b + 1)
                nc.scalar.activation(pr[:, :, :], sc[:, :, :], ACT.Exp, scale=SCALE).then_inc(exp_done, 1)
                tokens = oT[:, :].rearrange("d (i s) -> d s i", s=SB)
                act.wait_ge(p_ps, b * 2 + 1)
                for h in range(2):
                    act.wait_ge(o_ps, b * 2 + (h + 2))
                    nc.scalar.activation(tokens[:, h * SB // 2:(h + 1) * SB // 2, :], psO[h][:, :].rearrange("d (s i) -> d s i", i=SB), ACT.Identity, bias=bcol[:, 2:3]).then_inc(o_done, 1)
                if one:
                    project_read(b + 1)
                if z:
                    route_exp(b - 1)
                copy_rows(b, par)

            def copy_rows(n, par):
                act.wait_ge(zn_done, (n + 1) * CPB)
                nc.scalar.activation(row[par][1][:, :, 0:D], row[par][0][:, :, 0:D], ACT.Copy).then_inc(row_done, 1)

            act.sem_inc(o_done, 2)
            act.wait_ge(w_in, 16 * 10)
            project_read(0)
            rounds(act, iteration)
            route_exp(B - 1)

        @block.tensor
        def _(pe):
            def turn(n, free):
                for ch in range(CPB):
                    pe.wait_ge(f_done, n * CPB + (ch + 1))
                    if free is not None:
                        pe.wait_ge(free[0], free[1] + ch)
                    for i in range(TPC):
                        last = nc.tensor.transpose(psX[ch][:, i * P:(i + 1) * P], f[:, ch * TPC + i, :], ident[:, :])
                    last.then_inc(x_ps, 1)

            def turn_z(n, par):
                for ch in range(CPB):
                    pe.wait_ge(zn_done, n * CPB + (ch + 1))
                    for i in range(TPC):
                        last = nc.tensor.transpose(psX[ch][:, i * P:(i + 1) * P], row[par][0][:, ch * TPC + i, 0:D], ident[:, :])
                    last.then_inc(z_ps, 1)

            def project(n):
                first = isinstance(n, int) and n == 0
                for m in range(4):
                    ch, i = divmod(m, 2)
                    pe.wait_ge(x_done, n * CPB + (ch + 1))
                    if not first or m >= 2:
                        pe.wait_ge(qk_done, n * 4 + (m - 1))
                    cols = slice(ch * CH, (ch + 1) * CH)
                    product(nc, psQ[m % 2][:, :], w_hi[:, i, :], w_lo[:, i, :], x_hi[:, cols], x_lo[:, cols]).then_inc(qk_ps, 1)

            def place(src, s):
                return src[:, :].rearrange("d (i s) -> d s i", s=SB)[:, s, :]

            def values(n):
                for g in range(G):
                    last = nc.tensor.matmul(psX[g // TPC][:, g % TPC * D:(g % TPC + 1) * D], xT[:, g * P:(g + 1) * P], w_v[:, :], start=True, stop=True)
                    if g % TPC == TPC - 1:
                        last.then_inc(v_ps, 1)

            def scores(n):
                pe.wait_ge(qk_done, n * 4 + 4)
                if not (isinstance(n, int) and n == 0):
                    pe.wait_ge(sub_done, n)
                for g in range(G):
                    for a in range(SG):
                        last = nc.tensor.matmul(psS[a * SB:(a + 1) * SB, g * SB:(g + 1) * SB], place(qk[0], g * SG + a), place(qk[1], g * SG + a),
                                                start=True, stop=True)
                last.then_inc(s_ps, 1)

            def attend(b):
                pe.wait_ge(diag_done, b + 1)
                pe.wait_ge(v_done, b * 2 + 2)
                for h in range(2):
                    pe.wait_ge(o_done, b * 2 + (h + 1))
                    for i in range(TPC):
                        g = h * TPC + i
                        last = nc.tensor.matmul(psO[h][:, i * P:(i + 1) * P], v[:, g, :], diag[:, g, :], start=True, stop=True)
                    last.then_inc(o_ps, 1)

            def output(b):
                pe.wait_ge(o_done, b * 2 + 4)
                for h in range(2):
                    pe.wait_ge(h_done, b * 2 + (h + 1))
                    nc.tensor.matmul(psP[:, :], ones[:, :], brow[:, :], start=True, stop=False)
                    for i in range(TPC):
                        t = h * TPC + i
                        last = nc.tensor.matmul(psP[:, i * P:(i + 1) * P], oT[:, t * P:(t + 1) * P], w_proj[:, :], start=False, stop=(i == TPC - 1))
                    last.then_inc(p_ps, 1)

            def logits(n):
                pe.wait_ge(z_done, (n + 1) * CPB)
                for t in range(T):
                    last = nc.tensor.matmul(psS[:, SC + t * E:SC + (t + 1) * E], zT[:, t * P:(t + 1) * P], w_r[:, :], start=True, stop=True)
                last.then_inc(l_ps, 1)

            def positions(n):
                pe.wait_ge(sel_done, n + 1)
                out = SC + T * E
                nc.tensor.matmul(psS[:, out:out + T * E], before[:, :], both[:, :, :], start=True, stop=False)
                nc.tensor.matmul(psS[:, out:out + T * E], all_ones[:, :], counts[:, :].unsqueeze(1).broadcast_to([P, T, E]), start=False, stop=False)
                for d in range(1, T):
                    last = nc.tensor.matmul(psS[:, out + d * E:out + T * E], all_ones[:, :], both[:, 0:T - d, :], start=False, stop=(d == T - 1))
                last.then_inc(pos_ps, 1)

            def iteration(b, par, z, one, two):
                if z:
                    pe.wait_ge(v_done, b * 2 + 2)
                    turn_z(b - 1, 1 - par)
                attend(b)
                if one:
                    turn(b + 1, (z_done, b * CPB - (CPB - 1)) if z else (v_done, 1))
                    project(b + 1)
                output(b)
                if one:
                    values(b + 1)
                if z:
                    logits(b - 1)
                if one:
                    scores(b + 1)
                if z:
                    positions(b - 1)

            pe.sem_inc(o_ps, 1)
            pe.sem_inc(p_ps, 1)
            pe.wait_ge(ready, 1)
            turn(0, None)
            project(0)
            values(0)
            scores(0)
            rounds(pe, iteration)
            pe.wait_ge(z_done, (B - 1) * CPB)
            turn_z(B - 1, 1)
            logits(B - 1)
            positions(B - 1)

        @block.vector
        def _(dve):
            norms = Tally(0)

            def normal(n, dst, done, turns):
                for ch in range(CPB):
                    normalise(nc, dve, lambda i: H[:, bass.ds(n * T + (ch * TPC + i), 1), :], dst(ch),
                              stat, mv, veps, rs, var_done, rs_done, turns.next()).then_inc(done, 1)

            def normal_x(n, turns):
                normal(n, lambda ch: lambda i: f[:, ch * TPC + i:ch * TPC + i + 1, :], f_done, turns)

            def normal_z(n, par, turns):
                if not isinstance(n, int) or n >= 2:
                    dve.wait_ge(sent, (n - 1) * (16 * K * T))
                normal(n, lambda ch: lambda i: row[par][0][:, ch * TPC + i:ch * TPC + i + 1, 0:D], zn_done, turns)

            def split_x(n):
                if not (isinstance(n, int) and n == 0):
                    dve.wait_ge(v_ps, n * 2)
                for ch in range(CPB):
                    cols = slice(ch * CH, (ch + 1) * CH)
                    dve.wait_ge(x_ps, n * CPB + (ch + 1))
                    nc.vector.tensor_copy(x_hi[:, cols], psX[ch][:, :])
                    nc.vector.tensor_copy(xT[:, :].rearrange("d (s i) -> d i s", i=SB)[:, ch * SB // 2:(ch + 1) * SB // 2, :],
                                          psX[ch][:, :].rearrange("d (i s) -> d i s", s=SB))
                    dve.drain()
                    nc.vector.tensor_tensor(x_lo[:, cols], psX[ch][:, :], x_hi[:, cols].bitcast(F32), ALU.subtract).then_inc(x_done, 1)

            def copy_z(n):
                for ch in range(CPB):
                    dve.wait_ge(z_ps, n * CPB + (ch + 1))
                    nc.vector.tensor_copy(zT[:, ch * CH:(ch + 1) * CH], psX[ch][:, :]).then_inc(z_done, 1)

            def attention(b):
                s = psS[:, 0:SC].rearrange("p (g j) -> p g j", j=SB)
                dve.wait_ge(s_ps, b + 1)
                nc.vector.tensor_reduce(mx[:, :], s, AX, ALU.max)
                dve.drain()
                nc.vector.tensor_tensor(sc[:, :, :], s, mx[:, :].unsqueeze(2).broadcast_to([P, G, SB]), ALU.subtract).then_inc(sub_done, 1)
                dve.wait_ge(exp_done, b + 1)
                nc.vector.tensor_reduce(sm[:, :], pr[:, :, :], AX, ALU.add)
                dve.drain()
                nc.vector.reciprocal(sm[:, :], sm[:, :])
                dve.drain()
                nc.vector.tensor_tensor(pr[:, :, :], pr[:, :, :], sm[:, :].unsqueeze(2).broadcast_to([P, G, SB]), ALU.mult)
                dve.drain()
                dve.wait_ge(o_ps, b * 2 + 1)
                for a in range(SG):
                    rows = slice(a * SB, (a + 1) * SB)
                    last = nc.vector.transpose(diag[rows, :, rows], pr[rows, :, :])
                last.then_inc(diag_done, 1)

            def add(b):
                for h in range(2):
                    dve.wait_ge(p_ps, b * 2 + (h + 2))
                    out = H[:, bass.ds(b * T + h * TPC, TPC), :]
                    nc.vector.tensor_tensor(out, out, psP[:, :].rearrange("p (i d) -> p i d", d=D), ALU.add).then_inc(h_done, 1)

            def route(n, par, one):
                dve.wait_ge(l_ps, n + 1)
                if one:
                    dve.wait_ge(s_ps, n + 3)
                whole = [P, T, E]
                nc.vector.tensor_copy(lg[:, :, :], psS[:, SC:SC + T * E].rearrange("p (t e) -> p t e", e=E))
                dve.drain()
                rank(nc, dve, rk[:, :, :], beats[:, :, :, :], ties[:, :, :, :], lg[:, :, :], lower[:, :, :])
                nc.vector.tensor_reduce(gm[:, :], lg[:, :, :], AX, ALU.max)
                dve.drain()
                nc.vector.tensor_tensor(lg[:, :, :], lg[:, :, :], gm[:, :].unsqueeze(2).broadcast_to(whole), ALU.subtract).then_inc(lsub_done, 1)
                nc.vector.tensor_scalar(both[:, :, :], rk[:, :, :], 2.0, None, ALU.is_lt).then_inc(sel_done, 1)
                dve.drain()
                nc.vector.tensor_reduce(newc[:, :], both[:, :, :].rearrange("p t e -> p e t"), AX, ALU.add)
                dve.wait_ge(lexp_done, n + 1)
                nc.vector.tensor_tensor(el[:, :, :], el[:, :, :], both[:, :, :], ALU.mult)
                dve.drain()
                nc.vector.tensor_reduce(gs[:, :], el[:, :, :], AX, ALU.add)
                dve.drain()
                nc.vector.reciprocal(gs[:, :], gs[:, :])
                dve.drain()
                nc.vector.tensor_tensor(el[:, :, :], el[:, :, :], gs[:, :].unsqueeze(2).broadcast_to(whole), ALU.mult)
                dve.wait_ge(pos_ps, n + 1)
                nc.vector.tensor_tensor(pos[:, :, :], psS[:, SC + T * E:SC + 2 * T * E].rearrange("p (t e) -> p t e", e=E),
                                        base[:, :, :].broadcast_to(whole), ALU.add)
                nc.vector.tensor_tensor(counts[:, :], counts[:, :], newc[:, :], ALU.add)
                for k in range(K):
                    dve.drain()
                    nc.vector.tensor_scalar(sel[:, :, :], rk[:, :, :], float(k), None, ALU.is_equal)
                    dve.drain()
                    nc.vector.tensor_tensor(vals[:, :, :], sel[:, :, :], pos[:, :, :], ALU.mult)
                    dve.drain()
                    nc.vector.tensor_reduce(slot[:, :], vals[:, :, :], AX, ALU.add)
                    dve.drain()
                    nc.vector.tensor_copy(idx[par][:, k, :], slot[:, :])
                    nc.vector.tensor_tensor(vals[:, :, :], sel[:, :, :], el[:, :, :], ALU.mult)
                    dve.drain()
                    nc.vector.tensor_reduce(row[par][k][:, :, D + 1:D + 2], vals[:, :, :], AX, ALU.add)
                    nc.vector.tensor_copy(row[par][k][:, :, D:D + 1].bitcast(I32), place_of[:, k, bass.ds(n * T, T)].unsqueeze(2))
                dve.drain()
                dve.sem_inc(slot_done, 1)

            def iteration(b, par, z, one, two):
                turns = Tally(roots_before(b))
                attention(b)
                if z:
                    copy_z(b - 1)
                if one:
                    split_x(b + 1)
                if two:
                    normal_x(b + 2, turns)
                add(b)
                if z:
                    route(b - 1, 1 - par, one)
                dve.drain()
                normal_z(b, par, turns)
                turns.ends(2 * CPB if two else CPB)

            dve.sem_inc(h_done, 1)
            nc.vector.memset(diag[:, :, :], 0.0)
            nc.vector.memset(ones[:, :], 1.0)
            nc.vector.memset(all_ones[:, :], 1.0)
            nc.vector.memset(counts[:, :], 0.0)
            dve.wait_ge(w_in, 16 * 10)
            split_f32r(nc, dve, w_hi[:, :, :], w_lo[:, :, :], w_qk[:, :, :]).then_inc(ready, 1)
            turns = Tally(0)
            normal_x(0, turns)
            split_x(0)
            normal_x(1, turns)
            rounds(dve, iteration)
            copy_z(B - 1)
            route(B - 1, 1, False)


def plan_tiles(nc, queue, counts, tile_e, tile_row, ins, E, B, S, D):
    STRIDE = B * S + CH
    N = tile_e.shape[1]
    M = B * S // CH
    with ExitStack() as ctx:
        c = Core(nc, ctx, "g1")
        ones = c.sb("ones", [P, P])
        n_f, n_i = c.sb("n_f", [1, 1, E]), c.sb("n_i", [1, E], I32)
        mark, upto = c.sb("mark", [1, E, M]), c.sb("upto", [1, E, E])
        tiles, ends = c.sb("tiles", [1, 1, E]), c.sb("ends", [1, 1, E])
        over, part = c.sb("over", [1, N, E]), c.sb("part", [1, N, E])
        e_f, done_f, row_f = (c.sb(n, [1, N]) for n in ("e_f", "done_f", "row_f"))
        steps, number = c.sb("steps", [1, 1, M]), c.sb("number", [1, N])
        pad = c.sb("pad", [P, TPC, ROW])
        pad_place = c.sb("pad_place", [P, TPC, 1], I32)
        ps = c.ps("ps", [P, CH])
        tab_in, ready, n_ps, counted, done, padded = (c.sem(n) for n in "tab_in ready n_ps counted done padded".split())
        with nc.Block() as block:
            @block.sync
            def _(sp):
                for dst, n in ((upto[:, :, :], "upto"), (steps[:, :, :], "steps"), (number[:, :], "number"), (pad_place[:, :, :], "pad_place")):
                    sp.dma_start(dst, ins[n]).then_inc(tab_in, 16)
                sp.wait_ge(done, 1)
                for e in range(E + 1):
                    first = e * STRIDE if e == E else e * STRIDE + sp.value_load(n_i[0:1, e:e + 1], min_val=0, max_val=B * S)
                    sp.dma_start(queue[bass.ds(first, CH), :].rearrange("(p i) c -> p i c", p=P), pad[:, :, :]).then_inc(padded, 16)
                sp.wait_ge(padded, 16 * (E + 1))

            @block.tensor
            def _(pe):
                pe.wait_ge(ready, 1)
                nc.tensor.matmul(ps[:, 0:E], ones[:, :], counts[:, :], start=True, stop=True).then_inc(n_ps, 1)

            @block.vector
            def _(dve):
                nc.vector.memset(ones[:, :], 1.0).then_inc(ready, 1)
                nc.vector.memset(pad[:, :, :], 0.0)
                dve.drain()
                dve.wait_ge(tab_in, 16 * 4)
                nc.vector.tensor_copy(pad[:, :, D:D + 1].bitcast(I32), pad_place[:, :, :])
                dve.wait_ge(n_ps, 1)
                nc.vector.tensor_copy(n_f[:, 0, :], ps[0:1, 0:E])
                dve.drain()
                nc.vector.tensor_copy(n_i[:, :], n_f[:, 0, :])
                nc.vector.tensor_tensor(mark[:, :, :], n_f[:, 0, :].unsqueeze(2).broadcast_to([1, E, M]), steps[:, :, :].broadcast_to([1, E, M]), ALU.is_gt)
                dve.drain()
                nc.vector.tensor_reduce(tiles[:, 0, :], mark[:, :, :], AX, ALU.add)
                dve.drain()
                nc.vector.tensor_tensor(upto[:, :, :], upto[:, :, :], tiles[:, :, :].broadcast_to([1, E, E]), ALU.mult)
                dve.drain()
                nc.vector.tensor_reduce(ends[:, 0, :], upto[:, :, :], AX, ALU.add)
                dve.drain()
                nc.vector.tensor_tensor(over[:, :, :], ends[:, :, :].broadcast_to([1, N, E]), number[:, :].unsqueeze(2).broadcast_to([1, N, E]), ALU.is_le)
                dve.drain()
                nc.vector.tensor_reduce(e_f[:, :], over[:, :, :], AX, ALU.add)
                nc.vector.tensor_tensor(part[:, :, :], over[:, :, :], tiles[:, :, :].broadcast_to([1, N, E]), ALU.mult)
                dve.drain()
                nc.vector.tensor_reduce(done_f[:, :], part[:, :, :], AX, ALU.add)
                dve.drain()
                nc.vector.tensor_tensor(row_f[:, :], number[:, :], done_f[:, :], ALU.subtract)
                dve.drain()
                nc.vector.tensor_scalar(row_f[:, :], row_f[:, :], float(CH), None, ALU.mult)
                nc.vector.tensor_scalar(done_f[:, :], e_f[:, :], float(STRIDE), None, ALU.mult)
                dve.drain()
                nc.vector.tensor_tensor(row_f[:, :], row_f[:, :], done_f[:, :], ALU.add)
                dve.drain()
                nc.vector.tensor_scalar(row_f[:, :], row_f[:, :], float(E * STRIDE), None, ALU.min)
                nc.vector.tensor_scalar(e_f[:, :], e_f[:, :], float(E - 1), None, ALU.min)
                dve.drain()
                nc.vector.tensor_copy(tile_row[:, :], row_f[:, :])
                nc.vector.tensor_copy(tile_e[:, :], e_f[:, :])
                dve.drain()
                dve.sem_inc(done, 1)


def token_experts(nc, queue, result, tile_e, tile_row, ident, ins, B, S, D):
    E, _, HID = ins["W1"].shape
    NB = HID // P
    N = tile_e.shape[1]
    assert NB == 4 and N % 4 == 0

    with ExitStack() as ctx:
        c = Core(nc, ctx, "f1")
        raw1 = [c.sb(f"raw1{r}", [D, HID]) for r in range(2)]
        raw2 = [c.sb(f"raw2{r}", [P, NB, D]) for r in range(2)]
        rawb1 = [c.sb(f"rawb1{r}", [P, NB]) for r in range(2)]
        rawb2 = [c.sb(f"rawb2{r}", [P, 1]) for r in range(2)]
        rows = [c.sb(f"rows{i}", [P, TPC, ROW]) for i in range(2)]
        meta = [c.sb(f"meta{i}", [P, TPC, 2]) for i in range(4)]
        idx = [c.sb(f"idx{i}", [P, TPC], U32) for i in range(2)]
        out = [c.sb(f"out{i}", [P, TPC, D]) for i in range(2)]
        step, x_ps, t_ps, w1_done, w2_done, meta_done, out_ready, waited = (c.sem(n) for n in "step x_ps t_ps w1_done w2_done meta_done out_ready waited".split())
        raw1_in, raw2_in, rows_in, sent = ([c.sem(f"{n}{i}") for i in range(2)] for n in ("raw1_in", "raw2_in", "rows_in", "sent"))
        items = Items(4, N // 4, 1, 1)

        block = ctx.enter_context(nc.Block())

        @block.sync
        def _(sp):
            def load(m, i, which):
                if which == 0:
                    first = sp.value_load(tile_row[0:1, bass.ds(m, 1)], min_val=0, max_val=E * (B * S + CH))
                    sp.dma_start(rows[i][:, :, :], queue[bass.ds(first, CH), :].rearrange("(p i) c -> p i c", p=P)).then_inc(rows_in[i], 16)
                    return
                e = sp.value_load(tile_e[0:1, bass.ds(m, 1)], min_val=0, max_val=E - 1)
                if which == 1:
                    sp.dma_start(raw1[i][:, :], ins["W1"][bass.ds(e, 1), :, :].rearrange("o d h -> d (o h)")).then_inc(raw1_in[i], 16)
                    sp.dma_start(rawb1[i][:, :], ins["B1"][bass.ds(e, 1), :, :].rearrange("o p n -> p (o n)")).then_inc(raw1_in[i], 16)
                else:
                    sp.dma_start(raw2[i][:, :, :], ins["W2"][bass.ds(e, 1), :, :].rearrange("o (n p) d -> p (o n) d", p=P)).then_inc(raw2_in[i], 16)
                    sp.dma_start(rawb2[i][:, :], ins["B2"][bass.ds(e, 1), :].rearrange("o p -> p o")).then_inc(raw2_in[i], 16)

            for i in range(2):
                for which in range(3):
                    load(i, i, which)
            with sp.Fori(0, N // 2 - 1) as it:
                for i in range(2):
                    m = it * 2 + i
                    sp.wait_ge(meta_done, m + 1)
                    sp.wait_ge(x_ps, m + 1)
                    sp.sem_inc(step, 1)
                    load(m + 2, i, 0)
                    for which, done in ((1, w1_done), (2, w2_done)):
                        sp.wait_ge(done, m + 1)
                        sp.sem_inc(step, 1)
                        load(m + 2, i, which)

        @block.gpsimd
        def _(pool):
            with pool.Fori(0, N // 2) as it:
                for i in range(2):
                    pool.wait_ge(out_ready, it * 2 + (i + 1))
                    pool.sem_inc(waited, 1)
                    for j in range(TPC):
                        pool.indirect_dma_start(result, bass.IndirectOffsetOnAxis(ap=idx[i][:, j:j + 1], axis=0), out[i][:, j, :], None,
                                                bounds_check=2 * B * S - 1, oob_is_err=False).then_inc(sent[i], 16)
            for i in range(2):
                pool.wait_ge(sent[i], N // 2 * 16 * TPC)

        def rows_wait(pe, it, k):
            pe.wait_ge(rows_in[k % 2], (it * 4 + (k - k % 2)) * 8 + 16)

        def rows_next(dve, it, k, does):
            if k + 2 < 0 or not does(2):
                return
            it, k = items.at(it, k, 2)
            rows_wait(dve, it, k)
            nc.vector.tensor_copy(meta[k][:, :, :], rows[k % 2][:, :, D:D + 2]).then_inc(meta_done, 1)

        def weigh(dve, psT, it, k):
            m = it * 4 + k
            if not isinstance(it, int) or it * 4 + k >= 2:
                dve.wait_ge(sent[k % 2], (it * 4 + (k - k % 2)) * 32)
            nc.vector.tensor_copy(idx[k % 2][:, :].bitcast(I32).unsqueeze(2), meta[k][:, :, 0:1].bitcast(I32))
            dve.wait_ge(t_ps, m + 3)
            last = nc.vector.tensor_tensor(out[k % 2][:, :, :], psT[:, :].rearrange("p (i d) -> p i d", d=D),
                                           meta[k][:, :, 1:2].broadcast_to([P, TPC, D]), ALU.mult)
            dve.drain()
            dve.sem_inc(out_ready, 1)
            return last

        expert_items(nc, c, block, items, ident, lambda it, k: rows[k % 2], raw1, raw2, rawb1, rawb2, ACT.Identity, rows_wait, rows_next,
                     weigh, raw1_in, raw2_in, w1_done, w2_done, x_ps, t_ps, NB, D)


def add_results(nc, H, result, out, B, S, D):
    T = S // P
    with ExitStack() as ctx:
        c = Core(nc, ctx, "out")
        y = [[c.sb(f"y{p}{k}", [P, T, D]) for k in range(2)] for p in range(2)]
        y_in = [c.sem(f"y_in{p}") for p in range(2)]
        summed, stored = c.sem("summed"), c.sem("stored")
        with nc.Block() as block:
            @block.sync
            def _(sp):
                def load(b, p):
                    for k in range(2):
                        rows = result[k * B * S + b * S:k * B * S + (b + 1) * S, :]
                        sp.dma_start(y[p][k][:, :, :], rows.rearrange("(t p) d -> p t d", p=P)).then_inc(y_in[p], 16)

                for b in range(2):
                    load(b, b)
                for b in range(B):
                    sp.wait_ge(summed, b + 1)
                    sp.dma_start(out[b * S:(b + 1) * S, :].rearrange("(t p) d -> p t d", p=P), H[:, b * T:(b + 1) * T, :]).then_inc(stored, 16)
                    if b + 2 < B:
                        load(b + 2, b % 2)
                sp.wait_ge(stored, B * 16)

            @block.vector
            def _(dve):
                for b in range(B):
                    dve.wait_ge(y_in[b % 2], (b // 2 + 1) * 32)
                    h = H[:, b * T:(b + 1) * T, :]
                    nc.vector.tensor_tensor(y[b % 2][0][:, :, :], y[b % 2][0][:, :, :], y[b % 2][1][:, :, :], ALU.add)
                    dve.drain()
                    nc.vector.tensor_tensor(h, h, y[b % 2][0][:, :, :], ALU.add).then_inc(summed, 1)


def tower(nc, ins, out):
    B, S, D, NH = 8, 1024, 128, 8
    nc.disable_value_cache = True
    with ExitStack() as ctx:
        c = Core(nc, ctx, "all")
        H = c.sb("H", [P, B * S // P, D])
        ident = c.sb("ident", [P, P])
        half = c.sb("half", [P, 8])
        mean1, rstd1, score1 = (c.sb(n, [P, B * S // P]) for n in ("mean1", "rstd1", "score1"))
        ld = c.sem("ld")
        with nc.Block() as block:
            @block.sync
            def _(sp):
                sp.dma_start(ident[:, :], ins["ident"]).then_inc(ld, 16)
                sp.wait_ge(ld, 16)

            @block.vector
            def _(dve):
                nc.vector.memset(half[:, :], -0.5)
        embed_and_attend(nc, H, ident, half, mean1, rstd1, score1, ins, B, S, D, NH)
        gate, chosen = c.sb("gate", [P, B, 2]), c.sb("chosen", [1, B * 2], I32)
        sequence_gates(nc, H, mean1, rstd1, score1, gate, chosen, ins, B, S, D)
        sequence_experts(nc, H, ident, mean1, rstd1, gate, chosen, ins, B, S, D)
        E = ins["Wr"].shape[1]
        K = 2
        counts = c.sb("counts", [P, E])
        tiles = -(-(K * B * S // CH + E - 1) // 4) * 4
        tile_e, tile_row = c.sb("tile_e", [1, tiles], I32), c.sb("tile_row", [1, tiles], I32)
        queue = nc.dram_tensor("queue", [E * (B * S + CH) + CH, ROW], F32).ap()
        result = nc.dram_tensor("result", [K * B * S, D], F32).ap()
        block_attention(nc, H, queue, counts, ident, half, ins, B, S, D)
        plan_tiles(nc, queue, counts, tile_e, tile_row, ins, E, B, S, D)
        token_experts(nc, queue, result, tile_e, tile_row, ident, ins, B, S, D)
        add_results(nc, H, result, out, B, S, D)


def host(inputs):
    import math
    import numpy as np
    g = {k: np.asarray(v) for k, v in inputs.items()}
    b, h, w, f = g["x"].shape
    S, D = h * w, g["L0_tok_W"].shape[1]
    pos = np.arange(2 * S, dtype=np.float32)[:, None]
    div = np.exp(np.arange(0, D, 2, dtype=np.float32) * (-math.log(10000.0) / D))
    pe = np.zeros((2 * S, D), np.float32)
    pe[:, 0::2], pe[:, 1::2] = np.sin(pos * div), np.cos(pos * div)
    a = {"xT": g["x"].reshape(b * S, f).T, "Wtok": g["L0_tok_W"], "pe": pe[:S], "ident": np.eye(128, dtype=np.float32),
         "pieces": (np.arange(D)[:, None] // 16 == np.arange(32)).astype(np.float32)}
    for n in ("Wq", "Wk", "Wv", "Wo"):
        a[n] = g["L0_attn_" + n].T
    for n in ("bq", "bk", "bv", "bo", "gamma", "beta"):
        a[n] = g["L0_attn_" + n]
    E, B = 8, b
    a["attn_w"] = g["L0_ffn_attn_w"].reshape(D)
    a["attn_b"] = g["L0_ffn_attn_b"]
    a["gate_w"], a["gate_b"] = g["L0_ffn_gate_w"], g["L0_ffn_gate_b"]
    a["w1"], a["w2"] = g["L0_ffn_w1"], g["L0_ffn_w2"]
    a["b1"], a["b2"] = g["L0_ffn_b1"].reshape(E, 4, 128).transpose(0, 2, 1), g["L0_ffn_b2"]
    w, b3 = g["L1_attn_W_qkv"].reshape(D, 8, 3, 16), g["L1_attn_b_qkv"].reshape(8, 3, 16)
    a["Wqk"] = w[:, :, 0:2].transpose(0, 2, 1, 3).reshape(D, 2, D)
    a["Wv1"] = w[:, :, 2].reshape(D, D)
    a["b_qkv"] = b3.transpose(0, 2, 1).reshape(D, 3)
    a["Wproj"], a["b_proj"] = g["L1_attn_W_proj"], g["L1_attn_b_proj"]
    a["Wr"], a["W1"], a["W2"] = g["L1_ffn_Wr"], g["L1_ffn_W1"], g["L1_ffn_W2"]
    a["B1"], a["B2"] = g["L1_ffn_b1"].reshape(E, 4, 128).transpose(0, 2, 1), g["L1_ffn_b2"]
    CH, K = 512, 2
    M, N = b * S // CH, -(-(K * b * S // CH + 7) // 4) * 4
    a["before"] = np.triu(np.ones((128, 128), np.float32), 1)
    a["base"] = np.tile((np.arange(8) * (b * S + CH)).astype(np.float32), (128, 1, 1))
    a["place_of"] = (np.arange(128)[:, None, None] + np.arange(K)[:, None] * b * S + np.arange(b * S // 128) * 128).astype(np.int32)
    a["upto"] = np.tril(np.ones((8, 8), np.float32))[None]
    a["steps"] = (np.arange(M) * CH).astype(np.float32)[None, None]
    a["number"] = np.arange(N).astype(np.float32)[None]
    a["pad_place"] = np.tile((K * b * S + np.arange(128)).astype(np.int32)[:, None, None], (1, 4, 1))
    T = S // 128
    a["own"] = np.tile((np.arange(B * T)[:, None] // T == np.arange(B)).astype(np.float32), (128, 1, 1))
    a["lower"] = np.tile(np.tril(np.ones((E, E), np.float32), -1), (128, 1, 1))
    r, e = np.meshgrid(np.arange(2), np.arange(E), indexing="ij")
    a["places"] = np.tile(np.stack([r, e]).astype(np.float32), (128, 1, 1, 1))
    return {k: np.ascontiguousarray(v) for k, v in a.items()}


def kernel(**inputs):
    import numpy as np
    import concourse.bacc as bacc
    from concourse.bass_utils import run_bass_kernel_spmd

    arrays = host(inputs)
    shape = inputs["x"].shape
    S, D = shape[1] * shape[2], inputs["L0_tok_W"].shape[1]
    nc = bacc.Bacc("TRN2", target_bir_lowering=False, num_devices=1)
    ins = {n: nc.dram_tensor(n, a.shape, mybir.dt.from_np(a.dtype), kind="ExternalInput").ap() for n, a in arrays.items()}
    out = nc.dram_tensor("out", [shape[0] * S, D], F32, kind="ExternalOutput").ap()
    tower(nc, ins, out)
    r = run_bass_kernel_spmd(nc, [arrays], core_ids=[0])
    return r.results[0]["out"].reshape(shape[0], S, D)
```

```python
from contextlib import ExitStack

import concourse.bass as bass
from concourse import mybir

F32 = mybir.dt.float32
F32R = mybir.dt.float32r
BF16 = mybir.dt.bfloat16
I32 = mybir.dt.int32
U32 = mybir.dt.uint32
ALU = mybir.AluOpType
ACT = mybir.ActivationFunctionType
AX = mybir.AxisListType.X

P = 128
EPS = 1e-5
CH = 512
TPC = CH // P
ROW = P + 2
LIMIT = 60.0


class Tally:

    def __init__(self, start, parity=0):
        self.start, self.count, self.parity = start, 0, parity

    def next(self):
        self.count += 1
        return self.start + self.count

    def buffer(self):
        return (self.parity + self.count + 1) % 2

    def ends(self, count):
        assert self.count == count, (self.count, count)


class Core:

    def __init__(self, nc, ctx, tag):
        self.nc, self.ctx, self.tag = nc, ctx, tag

    def sb(self, name, shape, dt=F32):
        return self.ctx.enter_context(self.nc.sbuf_tensor(f"{self.tag}_{name}", shape, dt))

    def ps(self, name, shape):
        return self.ctx.enter_context(self.nc.psum_tensor(f"{self.tag}_{name}", shape, F32))

    def sem(self, name):
        return self.ctx.enter_context(self.nc.semaphore(f"{self.tag}_{name}"))


def split_f32r(nc, eng, hi, lo, src):
    nc.vector.tensor_copy(hi, src)
    eng.drain()
    return nc.vector.tensor_tensor(lo, src, hi.bitcast(F32), ALU.subtract)


def product(nc, out, w_hi, w_lo, x_hi, x_lo, first=True, last=True):
    nc.tensor.matmul(out, w_lo, x_hi, start=first, stop=False)
    nc.tensor.matmul(out, w_hi, x_lo, start=False, stop=False)
    return nc.tensor.matmul(out, w_hi, x_hi, start=False, stop=last)


def normalise(nc, dve, src, dst, stat, mv, veps, rs, var_done, rs_done, n, tiles=TPC):
    for i in range(tiles):
        nc.vector.bn_stats(stat[:, i, :], src(i))
    dve.drain()
    for i in range(tiles):
        nc.vector.bn_aggr(mv[:, i, :], stat[:, i, :])
    dve.drain()
    nc.vector.tensor_scalar(veps[:, :], mv[:, :, 1], EPS, None, ALU.add).then_inc(var_done, 1)
    dve.wait_ge(rs_done, n)
    for i in range(tiles):
        last = nc.vector.tensor_scalar(dst(i), src(i), mv[:, i, 0:1], rs[:, i:i + 1], ALU.subtract, ALU.mult)
    return last


def embed_and_attend(nc, H, ident, half, mean1, rstd1, score1, ins, B, S, D, NH):
    DH = D // NH
    T = S // P
    KT = NH
    F = ins["xT"].shape[0]
    CPB = S // CH
    SCALE = float(DH) ** -0.5
    NPR = 4
    NSC = 2
    PAIRS = [(0, 0), (0, 1), (1, 0), (1, 1), (0, 2), (2, 0)]
    KQ = DH * len(PAIRS)
    KG = KQ + 3
    assert T == NH == 8 and DH == 16 and CPB == 2 and KG <= P

    with ExitStack() as ctx:
        c = Core(nc, ctx, "a0")
        qs = [c.sb(f"qs{p}", [P, KT, S], BF16) for p in range(2)]
        ks = [c.sb(f"ks{p}", [P, KT, S], BF16) for p in range(2)]
        v = [c.sb(f"v{p}", [P, T, KT, 32]) for p in range(2)]
        n0 = [c.sb(f"n0{p}", [P, T, D]) for p in range(2)]
        xt = [c.sb(f"xt{p}", [F, S]) for p in range(2)]
        probs = [c.sb(f"probs{p}", [P, KT * P]) for p in range(NPR)]
        pe_tab = c.sb("pe_tab", [P, T, D])
        w_tok = c.sb("w_tok", [F, D])
        w_raw = c.sb("w_raw", [D, 4, D])
        wq_hi, wq_lo, wk_hi, wk_lo = (c.sb(n, [D, D], F32R) for n in ("wq_hi", "wq_lo", "wk_hi", "wk_lo"))
        bcol = c.sb("bcol", [D, 2])
        brow = c.sb("brow", [P, 5, D])
        nT = c.sb("nT", [D, CH])
        nT_hi, nT_lo = c.sb("nT_hi", [D, CH], F32R), c.sb("nT_lo", [D, CH], F32R)
        qf = [c.sb(f"qf{p}", [D, CH]) for p in range(2)]
        rem = c.sb("rem", [D, CH])
        sq = [c.sb(f"sq{p}", [D, CH], BF16) for p in range(2)]
        pieces_f = c.sb("pieces_f", [D, 32])
        pieces = c.sb("pieces", [D, 32], BF16)
        norms2 = c.sb("norms2", [64, CPB])
        worst, pair2, most2 = c.sb("worst", [64, 1]), c.sb("pair2", [32, 2]), c.sb("most2", [32, 2])
        bound2, unsafe = c.sb("bound2", [1, 1]), c.sb("unsafe", [1, 1], I32)
        parts = [c.sb(f"parts{p}", [D, 3, CH], BF16) for p in range(2)]
        stat, mv = c.sb("stat", [P, TPC, 6]), c.sb("mv", [P, TPC, 2])
        veps, rs = c.sb("veps", [P, TPC]), c.sb("rs", [P, TPC])
        negmax = c.sb("negmax", [P, 2 * KT, T])
        gf, gr = c.sb("gf", [KT * T, P]), c.sb("gr", [KT * T, P])
        gparts = c.sb("gparts", [KT * T, 3, P], BF16)
        o_sb = c.sb("o_sb", [P, 2 * P])
        rden = c.sb("rden", [P, KT])
        ctx_tm, ctxT = c.sb("ctx_tm", [P, KT, DH]), c.sb("ctxT", [D, P])
        res = [c.sb(f"res{p}", [P, TPC, D]) for p in range(2)]
        dq = [nc.dram_tensor(f"qparts{p}", [D, 3, CH], BF16).ap() for p in range(2)]
        dk = [nc.dram_tensor(f"kparts{p}", [D, 3, CH], BF16).ap() for p in range(2)]

        psS = [c.ps(f"psS{p}", [P, 2, CH]) for p in range(NSC)]
        psO = [c.ps(f"psO{p}", [P, CH]) for p in range(2)]
        psA = [c.ps(f"psA{p}", [P, CH]) for p in range(2)]

        (w_in, wsplit, x_in0, x_in1, emb_ps, var_done, rs_done, n0_done, nt_ps,  q_ps, k_ps, v_ps,
         psA_free, cleared, normal_done, stream_done, qparts_done, kparts_done, qparts_out, kparts_out, stack_in, pre_qk, pre_max, gt_ps,
         gparts_done, guard_in, qk_done, exp_done, pv_done, o_evac, ht_ps,  ct_ps,
         op_done, sq_done, n_ps, norms_done, waited, qf_done, kf_done, unsafe_done) = (c.sem(n) for n in (
            "w_in wsplit x_in0 x_in1 emb_ps var_done rs_done n0_done nt_ps q_ps k_ps v_ps "
            "psA_free cleared normal_done stream_done qparts_done kparts_done qparts_out kparts_out stack_in pre_qk pre_max gt_ps "
            "gparts_done guard_in qk_done exp_done pv_done o_evac ht_ps ct_ps "
            "op_done sq_done n_ps norms_done waited qf_done kf_done unsafe_done").split())

        x_in = (x_in0, x_in1)
        N_W = 14
        STACK = 16 * 2 * len(PAIRS) * CPB
        GUARD = 16 * 3
        PSA_EMBED = 6 * CPB
        PSA_HEAD = 3
        PSA_BATCH = PSA_HEAD * T + PSA_EMBED
        RS_EMBED, RS_BATCH = CPB, 3 * CPB

        STEPS = {(1, 1): ("E", 0), (1, 4): ("E", 1), (2, 1): ("T", 0), (2, 4): ("q", 0), (3, 1): ("k", 0),
                 (3, 4): ("v", 0), (4, 1): ("T", 1), (4, 4): ("N", 0), (5, 1): ("q", 1), (5, 4): ("k", 1),
                 (6, 1): ("v", 1), (6, 4): ("N", 1)}

        def rounds(eng, batch):
            for par in range(2):
                batch(par, par, par == 1, True)
            with eng.Fori(1, B // 2 - 1) as it:
                for par in range(2):
                    batch(it * 2 + par, par, True, True)
            for par in range(2):
                batch(B - 2 + par, par, True, par == 0)

        def tally(b, embed, each, carried):
            assert embed % 2 == each % 2 == 0
            return Tally(embed, 0) if isinstance(b, int) and b == 0 else Tally(embed + b * each - carried, carried % 2)

        UPPER = {(0, 1): 0, (3, 1): 2, (4, 0): 3}
        LOWER = {(4, 1): 0, (7, 0): 2, (7, 1): 3}
        ROOTS = (0, 2)
        STREAM = 0

        block = ctx.enter_context(nc.Block())

        @block.sync
        def _(sp):
            for i, n in enumerate(("Wq", "Wk", "Wv", "Wo")):
                sp.dma_start(w_raw[:, i, :], ins[n]).then_inc(w_in, 16)
            sp.dma_start(w_tok[:, :], ins["Wtok"]).then_inc(w_in, 16)
            sp.dma_start(pe_tab[:, :, :], ins["pe"].rearrange("(t p) d -> p t d", p=P)).then_inc(w_in, 16)
            for i, n in enumerate(("bq", "bk")):
                sp.dma_start(bcol[:, i:i + 1], ins[n].rearrange("(d o) -> d o", o=1)).then_inc(w_in, 16)
            sp.dma_start(pieces_f[:, :], ins["pieces"]).then_inc(w_in, 16)
            for i, n in enumerate(("bv", "bo", "gamma", "beta", "attn_w")):
                sp.dma_start(brow[:, i, :], ins[n].rearrange("(o d) -> o d", o=1).broadcast_to([P, D])).then_inc(w_in, 16)
            sp.sem_inc(qparts_out, 16)
            sp.sem_inc(kparts_out, 16)

            def has_x(b):
                return not isinstance(b, int) or b + 2 < B

            def load_x(b, par):
                sp.dma_start(xt[par][:, :], ins["xT"][:, bass.ds(b * S, S)]).then_inc(x_in[par], 16)

            def redistribute(b, par):
                for ch in range(CPB):
                    for kind, done, out, dram in ((0, qparts_done, qparts_out, dq), (1, kparts_done, kparts_out, dk)):
                        sp.wait_ge(done, b * CPB + ch + 1)
                        sp.dma_start(dram[ch], parts[kind][:, :, :]).then_inc(out, 16)
                        sp.wait_ge(out, (b * CPB + ch) * 16 + 32)
                        src = dram[ch].rearrange("(j d) a t -> d j a t", d=DH)
                        for g, pair in enumerate(PAIRS):
                            sp.dma_start((qs, ks)[kind][par][g * DH:(g + 1) * DH, :, ch * CH:(ch + 1) * CH],
                                         src[:, :, pair[kind], :]).then_inc(stack_in, 16)

            def batch(b, par, prior, more):
                if more:
                    if has_x(b):
                        sp.wait_ge(emb_ps, (b + 1) * CPB)
                        load_x(b + 2, par)
                    redistribute(b + 1, 1 - par)
                    send_guard(b + 1, 1 - par)

            def send_guard(b, par):
                sp.wait_ge(gparts_done, b + 1)
                for i in range(3):
                    sp.dma_start(qs[par][KQ + i:KQ + i + 1, :, :].rearrange("o j (h t) -> o (j h) t", t=P),
                                 gparts[:, i, :]).then_inc(guard_in, 16)

            load_x(0, 0)
            load_x(1, 1)
            redistribute(0, 0)
            send_guard(0, 0)
            rounds(sp, batch)

        @block.gpsimd
        def _(pool):
            def root(turns):
                pool.wait_ge(var_done, turns.next())
                nc.gpsimd.tensor_tensor(rs[:, :], veps[:, :], half[:, 0:TPC], ALU.pow).then_inc(rs_done, 1)

            def embed_step(kind, ch, b, turns):
                if kind == "E":
                    root(turns)
                elif kind in ("q", "k"):
                    i = "qk".index(kind)
                    pool.wait_ge((qf_done, kf_done)[i], b * CPB + (ch + 1))
                    nc.gpsimd.tensor_tensor(sq[i][:, :], qf[i][:, :], qf[i][:, :], ALU.mult).then_inc(sq_done, 1)
                elif kind == "N" and ch == CPB - 1:
                    pool.wait_ge(norms_done, b + 1)
                    pool.sem_inc(waited, 1)
                    nc.gpsimd.partition_all_reduce(most2[:, :], pair2[:, :], 32, bass.bass_isa.ReduceOp.max)
                    pool.drain()
                    nc.gpsimd.tensor_tensor(bound2[:, :], most2[0:1, 0:1], most2[0:1, 1:2], ALU.mult)
                    pool.drain()
                    nc.gpsimd.tensor_scalar(unsafe[:, :], bound2[:, :], LIMIT * LIMIT, None, ALU.is_gt).then_inc(unsafe_done, 1)

            def stream(b, half_):
                rows = [brow[:, i:i + 1, :].broadcast_to([P, TPC, D]) for i in (2, 3)]
                r = res[half_][:, :, :]
                tiles = bass.ds(b * T + half_ * TPC, TPC)
                pool.wait_ge(normal_done, b * 2 + (half_ + 1))
                nc.gpsimd.tensor_tensor(r, r, rows[0], ALU.mult)
                pool.drain()
                nc.gpsimd.tensor_tensor(r, r, rows[1], ALU.add)
                pool.drain()
                nc.gpsimd.tensor_tensor(H[:, tiles, :], H[:, tiles, :], r, ALU.add).then_inc(stream_done, 1)

            def batch(b, par, prior, more):
                turns = tally(b, RS_EMBED, RS_BATCH, 2)
                for h in range(T):
                    for i, kt in enumerate((1, 4)):
                        if more and (h, kt) in STEPS:
                            embed_step(*STEPS[h, kt], b + 1, turns)
                        if prior and UPPER.get((h, i)) in ROOTS or LOWER.get((h, i)) in ROOTS:
                            root(turns)
                        if prior and UPPER.get((h, i)) == STREAM:
                            stream(b - 1, 1)
                        if LOWER.get((h, i)) == STREAM:
                            stream(b, 0)
                turns.ends(2 * (1 + prior) + RS_EMBED * more)

            nc.gpsimd.memset(v[0][:, :, :, :], 0.0)
            pool.drain()
            nc.gpsimd.memset(v[0][:, :, :, DH:DH + 1], 1.0)
            pool.drain()
            pool.sem_inc(cleared, 1)
            turns = Tally(0)
            for kind, ch in STEPS.values():
                embed_step(kind, ch, 0, turns)
            pool.drain()
            nc.gpsimd.memset(ks[0][KQ:KG, :, :], 1.0)
            pool.drain()
            nc.gpsimd.memset(negmax[:, :, :], 0.0)
            pool.drain()
            pool.sem_inc(cleared, 1)
            nc.gpsimd.memset(v[1][:, :, :, :], 0.0)
            pool.drain()
            nc.gpsimd.memset(v[1][:, :, :, DH:DH + 1], 1.0)
            pool.drain()
            nc.gpsimd.memset(ks[1][KQ:KG, :, :], 1.0)
            pool.drain()
            pool.sem_inc(cleared, 1)
            rounds(pool, batch)
            turns = Tally(RS_EMBED + B * RS_BATCH - RS_EMBED - 2)
            root(turns)
            stream(B - 1, 1)
            root(turns)

        @block.scalar
        def _(act):
            def batch(b, par, prior, more):
                for h in range(T):
                    for kt in range(KT):
                        u = b * (T * KT) + (h * KT + kt)
                        act.wait_ge(qk_done, u + 1)
                        act.wait_ge(pv_done, u + 1)
                        nc.scalar.activation(probs[kt % NPR][:, :], psS[(h * KT + kt) % NSC][:, :, :].rearrange("p a n -> p (a n)"),
                                             ACT.Exp).then_inc(exp_done, 1)
            rounds(act, batch)

        @block.tensor
        def _(pe):
            def take(uses, all_read=False):
                n = uses.next()
                pe.wait_ge(psA_free, n + 1 if all_read else n)
                return psA[uses.buffer()]

            def embed_step(kind, ch, b, par, uses):
                n = b * CPB + (ch + 1)
                if kind == "E":
                    pe.wait_ge(x_in[par], (b + (2 - par)) * 8)
                    ps = take(uses)
                    for i in range(TPC):
                        last = nc.tensor.matmul(ps[:, i * P:(i + 1) * P], xt[par][:, ch * CH + i * P:ch * CH + (i + 1) * P],
                                                w_tok[:, :], start=True, stop=True)
                    last.then_inc(emb_ps, 1)
                elif kind == "T":
                    pe.wait_ge(n0_done, n)
                    ps = take(uses)
                    for i in range(TPC):
                        last = nc.tensor.transpose(ps[:, i * P:(i + 1) * P], n0[par][:, ch * TPC + i, :], ident[:, :])
                    last.then_inc(nt_ps, 1)
                elif kind in ("q", "k"):
                    ps = take(uses, all_read=(kind == "q"))
                    hi, lo, done = (wq_hi, wq_lo, q_ps) if kind == "q" else (wk_hi, wk_lo, k_ps)
                    product(nc, ps[:, :], hi[:, :], lo[:, :], nT_hi[:, :], nT_lo[:, :]).then_inc(done, 1)
                elif kind == "N":
                    pe.wait_ge(sq_done, 2 * n)
                    ps = take(uses)
                    for i in range(2):
                        last = nc.tensor.matmul(ps[32 * i:32 * i + 32, :], pieces[:, :], sq[i][:, :], start=True, stop=True)
                    last.then_inc(n_ps, 1)
                else:
                    ps = take(uses)
                    for i in range(TPC):
                        last = nc.tensor.matmul(ps[:, i * P:(i + 1) * P], nT[:, i * P:(i + 1) * P], w_raw[:, 2, :],
                                                start=True, stop=True)
                    last.then_inc(v_ps, 1)

            def maximum(b, par, psA_free, uses):
                for j in range(KT):
                    for h in range(T):
                        u = j * T + h
                        if u >= 2:
                            pe.wait_ge(pre_max, b * (T * KT) + (u - 1))
                        for a in range(2):
                            last = nc.tensor.matmul(psS[u % 2][:, a, :], qs[par][0:KQ, j, h * P:(h + 1) * P],
                                                    ks[par][0:KQ, 4 * a:4 * a + 4, h * P:(h + 1) * P], start=True, stop=True)
                        last.then_inc(pre_qk, 1)
                pe.wait_ge(pre_max, (b + 1) * (T * KT))
                pe.wait_ge(psA_free, uses.start + 2)
                pe.wait_ge(cleared, 3)
                nc.tensor.transpose(psA[0][:, 0:P], negmax[:, :, :].rearrange("p j h -> p (j h)"), ident[:, :]).then_inc(gt_ps, 1)

            def turn(b, h, uses):
                pe.wait_ge(o_evac, b * T + (h + 3))
                ps = take(uses)
                for a in range(2):
                    last = nc.tensor.transpose(ps[:, a * P:(a + 1) * P], o_sb[:, a * P:(a + 1) * P], ident[:, :])
                last.then_inc(ht_ps, 1)

            def turn_back(uses):
                ps = take(uses, all_read=True)
                nc.tensor.transpose(ps[:, 0:P], ctx_tm[:, :, :].rearrange("p j d -> p (j d)"), ident[:, :]).then_inc(ct_ps, 1)

            def project(uses):
                ps = take(uses, all_read=True)
                nc.tensor.matmul(ps[:, 0:P], ctxT[:, :], w_raw[:, 3, :], start=True, stop=True).then_inc(op_done, 1)

            def batch(b, par, prior, more):
                uses = tally(b, PSA_EMBED, PSA_BATCH, PSA_HEAD)
                pe.wait_ge(stack_in, (b + 1) * STACK)
                pe.wait_ge(unsafe_done, b + 1)
                pe.sem_inc(waited, 1)
                with pe.If(pe.value_load(unsafe[0:1, 0:1], min_val=0, max_val=1)):
                    maximum(b, par, psA_free, uses)
                pe.wait_ge(guard_in, (b + 1) * GUARD)
                if isinstance(b, int) and b < 2:
                    pe.wait_ge(cleared, (2, 3)[b])

                def scores(u):
                    h, kt = divmod(u, KT)
                    for a in range(2):
                        last = nc.tensor.matmul(psS[u % NSC][:, a, :], ks[par][0:KG, kt, h * P:(h + 1) * P],
                                                qs[par][0:KG, 4 * a:4 * a + 4, h * P:(h + 1) * P], start=True, stop=True)
                    last.then_inc(qk_done, 1)

                def weigh(h, kt):
                    if kt == 0:
                        pe.wait_ge(o_evac, b * T + (h + 1))
                    pe.wait_ge(exp_done, b * (T * KT) + (h * KT + kt + 1))
                    for g in range(4):
                        last = nc.tensor.matmul(psO[h % 2][32 * g:32 * g + 32, 0:2 * P], v[par][:, h, kt, :],
                                                probs[kt % NPR][:, g * 2 * P:(g + 1) * 2 * P], start=(kt == 0), stop=(kt == KT - 1))
                    last.then_inc(pv_done, 1)

                for u in range(NSC - 1):
                    scores(u)
                for h in range(T):
                    for kt in range(KT):
                        if h * KT + kt + NSC - 1 < T * KT:
                            scores(h * KT + kt + NSC - 1)
                        weigh(h, kt)
                        if more and (h, kt) in STEPS:
                            embed_step(*STEPS[h, kt], b + 1, 1 - par, uses)
                        if h or prior:
                            if kt == 2:
                                turn(b, h - 1, uses)
                            if kt == 3:
                                turn_back(uses)
                            if kt == 5:
                                project(uses)
                uses.ends(PSA_HEAD * (T - 1 + prior) + PSA_EMBED * more)

            pe.sem_inc(pv_done, NPR)
            pe.wait_ge(wsplit, 1)
            uses = Tally(0)
            for kind, ch in STEPS.values():
                embed_step(kind, ch, 0, 0, uses)
            uses.ends(PSA_EMBED)
            rounds(pe, batch)
            uses = Tally(PSA_EMBED + B * PSA_BATCH - PSA_EMBED - PSA_HEAD, PSA_HEAD % 2)
            turn(B, -1, uses)
            turn_back(uses)
            project(uses)

        @block.vector
        def _(dve):
            dve.sem_inc(psA_free, 2)
            dve.sem_inc(o_evac, 2)
            dve.wait_ge(w_in, N_W * 16)
            nc.vector.tensor_copy(pieces[:, :], pieces_f[:, :])
            split_f32r(nc, dve, wq_hi[:, :], wq_lo[:, :], w_raw[:, 0, :])
            split_f32r(nc, dve, wk_hi[:, :], wk_lo[:, :], w_raw[:, 1, :]).then_inc(wsplit, 1)

            def thirds(dst, src, scratch, begun=None):
                first = nc.vector.tensor_copy(dst[0], src)
                if begun is not None:
                    first.then_inc(begun, 1)
                dve.drain()
                nc.vector.tensor_tensor(scratch, src, dst[0], ALU.subtract)
                dve.drain()
                nc.vector.tensor_copy(dst[1], scratch)
                dve.drain()
                return nc.vector.tensor_tensor(dst[2], scratch, dst[1], ALU.subtract)

            def embed_read(kind, ch, b, par, uses):
                n = b * CPB + (ch + 1)
                uses.next()
                ps = psA[uses.buffer()]
                if kind == "E":
                    dve.wait_ge(emb_ps, n)
                    nc.vector.tensor_tensor(H[:, bass.ds(b * T + ch * TPC, TPC), :], ps[:, :].rearrange("p (i d) -> p i d", d=D),
                                            pe_tab[:, ch * TPC:(ch + 1) * TPC, :], ALU.add).then_inc(psA_free, 1)
                elif kind == "T":
                    dve.wait_ge(nt_ps, n)
                    nc.vector.tensor_copy(nT_hi[:, :], ps[:, :])
                    nc.vector.tensor_copy(nT[:, :], ps[:, :])
                    dve.drain()
                    nc.vector.tensor_tensor(nT_lo[:, :], ps[:, :], nT_hi[:, :].bitcast(F32), ALU.subtract).then_inc(psA_free, 1)
                elif kind in ("q", "k"):
                    i = "qk".index(kind)
                    dve.wait_ge((q_ps, k_ps)[i], n)
                    nc.vector.tensor_scalar(qf[i][:, :], ps[:, :], bcol[:, i:i + 1], (SCALE, 1.0)[i], ALU.add, ALU.mult).then_inc(psA_free, 1)
                elif kind == "N":
                    dve.wait_ge(n_ps, n)
                    nc.vector.tensor_reduce(norms2[:, ch:ch + 1], ps[0:64, :], AX, ALU.max).then_inc(psA_free, 1)
                else:
                    dve.wait_ge(v_ps, n)
                    if isinstance(b, int) and b < 2 and ch == 0:
                        dve.wait_ge(cleared, (1, 3)[b])
                    nc.vector.tensor_tensor(v[par][:, ch * TPC:(ch + 1) * TPC, :, 0:DH], ps[:, :].rearrange("p (i j d) -> p i j d", j=KT, d=DH),
                                            brow[:, 0:1, :].rearrange("p o (j d) -> p o j d", d=DH).broadcast_to([P, TPC, KT, DH]),
                                            ALU.add).then_inc(psA_free, 1)

            def embed_rest(kind, ch, b, par, norms):
                n = b * CPB + (ch + 1)
                if kind == "E":
                    dve.drain()
                    normalise(nc, dve, lambda i: H[:, bass.ds(b * T + (ch * TPC + i), 1), :], lambda i: n0[par][:, ch * TPC + i:ch * TPC + i + 1, :],
                              stat, mv, veps, rs, var_done, rs_done, norms.next()).then_inc(n0_done, 1)
                elif kind in ("q", "k"):
                    i = "qk".index(kind)
                    dve.drain()
                    dve.wait_ge((qparts_out, kparts_out)[i], n * 16)
                    thirds([parts[i][:, a, :] for a in range(3)], qf[i][:, :], rem[:, :], (qf_done, kf_done)[i]).then_inc((qparts_done, kparts_done)[i], 1)
                elif kind == "N" and ch == CPB - 1:
                    dve.drain()
                    nc.vector.tensor_reduce(worst[:, :], norms2[:, :], AX, ALU.max)
                    dve.drain()
                    nc.vector.tensor_copy(pair2[:, 0:1], worst[0:32, :])
                    nc.vector.tensor_copy(pair2[:, 1:2], worst[32:64, :]).then_inc(norms_done, 1)

            def embed_step(kind, ch, b, par, norms, uses):
                embed_read(kind, ch, b, par, uses)
                embed_rest(kind, ch, b, par, norms)

            def finish(part, b, half_, norms):
                rows = [brow[:, i:i + 1, :].broadcast_to([P, TPC, D]) for i in range(5)]
                r = res[half_]
                tiles = bass.ds(b * T + half_ * TPC, TPC)
                dve.drain()
                if part == 0:
                    nc.vector.tensor_tensor(r[:, :, :], r[:, :, :], rows[1], ALU.add)
                    dve.drain()
                    normalise(nc, dve, lambda i: r[:, i, :], lambda i: r[:, i, :], stat, mv, veps, rs, var_done, rs_done, norms.next())
                    dve.drain()
                    dve.sem_inc(normal_done, 1)
                elif part == 2:
                    dve.wait_ge(stream_done, b * 2 + (half_ + 1))
                    normalise(nc, dve, lambda i: H[:, bass.ds(b * T + (half_ * TPC + i), 1), :], lambda i: r[:, i:i + 1, :],
                              stat, mv, veps, rs, var_done, rs_done, norms.next())
                    nc.vector.tensor_copy(mean1[:, tiles], mv[:, :, 0])
                    nc.vector.tensor_copy(rstd1[:, tiles], rs[:, :])
                elif part == 3:
                    nc.vector.tensor_tensor(r[:, :, :], r[:, :, :], rows[4], ALU.mult)
                    dve.drain()
                    nc.vector.tensor_reduce(score1[:, tiles], r[:, :, :], AX, ALU.add)
                dve.drain()

            def maximum(b):
                dve.wait_ge(cleared, 3)
                for j in range(KT):
                    for h in range(T):
                        u = j * T + h
                        dve.wait_ge(pre_qk, b * (T * KT) + (u + 1))
                        nc.vector.tensor_reduce(negmax[:, j, h:h + 1], psS[u % 2][:, :, :].rearrange("p a n -> p (a n)"), AX, ALU.max,
                                                negate=True).then_inc(pre_max, 1)
                dve.wait_ge(gt_ps, b + 1)
                nc.vector.tensor_copy(gf[:, :], psA[0][0:T * KT, 0:P])
                dve.drain()
                thirds([gparts[:, a, :] for a in range(3)], gf[:, :], gr[:, :])

            def no_maximum():
                dve.sem_inc(pre_max, T * KT)
                dve.sem_inc(gt_ps, 1)
                dve.sem_inc(pre_qk, T * KT)
                nc.vector.memset(gparts[:, :, :], 0.0)
                dve.drain()
                dve.sem_inc(gparts_done, 1)

            def guard(b):
                dve.wait_ge(unsafe_done, b + 1)
                dve.sem_inc(waited, 1)
                with dve.If(dve.value_load(unsafe[0:1, 0:1], min_val=0, max_val=1)):
                    dve.sem_inc(waited, 1)
                with dve.Else():
                    no_maximum()

            def out_of_psum(b, h):
                dve.wait_ge(pv_done, b * (T * KT) + ((h + 1) * KT + NPR))
                nc.vector.tensor_copy(o_sb[:, :], psO[h % 2][:, 0:2 * P]).then_inc(o_evac, 1)

            def divide(b, h, uses):
                dve.wait_ge(ht_ps, b * T + (h + 1))
                uses.next()
                o = psA[uses.buffer()][:, 0:2 * P].rearrange("p (a g e) -> p a g e", a=2, e=32)
                r = rden[:, :].rearrange("p (a g o) -> p a g o", a=2, o=1)
                nc.vector.reciprocal(r, o[:, :, :, DH:DH + 1])
                dve.drain()
                nc.vector.tensor_tensor(ctx_tm[:, :, :].rearrange("p (g a) d -> p a g d", a=2), o[:, :, :, 0:DH],
                                        r.broadcast_to([P, 2, 4, DH]), ALU.mult).then_inc(psA_free, 1)

            def evacuate(b, h, uses):
                uses.next()
                dve.wait_ge(ct_ps, b * T + (h + 1))
                nc.vector.tensor_copy(ctxT[:, :], psA[uses.buffer()][:, 0:P]).then_inc(psA_free, 1)

            def add_input(b, par, h, uses):
                uses.next()
                h_ = h % T
                dve.wait_ge(op_done, b * T + (h + 1))
                nc.vector.tensor_tensor(res[h_ // TPC][:, h_ % TPC, :], psA[uses.buffer()][:, 0:P], n0[par][:, h_, :], ALU.add).then_inc(psA_free, 1)

            def batch(b, par, prior, more):
                norms = tally(b, RS_EMBED, RS_BATCH, 2)
                uses = tally(b, PSA_EMBED, PSA_BATCH, PSA_HEAD)
                with dve.If(dve.value_load(unsafe[0:1, 0:1], min_val=0, max_val=1)):
                    maximum(b)
                    dve.drain()
                    dve.sem_inc(gparts_done, 1)

                for h in range(T):
                    steps = [STEPS.get((h, kt)) if more else None for kt in (1, 4)]
                    owner = par if h else 1 - par
                    if h or prior:
                        out_of_psum(b, h - 1)
                    for i, step in enumerate(steps):
                        if step:
                            embed_read(*step, b + 1, 1 - par, uses)
                        if h or prior:
                            divide(b, h - 1, uses) if i == 0 else add_input(b, owner, h - 1, uses)
                        if step:
                            embed_rest(*step, b + 1, 1 - par, norms)
                        if i == 0 and (h or prior):
                            evacuate(b, h - 1, uses)
                        if i == 0 and h == T - 1 and more:
                            guard(b + 1)
                        if prior and (h, i) in UPPER:
                            finish(UPPER[h, i], b - 1, 1, norms)
                        if (h, i) in LOWER:
                            finish(LOWER[h, i], b, 0, norms)
                norms.ends(2 * (1 + prior) + RS_EMBED * more)

            norms, uses = Tally(0), Tally(0)
            for kind, ch in STEPS.values():
                embed_step(kind, ch, 0, 0, norms, uses)
            norms.ends(RS_EMBED)
            guard(0)
            rounds(dve, batch)
            norms = Tally(RS_EMBED + B * RS_BATCH - RS_EMBED - 2)
            uses = Tally(PSA_EMBED + B * PSA_BATCH - PSA_EMBED - PSA_HEAD, PSA_HEAD % 2)
            out_of_psum(B, -1)
            divide(B, -1, uses)
            evacuate(B, -1, uses)
            add_input(B, 1, -1, uses)
            for part in range(4):
                finish(part, B - 1, 1, norms)


def rank(nc, dve, out, more, same, p, lower):
    shape = list(more.shape)
    mine, theirs = p.unsqueeze(3).broadcast_to(shape), p.unsqueeze(2).broadcast_to(shape)
    nc.vector.tensor_tensor(more, theirs, mine, ALU.is_gt)
    nc.vector.tensor_tensor(same, theirs, mine, ALU.is_equal)
    dve.drain()
    nc.vector.tensor_tensor(same, same, lower.unsqueeze(1).broadcast_to(shape), ALU.mult)
    dve.drain()
    nc.vector.tensor_tensor(more, more, same, ALU.add)
    dve.drain()
    return nc.vector.tensor_reduce(out, more, AX, ALU.add)


class Items:

    def __init__(self, R, rounds, per_x, per_w):
        self.R, self.rounds, self.per_x, self.per_w = R, rounds, per_x, per_w

    def at(self, it, k, ahead):
        k += ahead
        return (it + k // self.R if k < 0 or k >= self.R else it), k % self.R

    def x_of(self, it, k):
        return it * (self.R // self.per_x) + k // self.per_x

    def new_x(self, k):
        return k % self.per_x == 0

    def w_of(self, it, k):
        return it * (self.R // self.per_w) + k % (self.R // self.per_w)

    def new_w(self, k):
        return k < self.R // self.per_w

    def run(self, eng, body):
        def round_(it, first, last):
            for k in range(self.R):
                body(it, k, lambda ahead: (k + ahead >= 0 or not first) and (k + ahead < self.R or not last))

        round_(0, True, False)
        with eng.Fori(1, self.rounds - 1) as it:
            round_(it, False, False)
        round_(self.rounds - 1, False, True)


def expert_items(nc, c, block, items, ident, rows, raw1, raw2, rawb1, rawb2, out_func, rows_wait, rows_next, weigh,
                 raw1_in, raw2_in, w1_done, w2_done, x_ps, t_ps, NB, D):
    HID = NB * P
    R = items.R
    x_hi, x_lo = ([c.sb(f"{n}{i}", [D, CH], F32R) for i in range(2)] for n in ("x_hi", "x_lo"))
    w1_hi, w1_lo = ([c.sb(f"{n}{i}", [D, HID], F32R) for i in range(2)] for n in ("w1_hi", "w1_lo"))
    w2_hi, w2_lo = ([c.sb(f"{n}{i}", [P, NB, D], F32R) for i in range(2)] for n in ("w2_hi", "w2_lo"))
    b_hid, b_out = [c.sb(f"b_hid{i}", [P, NB]) for i in range(2)], [c.sb(f"b_out{i}", [P, 1]) for i in range(2)]
    g = c.sb("g", [P, NB, CH])
    g_hi, g_lo = ([c.sb(f"{n}{i}", [P, NB, CH], F32R) for i in range(2)] for n in ("g_hi", "g_lo"))
    y = [c.sb(f"y{i}", [D, CH]) for i in range(2)]
    psH = [c.ps(f"psH{i}", [P, CH]) for i in range(NB)]
    psY = [c.ps(f"psY{i}", [P, CH]) for i in range(2)]
    psX = c.ps("psX", [P, CH])
    psT = c.ps("psT", [P, CH])
    hi_done, x_done, h_ps, g_done, lo_done, y_ps, y_done, t_read = (c.sem(n) for n in "hi_done x_done h_ps g_done lo_done y_ps y_done t_read".split())

    def xb(it, k):
        return k // items.per_x % 2

    @block.scalar
    def _(act):
        def hidden(it, k, then=None):
            m, i = it * R + k, k % 2
            act.wait_ge(w1_done, items.w_of(it, k) + 1)
            for n in range(NB):
                act.wait_ge(h_ps, m * NB + (n + 1))
                if n == 0:
                    act.wait_ge(y_ps, m + 1)
                nc.scalar.activation(g_hi[i][:, n, :], psH[n][:, :], ACT.Gelu, bias=b_hid[i][:, n:n + 1])
                act.wait_ge(lo_done, m * NB + (n + 1))
                nc.scalar.activation(g[:, n, :], psH[n][:, :], ACT.Gelu, bias=b_hid[i][:, n:n + 1]).then_inc(g_done, 1)
                if n == 0 and then is not None:
                    first_bits(*then)

        def first_bits(it, k):
            j = items.x_of(it, k)
            act.wait_ge(x_ps, j + 1)
            nc.scalar.activation(x_hi[xb(it, k)][:, :], psX[:, :], ACT.Copy).then_inc(hi_done, 1)

        def output(it, k):
            m, i = it * R + k, k % 2
            act.wait_ge(y_ps, m + 3)
            act.wait_ge(t_ps, m + 1)
            nc.scalar.activation(y[i][:, :], psY[i][:, :], out_func, bias=b_out[i][:, :]).then_inc(y_done, 1)

        def body(it, k, does):
            ahead = items.at(it, k, 2) if does(2) and items.new_x((k + 2) % R) else None
            if does(1):
                hidden(*items.at(it, k, 1), then=ahead)
            output(it, k)

        first_bits(0, 0)
        if items.new_x(1):
            first_bits(0, 1)
        hidden(0, 0)
        items.run(act, body)

    @block.tensor
    def _(pe):
        def turn_x(it, k):
            rows_wait(pe, it, k)
            j = items.x_of(it, k)
            if not (isinstance(j, int) and j == 0):
                pe.wait_ge(x_done, j)
            for i in range(TPC):
                last = nc.tensor.transpose(psX[:, i * P:(i + 1) * P], rows(it, k)[:, i, 0:D], ident[:, :])
            last.then_inc(x_ps, 1)

        def first(it, k, n):
            i, b = k % 2, xb(it, k)
            if n == 0:
                pe.wait_ge(w1_done, items.w_of(it, k) + 1)
                pe.wait_ge(x_done, items.x_of(it, k) + 1)
            pe.wait_ge(g_done, (it * R + k) * NB + (n + 1))
            product(nc, psH[n][:, :], w1_hi[i][:, n * P:(n + 1) * P], w1_lo[i][:, n * P:(n + 1) * P],
                    x_hi[b][:, :], x_lo[b][:, :]).then_inc(h_ps, 1)

        def second(it, k, n):
            m, i = it * R + k, k % 2
            if n == 0:
                pe.wait_ge(w2_done, items.w_of(it, k) + 1)
                pe.wait_ge(y_done, m + 1)
            pe.wait_ge(lo_done, m * NB + (n + 1 + NB))
            last = product(nc, psY[i][:, :], w2_hi[i][:, n, :], w2_lo[i][:, n, :], g_hi[i][:, n, :], g_lo[i][:, n, :],
                           first=(n == 0), last=(n == NB - 1))
            if n == NB - 1:
                last.then_inc(y_ps, 1)

        def turn_y(it, k):
            m = it * R + k
            pe.wait_ge(y_done, m + 3)
            pe.wait_ge(t_read, m + 1)
            for i in range(TPC):
                last = nc.tensor.transpose(psT[:, i * P:(i + 1) * P], y[k % 2][:, i * P:(i + 1) * P], ident[:, :])
            last.then_inc(t_ps, 1)

        def body(it, k, does):
            if does(2) and items.new_x((k + 2) % R):
                turn_x(*items.at(it, k, 2))
            for n in range(NB):
                if does(1):
                    first(*items.at(it, k, 1), n)
                second(it, k, n)
                if n == 2 and does(-1):
                    turn_y(*items.at(it, k, -1))

        pe.sem_inc(y_ps, 2)
        pe.sem_inc(t_ps, 2)
        turn_x(0, 0)
        if items.new_x(1):
            turn_x(0, 1)
        for n in range(NB):
            first(0, 0, n)
        items.run(pe, body)
        turn_y(items.rounds - 1, R - 1)

    @block.vector
    def _(dve):
        def split_x(it, k):
            j, b = items.x_of(it, k), xb(it, k)
            dve.wait_ge(hi_done, j + 1)
            nc.vector.tensor_tensor(x_lo[b][:, :], psX[:, :], x_hi[b][:, :].bitcast(F32), ALU.subtract).then_inc(x_done, 1)

        def split_w1(it, k):
            j = items.w_of(it, k)
            dve.wait_ge(raw1_in[k % 2], (j - k % 2) * 16 + 32)
            nc.vector.tensor_copy(b_hid[k % 2][:, :], rawb1[k % 2][:, :])
            split_f32r(nc, dve, w1_hi[k % 2][:, :], w1_lo[k % 2][:, :], raw1[k % 2][:, :]).then_inc(w1_done, 1)

        def split_w2(it, k):
            j = items.w_of(it, k)
            dve.wait_ge(raw2_in[k % 2], (j - k % 2) * 16 + 32)
            dve.wait_ge(y_done, it * R + k + 1)
            nc.vector.tensor_copy(b_out[k % 2][:, :], rawb2[k % 2][:, :])
            split_f32r(nc, dve, w2_hi[k % 2][:, :, :], w2_lo[k % 2][:, :, :], raw2[k % 2][:, :, :]).then_inc(w2_done, 1)

        def low(it, k, n):
            m, i = it * R + k, k % 2
            dve.wait_ge(g_done, m * NB + (n + 1 + NB))
            nc.vector.tensor_tensor(g_lo[i][:, n, :], g[:, n, :], g_hi[i][:, n, :].bitcast(F32), ALU.subtract).then_inc(lo_done, 1)

        def body(it, k, does):
            rows_next(dve, it, k, does)
            others = [(does(2) and items.new_w((k + 2) % R), split_w1, 2), (does(2) and items.new_x((k + 2) % R), split_x, 2),
                      (does(1) and items.new_w((k + 1) % R), split_w2, 1), (does(-1), lambda it, k: weigh(dve, psT, it, k).then_inc(t_read, 1), -1)]
            for n in range(NB):
                if does(1):
                    low(*items.at(it, k, 1), n)
                due, step, ahead = others[n]
                if due:
                    step(*items.at(it, k, ahead))

        dve.sem_inc(g_done, NB)
        dve.sem_inc(lo_done, NB)
        dve.sem_inc(y_done, 2)
        dve.sem_inc(t_read, 1)
        rows_next(dve, 0, -3, lambda ahead: True)
        rows_next(dve, 0, -2, lambda ahead: True)
        split_x(0, 0)
        split_w1(0, 0)
        rows_next(dve, 0, -1, lambda ahead: True)
        if items.new_x(1):
            split_x(0, 1)
        split_w1(0, 1)
        split_w2(0, 0)
        for n in range(NB):
            low(0, 0, n)
        items.run(dve, body)
        weigh(dve, psT, items.rounds - 1, R - 1).then_inc(t_read, 1)


def sequence_gates(nc, H, mean1, rstd1, score1, gate, chosen, ins, B, S, D):
    E = ins["w1"].shape[0]
    T = S // P
    NT = B * T
    K = 2
    assert E == B == 8

    with ExitStack() as ctx:
        c = Core(nc, ctx, "g0")
        attn_b, ones = c.sb("attn_b", [P, 1]), c.sb("ones", [P, P])
        ident_b = c.sb("ident_b", [B, B])
        sc, e_sc = c.sb("sc", [P, B, T]), c.sb("e_sc", [P, B, T])
        mx, mx_all, zs, rz, corr = (c.sb(n, [P, B]) for n in ("mx", "mx_all", "zs", "rz", "corr"))
        spread = c.sb("spread", [P, NT, B])
        own = c.sb("own", [P, NT, B])
        pooled, pooledT = c.sb("pooled", [B, D]), c.sb("pooledT", [D, B])
        gate_w, gate_b = c.sb("gate_w", [D, E]), c.sb("gate_b", [B, E])
        lg, pr = c.sb("lg", [B, E]), c.sb("pr", [B, 1, E])
        nmx, sm, rsm = c.sb("nmx", [B, 1]), c.sb("sm", [B, 1]), c.sb("rsm", [B, 1])
        beats, ties, rk = c.sb("beats", [B, 1, E, E]), c.sb("ties", [B, 1, E, E]), c.sb("rk", [B, 1, E])
        lower = c.sb("lower", [P, E, E])
        places = c.sb("places", [P, 2, K, E])
        sel, val = c.sb("sel", [B, K, E]), c.sb("val", [B, K, E])
        g2, i2, i2i = c.sb("g2", [B, K]), c.sb("i2", [B, K]), c.sb("i2i", [B, K], I32)
        d_gate = nc.dram_tensor("d_gate", [B, K], F32).ap()
        d_chosen = nc.dram_tensor("d_chosen", [B, K], I32).ap()
        psX, psT = c.ps("psX", [P, CH]), c.ps("psT", [P, CH])
        tab_in, mx_done, pool_done, exp_done, gate_out, gate_in, pe_gate, dve_gate = (c.sem(n) for n in (
            "tab_in mx_done pool_done exp_done gate_out gate_in pe_gate dve_gate").split())

        block = ctx.enter_context(nc.Block())

        @block.sync
        def _(sp):
            for dst, n in ((own[:, :, :], "own"), (lower[:, :, :], "lower"), (places[:, :, :, :], "places")):
                sp.dma_start(dst, ins[n]).then_inc(tab_in, 16)
            sp.dma_start(attn_b[:, :], ins["attn_b"].rearrange("(o d) -> o d", o=1).broadcast_to([P, 1])).then_inc(tab_in, 16)
            sp.dma_start(gate_w[:, :], ins["gate_w"]).then_inc(tab_in, 16)
            sp.dma_start(gate_b[:, :], ins["gate_b"].rearrange("(o d) -> o d", o=1).broadcast_to([B, E])).then_inc(tab_in, 16)
            sp.dma_start(ident_b[:, :], ins["ident"][0:B, 0:B]).then_inc(tab_in, 16)
            sp.wait_ge(dve_gate, 7)
            sp.dma_start(d_gate, g2[:, :]).then_inc(gate_out, 16)
            sp.dma_start(d_chosen, i2i[:, :]).then_inc(gate_out, 16)
            sp.wait_ge(gate_out, 32)
            sp.dma_start(gate[:, :, :], d_gate.rearrange("(o b) k -> o b k", o=1).broadcast_to([P, B, K])).then_inc(gate_in, 16)
            sp.dma_start(chosen[:, :], d_chosen.rearrange("(o b) k -> o (b k)", o=1)).then_inc(gate_in, 16)
            sp.wait_ge(gate_in, 32)

        @block.gpsimd
        def _(pool):
            pool.wait_ge(mx_done, 1)
            nc.gpsimd.partition_all_reduce(mx_all[:, :], mx[:, :], P, bass.bass_isa.ReduceOp.max).then_inc(pool_done, 1)

        @block.scalar
        def _(act):
            act.wait_ge(dve_gate, 1)
            nc.scalar.activation(e_sc[:, :, :], sc[:, :, :], ACT.Exp).then_inc(exp_done, 1)
            act.wait_ge(dve_gate, 6)
            nc.scalar.activation(pr[:, 0, :], lg[:, :], ACT.Exp, bias=nmx[:, :]).then_inc(exp_done, 1)

        @block.tensor
        def _(pe):
            pe.wait_ge(dve_gate, 2)
            nc.tensor.matmul(psT[:, 0:B], ones[:, :], zs[:, :], start=True, stop=True).then_inc(pe_gate, 1)
            pe.wait_ge(dve_gate, 3)
            for n in range(NT):
                nc.tensor.matmul(psT[0:B, 0:D], spread[:, n, :], H[:, n, :], start=(n == 0), stop=False)
            nc.tensor.matmul(psT[0:B, 0:D], corr[:, :], ones[:, :], start=False, stop=True).then_inc(pe_gate, 1)
            pe.wait_ge(dve_gate, 4)
            nc.tensor.transpose(psX[:, 0:B], pooled[:, :], ident_b[:, :]).then_inc(pe_gate, 1)
            pe.wait_ge(dve_gate, 5)
            nc.tensor.matmul(psT[0:B, 0:E], pooledT[:, :], gate_w[:, :], start=True, stop=True).then_inc(pe_gate, 1)

        @block.vector
        def _(dve):
            nc.vector.memset(ones[:, :], 1.0)
            dve.wait_ge(tab_in, 16 * 7)
            nc.vector.tensor_scalar(sc[:, :, :], score1[:, :].rearrange("p (b t) -> p b t", b=B), attn_b[:, :], None, ALU.add)
            dve.drain()
            nc.vector.tensor_reduce(mx[:, :], sc[:, :, :], AX, ALU.max).then_inc(mx_done, 1)
            dve.wait_ge(pool_done, 1)
            nc.vector.tensor_tensor(sc[:, :, :], sc[:, :, :], mx_all[:, :].unsqueeze(2).broadcast_to([P, B, T]), ALU.subtract).then_inc(dve_gate, 1)
            dve.wait_ge(exp_done, 1)
            nc.vector.tensor_reduce(zs[:, :], e_sc[:, :, :], AX, ALU.add).then_inc(dve_gate, 1)
            dve.wait_ge(pe_gate, 1)
            nc.vector.reciprocal(rz[:, :], psT[:, 0:B])
            dve.drain()
            nc.vector.tensor_tensor(e_sc[:, :, :], e_sc[:, :, :], rz[:, :].unsqueeze(2).broadcast_to([P, B, T]), ALU.mult)
            dve.drain()
            nc.vector.tensor_tensor(e_sc[:, :, :], e_sc[:, :, :], rstd1[:, :].rearrange("p (b t) -> p b t", b=B), ALU.mult)
            dve.drain()
            nc.vector.tensor_tensor(sc[:, :, :], e_sc[:, :, :], mean1[:, :].rearrange("p (b t) -> p b t", b=B), ALU.mult)
            dve.drain()
            nc.vector.tensor_reduce(corr[:, :], sc[:, :, :], AX, ALU.add, negate=True)
            nc.vector.tensor_tensor(spread[:, :, :], own[:, :, :], e_sc[:, :, :].rearrange("p b t -> p (b t)").unsqueeze(2).broadcast_to([P, NT, B]),
                                    ALU.mult).then_inc(dve_gate, 1)
            dve.wait_ge(pe_gate, 2)
            nc.vector.tensor_copy(pooled[:, :], psT[0:B, 0:D]).then_inc(dve_gate, 1)
            dve.wait_ge(pe_gate, 3)
            nc.vector.tensor_copy(pooledT[:, :], psX[:, 0:B]).then_inc(dve_gate, 1)
            dve.wait_ge(pe_gate, 4)
            nc.vector.tensor_tensor(lg[:, :], psT[0:B, 0:E], gate_b[:, :], ALU.add)
            dve.drain()
            nc.vector.tensor_reduce(nmx[:, :], lg[:, :], AX, ALU.max, negate=True).then_inc(dve_gate, 1)
            dve.wait_ge(exp_done, 2)
            nc.vector.tensor_reduce(sm[:, :], pr[:, 0, :], AX, ALU.add)
            dve.drain()
            nc.vector.reciprocal(rsm[:, :], sm[:, :])
            dve.drain()
            nc.vector.tensor_scalar(pr[:, 0, :], pr[:, 0, :], rsm[:, :], None, ALU.mult)
            dve.drain()
            rank(nc, dve, rk[:, :, :], beats[:, :, :, :], ties[:, :, :, :], pr[:, :, :], lower[0:B, :, :])
            dve.drain()
            nc.vector.tensor_tensor(sel[:, :, :], rk[:, :, :].broadcast_to([B, K, E]), places[0:B, 0, :, :], ALU.is_equal)
            dve.drain()
            nc.vector.tensor_tensor(val[:, :, :], sel[:, :, :], pr[:, :, :].broadcast_to([B, K, E]), ALU.mult)
            dve.drain()
            nc.vector.tensor_reduce(g2[:, :], val[:, :, :], AX, ALU.add)
            dve.drain()
            nc.vector.tensor_tensor(val[:, :, :], sel[:, :, :], places[0:B, 1, :, :], ALU.mult)
            dve.drain()
            nc.vector.tensor_reduce(i2[:, :], val[:, :, :], AX, ALU.add)
            nc.vector.tensor_reduce(sm[:, :], g2[:, :], AX, ALU.add)
            dve.drain()
            nc.vector.tensor_copy(i2i[:, :], i2[:, :])
            nc.vector.tensor_scalar(sm[:, :], sm[:, :], 1e-9, None, ALU.add)
            dve.drain()
            nc.vector.reciprocal(rsm[:, :], sm[:, :])
            dve.drain()
            nc.vector.tensor_scalar(g2[:, :], g2[:, :], rsm[:, :], None, ALU.mult).then_inc(dve_gate, 1)


def sequence_experts(nc, H, ident, mean1, rstd1, gate, chosen, ins, B, S, D):
    E, _, HID = ins["w1"].shape
    NB = HID // P
    T = S // P
    CPB = S // CH
    K = 2
    assert NB == 4 and CPB == 2

    with ExitStack() as ctx:
        c = Core(nc, ctx, "f0")
        f = c.sb("f", [P, TPC, D])
        raw1 = [c.sb(f"raw1{r}", [D, HID]) for r in range(K)]
        raw2 = [c.sb(f"raw2{r}", [P, NB, D]) for r in range(K)]
        rawb1 = [c.sb(f"rawb1{r}", [P, NB]) for r in range(K)]
        rawb2 = [c.sb(f"rawb2{r}", [P, 1]) for r in range(K)]
        step, f_done, x_ps, t_ps, w1_done, w2_done = (c.sem(n) for n in "step f_done x_ps t_ps w1_done w2_done".split())
        raw1_in, raw2_in = ([c.sem(f"{n}{r}") for r in range(K)] for n in ("raw1_in", "raw2_in"))
        items = Items(K * CPB, B, K, CPB)

        block = ctx.enter_context(nc.Block())

        @block.sync
        def _(sp):
            def load(b, r, which):
                e = sp.value_load(chosen[0:1, bass.ds(b * K + r, 1)], min_val=0, max_val=E - 1)
                if which == 1:
                    sp.dma_start(raw1[r][:, :], ins["w1"][bass.ds(e, 1), :, :].rearrange("o d h -> d (o h)")).then_inc(raw1_in[r], 16)
                    sp.dma_start(rawb1[r][:, :], ins["b1"][bass.ds(e, 1), :, :].rearrange("o p n -> p (o n)")).then_inc(raw1_in[r], 16)
                else:
                    sp.dma_start(raw2[r][:, :, :], ins["w2"][bass.ds(e, 1), :, :].rearrange("o (n p) d -> p (o n) d", p=P)).then_inc(raw2_in[r], 16)
                    sp.dma_start(rawb2[r][:, :], ins["b2"][bass.ds(e, 1), :].rearrange("o p -> p o")).then_inc(raw2_in[r], 16)

            for r in range(K):
                load(0, r, 1)
                load(0, r, 2)
            with sp.Fori(0, B - 1) as b:
                for r in range(K):
                    for which, done in ((1, w1_done), (2, w2_done)):
                        sp.wait_ge(done, b * K + (r + 1))
                        sp.sem_inc(step, 1)
                        load(b + 1, r, which)

        def rows_wait(pe, it, k):
            pe.wait_ge(f_done, items.x_of(it, k) + 1)

        def rows_next(dve, it, k, does):
            if items.new_x((k + 3) % items.R) and does(3):
                b, k = items.at(it, k, 3)
                j, ch = items.x_of(b, k), k // K
                if not (isinstance(j, int) and j == 0):
                    dve.wait_ge(x_ps, j)
                for i in range(TPC):
                    n = b * T + (ch * TPC + i)
                    last = nc.vector.tensor_scalar(f[:, i:i + 1, :], H[:, bass.ds(n, 1), :], mean1[:, bass.ds(n, 1)], rstd1[:, bass.ds(n, 1)],
                                                   ALU.subtract, ALU.mult)
                last.then_inc(f_done, 1)

        def weigh(dve, psT, b, k):
            ch, r = divmod(k, K)
            dve.wait_ge(t_ps, b * items.R + (k + 3))
            out = H[:, bass.ds(b * T + ch * TPC, TPC), :]
            return nc.vector.scalar_tensor_tensor(out, psT[:, :].rearrange("p (i d) -> p i d", d=D), gate[:, bass.ds(b, 1), r], out,
                                                  ALU.mult, ALU.add)

        expert_items(nc, c, block, items, ident, lambda it, k: f, raw1, raw2, rawb1, rawb2, ACT.Gelu, rows_wait, rows_next, weigh,
                     raw1_in, raw2_in, w1_done, w2_done, x_ps, t_ps, NB, D)


def send_rows(pool, queue, rows, idx, k, T, sent):
    for t in range(T):
        pool.indirect_dma_start(queue, bass.IndirectOffsetOnAxis(ap=idx[:, k, t:t + 1], axis=0), rows[:, t, :], None).then_inc(sent, 16)


def block_attention(nc, H, queue, counts, row, idx, sent, ident, half, ins, B, S, D):
    SB = 32
    SG = P // SB
    T = S // P
    G = SB // SG
    E = ins["Wr"].shape[1]
    CPB = S // CH
    K = 2
    SCALE = float(D // 8) ** -0.5
    assert S == SB * SB and G == T and CPB == 2

    with ExitStack() as ctx:
        c = Core(nc, ctx, "a1")
        f, xT = [c.sb(f"f{p}", [P, T, D]) for p in range(2)], c.sb("xT", [D, S])
        x_hi, x_lo = c.sb("x_hi", [D, S], F32R), c.sb("x_lo", [D, S], F32R)
        w_qk, w_v, w_proj, w_r = c.sb("w_qk", [D, 2, D]), c.sb("w_v", [D, D]), c.sb("w_proj", [D, D]), c.sb("w_r", [D, E])
        w_hi, w_lo = c.sb("w_hi", [D, 2, D], F32R), c.sb("w_lo", [D, 2, D], F32R)
        bcol = c.sb("bcol", [D, 3])
        brow, ones = c.sb("brow", [1, CH]), c.sb("ones", [1, P])
        lower = c.sb("lower", [P, E, E])
        before, all_ones = c.sb("before", [P, P]), c.sb("all_ones", [P, P])
        base = c.sb("base", [P, 1, E])
        place_of = c.sb("place_of", [P, K, B * T], I32)
        qk = [c.sb(n, [D, S]) for n in ("q", "k")]
        v = c.sb("v", [P, G, D])
        mx, sm = c.sb("mx", [P, G]), c.sb("sm", [P, G])
        sc, pr = c.sb("sc", [P, G, SB]), c.sb("pr", [P, G, SB])
        diag = c.sb("diag", [P, G, P])
        oT, zT = c.sb("oT", [D, S]), c.sb("zT", [D, S])
        both, sel, pos, vals = (c.sb(n, [P, T, E]) for n in ("both", "sel", "pos", "vals"))
        slot, newc = c.sb("slot", [P, T]), c.sb("newc", [P, E])
        stat, mv = c.sb("stat", [P, T, 6]), c.sb("mv", [P, T, 2])
        veps, rs = c.sb("veps", [P, T]), c.sb("rs", [P, T])
        lg, el = c.sb("lg", [P, T, E]), c.sb("el", [P, T, E])
        beats, ties = c.sb("beats", [P, T, E, E]), c.sb("ties", [P, T, E, E])
        rk, gm, gs = c.sb("rk", [P, T, E]), c.sb("gm", [P, T]), c.sb("gs", [P, T])

        psX = [c.ps(f"psX{i}", [P, CH]) for i in range(2)]
        psQ = [c.ps(f"psQ{i}", [P, CH]) for i in range(2)]
        psO = [c.ps(f"psO{i}", [P, CH]) for i in range(2)]
        psS, psR = c.ps("psS", [P, CH]), c.ps("psR", [P, CH])
        SC, TE = G * SB, T * E

        (w_in, ready, var_done, rs_done, f_done, x_ps, hi_done, x_done, qk_ps, qk_done, v_ps, v_done, s_ps, sub_done, exp_done,
         diag_done, o_ps, o_done, p_ps, h_done, zn_done, z_ps, z_done, l_ps, lsub_done, lexp_done, row_done, sel_done, pos_ps, slot_done, waited) = (c.sem(n) for n in (
            "w_in ready var_done rs_done f_done x_ps hi_done x_done qk_ps qk_done v_ps v_done s_ps sub_done exp_done "
            "diag_done o_ps o_done p_ps h_done zn_done z_ps z_done l_ps lsub_done lexp_done row_done sel_done pos_ps slot_done waited").split())

        def rounds(eng, iteration):
            iteration(0, 0, False, True, True)
            iteration(1, 1, True, True, True)
            with eng.Fori(1, B // 2 - 1) as it:
                for i in range(2):
                    iteration(it * 2 + i, i, True, True, True)
            iteration(B - 2, 0, True, True, False)
            iteration(B - 1, 1, True, False, False)

        def roots_before(b):
            return 2 + b * 2 if not isinstance(b, int) or b < B - 1 else 2 + (B - 2) * 2 + 1

        block = ctx.enter_context(nc.Block())

        @block.sync
        def _(sp):
            for dst, n in ((w_qk[:, :, :], "Wqk"), (w_v[:, :], "Wv1"), (w_proj[:, :], "Wproj"), (w_r[:, :], "Wr"),
                           (bcol[:, :], "b_qkv"), (lower[:, :, :], "lower"), (before[:, :], "before"), (base[:, :, :], "base"),
                           (place_of[:, :, :], "place_of")):
                sp.dma_start(dst, ins[n]).then_inc(w_in, 16)
            sp.dma_start(brow[:, :].rearrange("o (i d) -> o i d", d=D),
                         ins["b_proj"].rearrange("(o i d) -> o i d", o=1, i=1).broadcast_to([1, TPC, D])).then_inc(w_in, 16)

        @block.gpsimd
        def _(pool):
            def root(n):
                pool.wait_ge(var_done, n)
                nc.gpsimd.tensor_tensor(rs[:, :], veps[:, :], half[:, 0:T], ALU.pow).then_inc(rs_done, 1)

            def send(n, par, k):
                pool.wait_ge(slot_done, n + 1)
                pool.wait_ge(row_done, n + 1)
                pool.sem_inc(waited, 1)
                send_rows(pool, queue, row[par][k], idx[par], k, T, sent)

            def iteration(b, par, z, one, two):
                sends = not isinstance(b, int) or b >= 2
                n = roots_before(b)
                for i in range(2 if two else 1):
                    if sends and two:
                        send(b - 2, par, i)
                    elif sends and not two and i == 0:
                        send(b - 2, par, 0)
                        send(b - 2, par, 1)
                    root(n + (i + 1))

            for i in range(2):
                root(i + 1)
            rounds(pool, iteration)
            for k in range(K):
                send(B - 2, 0, k)

        @block.scalar
        def _(act):
            def copy_z(n):
                if not (isinstance(n, int) and n == 0):
                    act.wait_ge(l_ps, n)
                for ch in range(CPB):
                    act.wait_ge(z_ps, n * CPB + (ch + 1))
                    nc.scalar.activation(zT[:, ch * CH:(ch + 1) * CH], psX[ch][:, :], ACT.Copy).then_inc(z_done, 1)

            def copy_x(n):
                if not (isinstance(n, int) and n == 0):
                    act.wait_ge(v_ps, n * 2)
                for ch in range(CPB):
                    act.wait_ge(x_ps, n * CPB + (ch + 1))
                    nc.scalar.activation(xT[:, :].rearrange("d (s i) -> d i s", i=SB)[:, ch * SB // 2:(ch + 1) * SB // 2, :],
                                         psX[ch][:, :].rearrange("d (i s) -> d i s", s=SB), ACT.Copy)
                    nc.scalar.activation(x_hi[:, ch * CH:(ch + 1) * CH], psX[ch][:, :], ACT.Copy).then_inc(hi_done, 1)

            def project_read(n):
                if not (isinstance(n, int) and n == 0):
                    act.wait_ge(s_ps, n)
                for m in range(4):
                    act.wait_ge(qk_ps, n * 4 + (m + 1))
                    ch, i = divmod(m, 2)
                    nc.scalar.activation(qk[i][:, ch * CH:(ch + 1) * CH], psQ[m % 2][:, :], ACT.Identity, bias=bcol[:, i:i + 1]).then_inc(qk_done, 1)
                act.wait_ge(o_ps, n * 2 + 1)
                for h in range(2):
                    act.wait_ge(v_ps, n * 2 + (h + 1))
                    nc.scalar.activation(v[:, h * TPC:(h + 1) * TPC, :], psX[h][:, :].rearrange("p (i d) -> p i d", d=D), ACT.Copy).then_inc(v_done, 1)

            def route_exp(n):
                act.wait_ge(lsub_done, n + 1)
                nc.scalar.activation(el[:, :, :], lg[:, :, :], ACT.Exp).then_inc(lexp_done, 1)

            def iteration(b, par, z, one, two):
                act.wait_ge(sub_done, b + 1)
                nc.scalar.activation(pr[:, :, :], sc[:, :, :], ACT.Exp, scale=SCALE).then_inc(exp_done, 1)
                if z:
                    copy_z(b - 1)
                tokens = oT[:, :].rearrange("d (i s) -> d s i", s=SB)
                act.wait_ge(p_ps, b * 2 + 1)
                for h in range(2):
                    act.wait_ge(o_ps, b * 2 + (h + 2))
                    nc.scalar.activation(tokens[:, h * SB // 2:(h + 1) * SB // 2, :], psO[h][:, :].rearrange("d (s i) -> d s i", i=SB), ACT.Identity, bias=bcol[:, 2:3]).then_inc(o_done, 1)
                if one:
                    copy_x(b + 1)
                    project_read(b + 1)
                if z:
                    route_exp(b - 1)
                copy_rows(b, par)

            def copy_rows(n, par):
                act.wait_ge(zn_done, n + 1)
                nc.scalar.activation(row[par][1][:, :, 0:D], row[par][0][:, :, 0:D], ACT.Copy).then_inc(row_done, 1)

            act.wait_ge(w_in, 16 * 10)
            copy_x(0)
            project_read(0)
            rounds(act, iteration)
            copy_z(B - 1)
            route_exp(B - 1)

        @block.tensor
        def _(pe):
            def turn(n, par, free):
                pe.wait_ge(f_done, n + 1)
                for ch in range(CPB):
                    if free is not None:
                        pe.wait_ge(free[0], free[1] + ch)
                    for i in range(TPC):
                        last = nc.tensor.transpose(psX[ch][:, i * P:(i + 1) * P], f[par][:, ch * TPC + i, :], ident[:, :])
                    last.then_inc(x_ps, 1)

            def turn_z(n, par):
                pe.wait_ge(zn_done, n + 1)
                for ch in range(CPB):
                    for i in range(TPC):
                        last = nc.tensor.transpose(psX[ch][:, i * P:(i + 1) * P], row[par][0][:, ch * TPC + i, 0:D], ident[:, :])
                    last.then_inc(z_ps, 1)

            def project(n):
                first = isinstance(n, int) and n == 0
                for m in range(4):
                    ch, i = divmod(m, 2)
                    pe.wait_ge(x_done, n * CPB + (ch + 1))
                    if not first or m >= 2:
                        pe.wait_ge(qk_done, n * 4 + (m - 1))
                    cols = slice(ch * CH, (ch + 1) * CH)
                    product(nc, psQ[m % 2][:, :], w_hi[:, i, :], w_lo[:, i, :], x_hi[:, cols], x_lo[:, cols]).then_inc(qk_ps, 1)

            def place(src, s):
                return src[:, :].rearrange("d (i s) -> d s i", s=SB)[:, s, :]

            def values(n):
                for g in range(G):
                    last = nc.tensor.matmul(psX[g // TPC][:, g % TPC * D:(g % TPC + 1) * D], xT[:, g * P:(g + 1) * P], w_v[:, :], start=True, stop=True)
                    if g % TPC == TPC - 1:
                        last.then_inc(v_ps, 1)

            def scores(n):
                pe.wait_ge(qk_done, n * 4 + 4)
                if not (isinstance(n, int) and n == 0):
                    pe.wait_ge(sub_done, n)
                for g in range(G):
                    for a in range(SG):
                        last = nc.tensor.matmul(psS[a * SB:(a + 1) * SB, g * SB:(g + 1) * SB], place(qk[0], g * SG + a), place(qk[1], g * SG + a),
                                                start=True, stop=True)
                last.then_inc(s_ps, 1)

            def attend(b):
                pe.wait_ge(diag_done, b + 1)
                pe.wait_ge(v_done, b * 2 + 2)
                for h in range(2):
                    pe.wait_ge(h_done, b * 2 + (h + 1))
                    for i in range(TPC):
                        g = h * TPC + i
                        last = nc.tensor.matmul(psO[h][:, i * P:(i + 1) * P], v[:, g, :], diag[:, g, :], start=True, stop=True)
                    last.then_inc(o_ps, 1)

            def output(b):
                pe.wait_ge(o_done, b * 2 + 2)
                for h in range(2):
                    nc.tensor.matmul(psO[h][:, :], ones[:, :], brow[:, :], start=True, stop=False)
                    for i in range(TPC):
                        t = h * TPC + i
                        last = nc.tensor.matmul(psO[h][:, i * P:(i + 1) * P], oT[:, t * P:(t + 1) * P], w_proj[:, :], start=False, stop=(i == TPC - 1))
                    last.then_inc(p_ps, 1)

            def logits(n):
                pe.wait_ge(z_done, (n + 1) * CPB)
                if not (isinstance(n, int) and n == 0):
                    pe.wait_ge(slot_done, n)
                for t in range(T):
                    last = nc.tensor.matmul(psR[:, t * E:(t + 1) * E], zT[:, t * P:(t + 1) * P], w_r[:, :], start=True, stop=True)
                last.then_inc(l_ps, 1)

            def positions(n):
                pe.wait_ge(sel_done, n + 1)
                nc.tensor.matmul(psR[:, TE:2 * TE], before[:, :], both[:, :, :], start=True, stop=False)
                nc.tensor.matmul(psR[:, TE:2 * TE], all_ones[:, :], counts[:, :].unsqueeze(1).broadcast_to([P, T, E]), start=False, stop=False)
                for d in range(1, T):
                    last = nc.tensor.matmul(psR[:, TE + d * E:2 * TE], all_ones[:, :], both[:, 0:T - d, :], start=False, stop=(d == T - 1))
                last.then_inc(pos_ps, 1)

            def iteration(b, par, z, one, two):
                if z:
                    pe.wait_ge(v_done, b * 2 + 2)
                    turn_z(b - 1, 1 - par)
                attend(b)
                if z:
                    logits(b - 1)
                if one:
                    turn(b + 1, 1 - par, (z_done, b * CPB - (CPB - 1)) if z else (v_done, 1))
                output(b)
                if one:
                    project(b + 1)
                if z:
                    positions(b - 1)
                if one:
                    values(b + 1)
                    scores(b + 1)

            pe.sem_inc(o_ps, 1)
            pe.sem_inc(p_ps, 1)
            pe.wait_ge(ready, 1)
            turn(0, 0, None)
            project(0)
            values(0)
            scores(0)
            rounds(pe, iteration)
            pe.wait_ge(z_done, (B - 1) * CPB)
            turn_z(B - 1, 1)
            logits(B - 1)
            positions(B - 1)

        @block.vector
        def _(dve):
            norms = Tally(0)

            def normal(n, dst, done, turns):
                normalise(nc, dve, lambda i: H[:, bass.ds(n * T + i, 1), :], dst, stat, mv, veps, rs, var_done, rs_done,
                          turns.next(), T).then_inc(done, 1)

            def normal_x(n, par, turns):
                normal(n, lambda i: f[par][:, i:i + 1, :], f_done, turns)

            def normal_z(n, par, turns):
                if not isinstance(n, int) or n >= 2:
                    dve.wait_ge(sent, (n - 1) * (16 * K * T))
                normal(n, lambda i: row[par][0][:, i:i + 1, 0:D], zn_done, turns)

            def split_x(n):
                if not (isinstance(n, int) and n == 0):
                    dve.wait_ge(v_ps, n * 2)
                for ch in range(CPB):
                    cols = slice(ch * CH, (ch + 1) * CH)
                    dve.wait_ge(hi_done, n * CPB + (ch + 1))
                    nc.vector.tensor_tensor(x_lo[:, cols], psX[ch][:, :], x_hi[:, cols].bitcast(F32), ALU.subtract).then_inc(x_done, 1)

            def attention(b):
                s = psS[:, 0:SC].rearrange("p (g j) -> p g j", j=SB)
                dve.wait_ge(s_ps, b + 1)
                nc.vector.tensor_reduce(mx[:, :], s, AX, ALU.max)
                dve.drain()
                nc.vector.tensor_tensor(sc[:, :, :], s, mx[:, :].unsqueeze(2).broadcast_to([P, G, SB]), ALU.subtract).then_inc(sub_done, 1)
                dve.wait_ge(exp_done, b + 1)
                nc.vector.tensor_reduce(sm[:, :], pr[:, :, :], AX, ALU.add)
                dve.drain()
                nc.vector.reciprocal(sm[:, :], sm[:, :])
                dve.drain()
                nc.vector.tensor_tensor(pr[:, :, :], pr[:, :, :], sm[:, :].unsqueeze(2).broadcast_to([P, G, SB]), ALU.mult)
                dve.drain()
                dve.wait_ge(o_ps, b * 2 + 1)
                for a in range(SG):
                    rows = slice(a * SB, (a + 1) * SB)
                    last = nc.vector.transpose(diag[rows, :, rows], pr[rows, :, :])
                last.then_inc(diag_done, 1)

            def add(b):
                for h in range(2):
                    dve.wait_ge(p_ps, b * 2 + (h + 2))
                    out = H[:, bass.ds(b * T + h * TPC, TPC), :]
                    nc.vector.tensor_tensor(out, out, psO[h][:, :].rearrange("p (i d) -> p i d", d=D), ALU.add).then_inc(h_done, 1)

            def choose(n):
                dve.wait_ge(l_ps, n + 1)
                whole = [P, T, E]
                nc.vector.tensor_copy(lg[:, :, :], psR[:, 0:TE].rearrange("p (t e) -> p t e", e=E))
                dve.drain()
                rank(nc, dve, rk[:, :, :], beats[:, :, :, :], ties[:, :, :, :], lg[:, :, :], lower[:, :, :])
                nc.vector.tensor_reduce(gm[:, :], lg[:, :, :], AX, ALU.max)
                dve.drain()
                nc.vector.tensor_tensor(lg[:, :, :], lg[:, :, :], gm[:, :].unsqueeze(2).broadcast_to(whole), ALU.subtract).then_inc(lsub_done, 1)
                nc.vector.tensor_scalar(both[:, :, :], rk[:, :, :], 2.0, None, ALU.is_lt).then_inc(sel_done, 1)
                dve.drain()
                nc.vector.tensor_reduce(newc[:, :], both[:, :, :].rearrange("p t e -> p e t"), AX, ALU.add)

            def route(n, par):
                whole = [P, T, E]
                dve.wait_ge(lexp_done, n + 1)
                nc.vector.tensor_tensor(el[:, :, :], el[:, :, :], both[:, :, :], ALU.mult)
                dve.drain()
                nc.vector.tensor_reduce(gs[:, :], el[:, :, :], AX, ALU.add)
                dve.drain()
                nc.vector.reciprocal(gs[:, :], gs[:, :])
                dve.drain()
                nc.vector.tensor_tensor(el[:, :, :], el[:, :, :], gs[:, :].unsqueeze(2).broadcast_to(whole), ALU.mult)
                dve.wait_ge(pos_ps, n + 1)
                nc.vector.tensor_tensor(pos[:, :, :], psR[:, TE:2 * TE].rearrange("p (t e) -> p t e", e=E),
                                        base[:, :, :].broadcast_to(whole), ALU.add)
                nc.vector.tensor_tensor(counts[:, :], counts[:, :], newc[:, :], ALU.add)
                for k in range(K):
                    dve.drain()
                    nc.vector.tensor_scalar(sel[:, :, :], rk[:, :, :], float(k), None, ALU.is_equal)
                    dve.drain()
                    nc.vector.tensor_tensor(vals[:, :, :], sel[:, :, :], pos[:, :, :], ALU.mult)
                    dve.drain()
                    nc.vector.tensor_reduce(slot[:, :], vals[:, :, :], AX, ALU.add)
                    dve.drain()
                    nc.vector.tensor_copy(idx[par][:, k, :], slot[:, :])
                    nc.vector.tensor_tensor(vals[:, :, :], sel[:, :, :], el[:, :, :], ALU.mult)
                    dve.drain()
                    nc.vector.tensor_reduce(row[par][k][:, :, D + 1:D + 2], vals[:, :, :], AX, ALU.add)
                    nc.vector.tensor_copy(row[par][k][:, :, D:D + 1].bitcast(I32), place_of[:, k, bass.ds(n * T, T)].unsqueeze(2))
                dve.drain()
                dve.sem_inc(slot_done, 1)

            def iteration(b, par, z, one, two):
                turns = Tally(roots_before(b))
                attention(b)
                if two:
                    normal_x(b + 2, par, turns)
                if one:
                    split_x(b + 1)
                if z:
                    choose(b - 1)
                add(b)
                dve.drain()
                normal_z(b, par, turns)
                if z:
                    route(b - 1, 1 - par)
                turns.ends(2 if two else 1)

            dve.sem_inc(h_done, 2)
            nc.vector.memset(diag[:, :, :], 0.0)
            nc.vector.memset(ones[:, :], 1.0)
            nc.vector.memset(all_ones[:, :], 1.0)
            nc.vector.memset(counts[:, :], 0.0)
            dve.wait_ge(w_in, 16 * 10)
            split_f32r(nc, dve, w_hi[:, :, :], w_lo[:, :, :], w_qk[:, :, :]).then_inc(ready, 1)
            turns = Tally(0)
            normal_x(0, 0, turns)
            split_x(0)
            normal_x(1, 1, turns)
            rounds(dve, iteration)
            choose(B - 1)
            route(B - 1, 1)


def plan_tiles(nc, queue, counts, row, idx, sent, tile_e, tile_row, ins, E, B, S, D):
    STRIDE = B * S + CH
    N = tile_e.shape[1]
    M = B * S // CH
    with ExitStack() as ctx:
        c = Core(nc, ctx, "g1")
        ones = c.sb("ones", [P, P])
        n_f, n_i = c.sb("n_f", [1, 1, E]), c.sb("n_i", [1, E], I32)
        mark, upto = c.sb("mark", [1, E, M]), c.sb("upto", [1, E, E])
        tiles, ends = c.sb("tiles", [1, 1, E]), c.sb("ends", [1, 1, E])
        over, part = c.sb("over", [1, N, E]), c.sb("part", [1, N, E])
        e_f, done_f, row_f = (c.sb(n, [1, N]) for n in ("e_f", "done_f", "row_f"))
        steps, number = c.sb("steps", [1, 1, M]), c.sb("number", [1, N])
        pad = c.sb("pad", [P, TPC, ROW])
        pad_place = c.sb("pad_place", [P, TPC, 1], I32)
        ps = c.ps("ps", [P, CH])
        tab_in, ready, n_ps, counted, done, padded = (c.sem(n) for n in "tab_in ready n_ps counted done padded".split())
        with nc.Block() as block:
            @block.sync
            def _(sp):
                for dst, n in ((upto[:, :, :], "upto"), (steps[:, :, :], "steps"), (number[:, :], "number"), (pad_place[:, :, :], "pad_place")):
                    sp.dma_start(dst, ins[n]).then_inc(tab_in, 16)
                sp.wait_ge(done, 1)
                for e in range(E + 1):
                    first = e * STRIDE if e == E else e * STRIDE + sp.value_load(n_i[0:1, e:e + 1], min_val=0, max_val=B * S)
                    sp.dma_start(queue[bass.ds(first, CH), :].rearrange("(p i) c -> p i c", p=P), pad[:, :, :]).then_inc(padded, 16)
                sp.wait_ge(padded, 16 * (E + 1))

            @block.gpsimd
            def _(pool):
                for k in range(2):
                    send_rows(pool, queue, row[1][k], idx[1], k, S // P, sent)
                pool.wait_ge(sent, B * 16 * 2 * (S // P))

            @block.tensor
            def _(pe):
                pe.wait_ge(ready, 1)
                nc.tensor.matmul(ps[:, 0:E], ones[:, :], counts[:, :], start=True, stop=True).then_inc(n_ps, 1)

            @block.vector
            def _(dve):
                nc.vector.memset(ones[:, :], 1.0).then_inc(ready, 1)
                nc.vector.memset(pad[:, :, :], 0.0)
                dve.drain()
                dve.wait_ge(tab_in, 16 * 4)
                nc.vector.tensor_copy(pad[:, :, D:D + 1].bitcast(I32), pad_place[:, :, :])
                dve.wait_ge(n_ps, 1)
                nc.vector.tensor_copy(n_f[:, 0, :], ps[0:1, 0:E])
                dve.drain()
                nc.vector.tensor_copy(n_i[:, :], n_f[:, 0, :])
                nc.vector.tensor_tensor(mark[:, :, :], n_f[:, 0, :].unsqueeze(2).broadcast_to([1, E, M]), steps[:, :, :].broadcast_to([1, E, M]), ALU.is_gt)
                dve.drain()
                nc.vector.tensor_reduce(tiles[:, 0, :], mark[:, :, :], AX, ALU.add)
                dve.drain()
                nc.vector.tensor_tensor(upto[:, :, :], upto[:, :, :], tiles[:, :, :].broadcast_to([1, E, E]), ALU.mult)
                dve.drain()
                nc.vector.tensor_reduce(ends[:, 0, :], upto[:, :, :], AX, ALU.add)
                dve.drain()
                nc.vector.tensor_tensor(over[:, :, :], ends[:, :, :].broadcast_to([1, N, E]), number[:, :].unsqueeze(2).broadcast_to([1, N, E]), ALU.is_le)
                dve.drain()
                nc.vector.tensor_reduce(e_f[:, :], over[:, :, :], AX, ALU.add)
                nc.vector.tensor_tensor(part[:, :, :], over[:, :, :], tiles[:, :, :].broadcast_to([1, N, E]), ALU.mult)
                dve.drain()
                nc.vector.tensor_reduce(done_f[:, :], part[:, :, :], AX, ALU.add)
                dve.drain()
                nc.vector.tensor_tensor(row_f[:, :], number[:, :], done_f[:, :], ALU.subtract)
                dve.drain()
                nc.vector.tensor_scalar(row_f[:, :], row_f[:, :], float(CH), None, ALU.mult)
                nc.vector.tensor_scalar(done_f[:, :], e_f[:, :], float(STRIDE), None, ALU.mult)
                dve.drain()
                nc.vector.tensor_tensor(row_f[:, :], row_f[:, :], done_f[:, :], ALU.add)
                dve.drain()
                nc.vector.tensor_scalar(row_f[:, :], row_f[:, :], float(E * STRIDE), None, ALU.min)
                nc.vector.tensor_scalar(e_f[:, :], e_f[:, :], float(E - 1), None, ALU.min)
                dve.drain()
                nc.vector.tensor_copy(tile_row[:, :], row_f[:, :])
                nc.vector.tensor_copy(tile_e[:, :], e_f[:, :])
                dve.drain()
                dve.sem_inc(done, 1)


def token_experts(nc, queue, result, tile_e, tile_row, ident, ins, B, S, D):
    E, _, HID = ins["W1"].shape
    NB = HID // P
    N = tile_e.shape[1]
    assert NB == 4 and N % 4 == 0

    with ExitStack() as ctx:
        c = Core(nc, ctx, "f1")
        raw1 = [c.sb(f"raw1{r}", [D, HID]) for r in range(2)]
        raw2 = [c.sb(f"raw2{r}", [P, NB, D]) for r in range(2)]
        rawb1 = [c.sb(f"rawb1{r}", [P, NB]) for r in range(2)]
        rawb2 = [c.sb(f"rawb2{r}", [P, 1]) for r in range(2)]
        rows = [c.sb(f"rows{i}", [P, TPC, ROW]) for i in range(2)]
        meta = [c.sb(f"meta{i}", [P, TPC, 2]) for i in range(4)]
        idx = [c.sb(f"idx{i}", [P, TPC], U32) for i in range(2)]
        out = [c.sb(f"out{i}", [P, TPC, D]) for i in range(2)]
        step, x_ps, t_ps, w1_done, w2_done, meta_done, out_ready, waited = (c.sem(n) for n in "step x_ps t_ps w1_done w2_done meta_done out_ready waited".split())
        raw1_in, raw2_in, rows_in, sent = ([c.sem(f"{n}{i}") for i in range(2)] for n in ("raw1_in", "raw2_in", "rows_in", "sent"))
        items = Items(4, N // 4, 1, 1)

        block = ctx.enter_context(nc.Block())

        @block.sync
        def _(sp):
            def load(m, i, which):
                if which == 0:
                    first = sp.value_load(tile_row[0:1, bass.ds(m, 1)], min_val=0, max_val=E * (B * S + CH))
                    sp.dma_start(rows[i][:, :, :], queue[bass.ds(first, CH), :].rearrange("(p i) c -> p i c", p=P)).then_inc(rows_in[i], 16)
                    return
                e = sp.value_load(tile_e[0:1, bass.ds(m, 1)], min_val=0, max_val=E - 1)
                if which == 1:
                    sp.dma_start(raw1[i][:, :], ins["W1"][bass.ds(e, 1), :, :].rearrange("o d h -> d (o h)")).then_inc(raw1_in[i], 16)
                    sp.dma_start(rawb1[i][:, :], ins["B1"][bass.ds(e, 1), :, :].rearrange("o p n -> p (o n)")).then_inc(raw1_in[i], 16)
                else:
                    sp.dma_start(raw2[i][:, :, :], ins["W2"][bass.ds(e, 1), :, :].rearrange("o (n p) d -> p (o n) d", p=P)).then_inc(raw2_in[i], 16)
                    sp.dma_start(rawb2[i][:, :], ins["B2"][bass.ds(e, 1), :].rearrange("o p -> p o")).then_inc(raw2_in[i], 16)

            for i in range(2):
                for which in range(3):
                    load(i, i, which)
            with sp.Fori(0, N // 2 - 1) as it:
                for i in range(2):
                    m = it * 2 + i
                    sp.wait_ge(meta_done, m + 1)
                    sp.wait_ge(x_ps, m + 1)
                    sp.sem_inc(step, 1)
                    load(m + 2, i, 0)
                    for which, done in ((1, w1_done), (2, w2_done)):
                        sp.wait_ge(done, m + 1)
                        sp.sem_inc(step, 1)
                        load(m + 2, i, which)

        @block.gpsimd
        def _(pool):
            with pool.Fori(0, N // 2) as it:
                for i in range(2):
                    pool.wait_ge(out_ready, it * 2 + (i + 1))
                    pool.sem_inc(waited, 1)
                    for j in range(TPC):
                        pool.indirect_dma_start(result, bass.IndirectOffsetOnAxis(ap=idx[i][:, j:j + 1], axis=0), out[i][:, j, :], None,
                                                bounds_check=2 * B * S - 1, oob_is_err=False).then_inc(sent[i], 16)
            for i in range(2):
                pool.wait_ge(sent[i], N // 2 * 16 * TPC)

        def rows_wait(pe, it, k):
            pe.wait_ge(rows_in[k % 2], (it * 4 + (k - k % 2)) * 8 + 16)

        def rows_next(dve, it, k, does):
            if k + 2 < 0 or not does(2):
                return
            it, k = items.at(it, k, 2)
            rows_wait(dve, it, k)
            nc.vector.tensor_copy(meta[k][:, :, :], rows[k % 2][:, :, D:D + 2]).then_inc(meta_done, 1)

        def weigh(dve, psT, it, k):
            m = it * 4 + k
            if not isinstance(it, int) or it * 4 + k >= 2:
                dve.wait_ge(sent[k % 2], (it * 4 + (k - k % 2)) * 32)
            nc.vector.tensor_copy(idx[k % 2][:, :].bitcast(I32).unsqueeze(2), meta[k][:, :, 0:1].bitcast(I32))
            dve.wait_ge(t_ps, m + 3)
            last = nc.vector.tensor_tensor(out[k % 2][:, :, :], psT[:, :].rearrange("p (i d) -> p i d", d=D),
                                           meta[k][:, :, 1:2].broadcast_to([P, TPC, D]), ALU.mult)
            dve.drain()
            dve.sem_inc(out_ready, 1)
            return last

        expert_items(nc, c, block, items, ident, lambda it, k: rows[k % 2], raw1, raw2, rawb1, rawb2, ACT.Identity, rows_wait, rows_next,
                     weigh, raw1_in, raw2_in, w1_done, w2_done, x_ps, t_ps, NB, D)


def add_results(nc, H, result, out, B, S, D):
    T = S // P
    with ExitStack() as ctx:
        c = Core(nc, ctx, "out")
        y = [[c.sb(f"y{b}{k}", [P, T, D]) for k in range(2)] for b in range(B)]
        y_in = [c.sem(f"y_in{b}") for b in range(B)]
        both, summed, stored = c.sem("both"), c.sem("summed"), c.sem("stored")
        with nc.Block() as block:
            def load(eng, k):
                for b in range(B):
                    rows = result[k * B * S + b * S:k * B * S + (b + 1) * S, :]
                    eng.dma_start(y[b][k][:, :, :], rows.rearrange("(t p) d -> p t d", p=P)).then_inc(y_in[b], 16)

            @block.sync
            def _(sp):
                load(sp, 0)
                for b in range(B):
                    sp.wait_ge(summed, b + 1)
                    sp.dma_start(out[b * S:(b + 1) * S, :].rearrange("(t p) d -> p t d", p=P), H[:, b * T:(b + 1) * T, :]).then_inc(stored, 16)
                sp.wait_ge(stored, B * 16)

            @block.scalar
            def _(act):
                load(act, 1)

            @block.gpsimd
            def _(pool):
                for b in range(B):
                    pool.wait_ge(y_in[b], 32)
                    nc.gpsimd.tensor_tensor(y[b][0][:, :, :], y[b][0][:, :, :], y[b][1][:, :, :], ALU.add).then_inc(both, 1)

            @block.vector
            def _(dve):
                for b in range(B):
                    dve.wait_ge(both, b + 1)
                    h = H[:, b * T:(b + 1) * T, :]
                    nc.vector.tensor_tensor(h, h, y[b][0][:, :, :], ALU.add).then_inc(summed, 1)


def tower(nc, ins, out):
    B, S, D, NH = 8, 1024, 128, 8
    nc.disable_value_cache = True
    with ExitStack() as ctx:
        c = Core(nc, ctx, "all")
        H = c.sb("H", [P, B * S // P, D])
        ident = c.sb("ident", [P, P])
        half = c.sb("half", [P, 8])
        mean1, rstd1, score1 = (c.sb(n, [P, B * S // P]) for n in ("mean1", "rstd1", "score1"))
        ld = c.sem("ld")
        with nc.Block() as block:
            @block.sync
            def _(sp):
                sp.dma_start(ident[:, :], ins["ident"]).then_inc(ld, 16)
                sp.wait_ge(ld, 16)

            @block.vector
            def _(dve):
                nc.vector.memset(half[:, :], -0.5)
        embed_and_attend(nc, H, ident, half, mean1, rstd1, score1, ins, B, S, D, NH)
        gate, chosen = c.sb("gate", [P, B, 2]), c.sb("chosen", [1, B * 2], I32)
        sequence_gates(nc, H, mean1, rstd1, score1, gate, chosen, ins, B, S, D)
        sequence_experts(nc, H, ident, mean1, rstd1, gate, chosen, ins, B, S, D)
        E = ins["Wr"].shape[1]
        K = 2
        counts = c.sb("counts", [P, E])
        tiles = -(-(K * B * S // CH + E - 1) // 4) * 4
        tile_e, tile_row = c.sb("tile_e", [1, tiles], I32), c.sb("tile_row", [1, tiles], I32)
        queue = nc.dram_tensor("queue", [E * (B * S + CH) + CH, ROW], F32).ap()
        result = nc.dram_tensor("result", [K * B * S, D], F32).ap()
        row = [[c.sb(f"row{p}{k}", [P, S // P, ROW]) for k in range(K)] for p in range(2)]
        idx = [c.sb(f"idx{p}", [P, K, S // P], U32) for p in range(2)]
        sent = c.sem("sent")
        block_attention(nc, H, queue, counts, row, idx, sent, ident, half, ins, B, S, D)
        plan_tiles(nc, queue, counts, row, idx, sent, tile_e, tile_row, ins, E, B, S, D)
        token_experts(nc, queue, result, tile_e, tile_row, ident, ins, B, S, D)
        add_results(nc, H, result, out, B, S, D)


def host(inputs):
    import math
    import numpy as np
    g = {k: np.asarray(v) for k, v in inputs.items()}
    b, h, w, f = g["x"].shape
    S, D = h * w, g["L0_tok_W"].shape[1]
    pos = np.arange(2 * S, dtype=np.float32)[:, None]
    div = np.exp(np.arange(0, D, 2, dtype=np.float32) * (-math.log(10000.0) / D))
    pe = np.zeros((2 * S, D), np.float32)
    pe[:, 0::2], pe[:, 1::2] = np.sin(pos * div), np.cos(pos * div)
    a = {"xT": g["x"].reshape(b * S, f).T, "Wtok": g["L0_tok_W"], "pe": pe[:S], "ident": np.eye(128, dtype=np.float32),
         "pieces": (np.arange(D)[:, None] // 16 == np.arange(32)).astype(np.float32)}
    for n in ("Wq", "Wk", "Wv", "Wo"):
        a[n] = g["L0_attn_" + n].T
    for n in ("bq", "bk", "bv", "bo", "gamma", "beta"):
        a[n] = g["L0_attn_" + n]
    E, B = 8, b
    a["attn_w"] = g["L0_ffn_attn_w"].reshape(D)
    a["attn_b"] = g["L0_ffn_attn_b"]
    a["gate_w"], a["gate_b"] = g["L0_ffn_gate_w"], g["L0_ffn_gate_b"]
    a["w1"], a["w2"] = g["L0_ffn_w1"], g["L0_ffn_w2"]
    a["b1"], a["b2"] = g["L0_ffn_b1"].reshape(E, 4, 128).transpose(0, 2, 1), g["L0_ffn_b2"]
    w, b3 = g["L1_attn_W_qkv"].reshape(D, 8, 3, 16), g["L1_attn_b_qkv"].reshape(8, 3, 16)
    a["Wqk"] = w[:, :, 0:2].transpose(0, 2, 1, 3).reshape(D, 2, D)
    a["Wv1"] = w[:, :, 2].reshape(D, D)
    a["b_qkv"] = b3.transpose(0, 2, 1).reshape(D, 3)
    a["Wproj"], a["b_proj"] = g["L1_attn_W_proj"], g["L1_attn_b_proj"]
    a["Wr"], a["W1"], a["W2"] = g["L1_ffn_Wr"], g["L1_ffn_W1"], g["L1_ffn_W2"]
    a["B1"], a["B2"] = g["L1_ffn_b1"].reshape(E, 4, 128).transpose(0, 2, 1), g["L1_ffn_b2"]
    CH, K = 512, 2
    M, N = b * S // CH, -(-(K * b * S // CH + 7) // 4) * 4
    a["before"] = np.triu(np.ones((128, 128), np.float32), 1)
    a["base"] = np.tile((np.arange(8) * (b * S + CH)).astype(np.float32), (128, 1, 1))
    a["place_of"] = (np.arange(128)[:, None, None] + np.arange(K)[:, None] * b * S + np.arange(b * S // 128) * 128).astype(np.int32)
    a["upto"] = np.tril(np.ones((8, 8), np.float32))[None]
    a["steps"] = (np.arange(M) * CH).astype(np.float32)[None, None]
    a["number"] = np.arange(N).astype(np.float32)[None]
    a["pad_place"] = np.tile((K * b * S + np.arange(128)).astype(np.int32)[:, None, None], (1, 4, 1))
    T = S // 128
    a["own"] = np.tile((np.arange(B * T)[:, None] // T == np.arange(B)).astype(np.float32), (128, 1, 1))
    a["lower"] = np.tile(np.tril(np.ones((E, E), np.float32), -1), (128, 1, 1))
    r, e = np.meshgrid(np.arange(2), np.arange(E), indexing="ij")
    a["places"] = np.tile(np.stack([r, e]).astype(np.float32), (128, 1, 1, 1))
    return {k: np.ascontiguousarray(v) for k, v in a.items()}


def kernel(**inputs):
    import numpy as np
    import concourse.bacc as bacc
    from concourse.bass_utils import run_bass_kernel_spmd

    arrays = host(inputs)
    shape = inputs["x"].shape
    S, D = shape[1] * shape[2], inputs["L0_tok_W"].shape[1]
    nc = bacc.Bacc("TRN2", target_bir_lowering=False, num_devices=1)
    ins = {n: nc.dram_tensor(n, a.shape, mybir.dt.from_np(a.dtype), kind="ExternalInput").ap() for n, a in arrays.items()}
    out = nc.dram_tensor("out", [shape[0] * S, D], F32, kind="ExternalOutput").ap()
    tower(nc, ins, out)
    r = run_bass_kernel_spmd(nc, [arrays], core_ids=[0])
    return r.results[0]["out"].reshape(shape[0], S, D)
```
